# Optimizing a Trainium2 kernel written in Bass

```python
import numpy as np
import jax
import jax.numpy as jnp

def _softmax(x, axis=-1):
    return jax.nn.softmax(x, axis=axis)

def _gelu(x):
    return jax.nn.gelu(x, approximate=True)

def _silu(x):
    return jax.nn.silu(x)

def _sigmoid(x):
    return jax.nn.sigmoid(x)

def _layernorm(x, axis=-1, eps=1e-05):
    m = jnp.mean(x, axis=axis, keepdims=True)
    v = jnp.var(x, axis=axis, keepdims=True)
    return (x - m) / jnp.sqrt(v + eps)

def _scatter_add(tgt, idx, src, axis=0):
    return tgt.at[idx].add(src)

def _segment_sum(src, seg, n):
    return jax.ops.segment_sum(src, seg, n)
kernel_name = 'mk_recurrent_d2_jaxref_r8_93f330'

def setup_inputs(seed: int=0):
    np.random.seed(seed)
    _w = jnp.asarray

    def _L0_attn_setup():
        import jax, jax.numpy as jnp
        import numpy as np
        import math
        B, S, H, L = (4, 128, 128, 2)
        DPH = 64
        NH = H // DPH
        ROT = 32
        EXP = 4
        MAX_FREQ = 10.0

        def _sinusoids(seq_len, rot=ROT, max_freq=MAX_FREQ):
            dim_exp = rot // 2
            freqs = 2.0 ** jnp.linspace(0.0, math.log2(max_freq / 2.0), dim_exp)
            coords = (1.0 + jnp.arange(seq_len, dtype=jnp.float32))[None, :, None]
            radians = (coords[..., None] * freqs * math.pi).reshape(1, seq_len, dim_exp)
            sinu = jnp.stack([jnp.cos(radians), jnp.sin(radians)], axis=-3)
            return jnp.tile(sinu, (1, 1, 1, 2))

        def _apply_rotary(qk, sinu):
            rot = sinu.shape[-1]
            sin = sinu[..., 0, :, None, :]
            cos = sinu[..., 1, :, None, :]
            r = qk[..., :rot]
            r2 = jnp.stack([-r[..., ::2], r[..., 1::2]], -1).reshape(r.shape)
            r = r * cos + r2 * sin
            return jnp.concatenate([r, qk[..., rot:]], -1)

        def _ln(x, g, b):
            m = x.mean(-1, keepdims=True)
            v = ((x - m) ** 2).mean(-1, keepdims=True)
            return (x - m) / jnp.sqrt(v + 1e-05) * g + b

        def _layer(x, sinu, ln1_g, ln1_b, ln2_g, ln2_b, wq, bq, wk, bk, wv, bv, wo, w1, b1, w2):
            b_, s_, h_ = x.shape
            xl = _ln(x, ln1_g, ln1_b)
            q = (xl @ wq + bq).reshape(b_, s_, NH, DPH)
            k = (xl @ wk + bk).reshape(b_, s_, NH, DPH)
            v = (xl @ wv + bv).reshape(b_, s_, NH, DPH)
            qk = _apply_rotary(jnp.concatenate([q, k], axis=-2), sinu)
            q, k = jnp.split(qk, 2, axis=-2)
            q = q / math.sqrt(DPH)
            probs = jax.nn.softmax(jnp.einsum('bqhd,bkhd->bhqk', q, k), axis=-1)
            att = jnp.einsum('bhqk,bkhd->bqhd', probs, v).reshape(b_, s_, h_)
            x = x + att @ wo
            xl2 = _ln(x, ln2_g, ln2_b)
            hid = xl2 @ w1 + b1
            hid = hid * jax.nn.sigmoid(1.702 * hid)
            return x + hid @ w2
        key = jax.random.key(seed)
        ks = jax.random.split(key, 16)
        sd = 0.02
        inp = {'x': jax.random.normal(ks[0], (B, S, H), dtype=jnp.float32), 'ln1_g': jnp.ones((L, H), jnp.float32), 'ln1_b': jnp.zeros((L, H), jnp.float32), 'ln2_g': jnp.ones((L, H), jnp.float32), 'ln2_b': jnp.zeros((L, H), jnp.float32), 'wq': sd * jax.random.normal(ks[1], (L, H, H), jnp.float32), 'bq': jnp.zeros((L, H), jnp.float32), 'wk': sd * jax.random.normal(ks[2], (L, H, H), jnp.float32), 'bk': jnp.zeros((L, H), jnp.float32), 'wv': sd * jax.random.normal(ks[3], (L, H, H), jnp.float32), 'bv': jnp.zeros((L, H), jnp.float32), 'wo': sd * jax.random.normal(ks[4], (L, H, H), jnp.float32), 'w1': sd * jax.random.normal(ks[5], (L, H, EXP * H), jnp.float32), 'b1': jnp.zeros((L, EXP * H), jnp.float32), 'w2': sd * jax.random.normal(ks[6], (L, EXP * H, H), jnp.float32)}
        return inp
    _L0_attn_in = _L0_attn_setup()

    def _L0_ffn_setup():
        import jax, jax.numpy as jnp
        import numpy as np
        B, S, D = (1, 256, 128)
        E, K, F = (64, 8, 96)
        SF = 96
        C = 64
        ROUTED_SCALE = 1.0

        def _moe_forward(x, router_w, w_gate, w_up, w_down, ws_gate_up, ws_down):
            T = x.shape[0]
            logits = x.astype(jnp.float32) @ router_w.T
            probs = jax.nn.softmax(logits, axis=-1)
            topk_w, topk_ids = jax.lax.top_k(probs, K)
            topk_w = topk_w / jnp.sum(topk_w, axis=-1, keepdims=True)
            topk_w = topk_w.astype(x.dtype)
            N = T * K
            flat_e = topk_ids.reshape(-1)
            flat_w = topk_w.reshape(-1)
            tok = jnp.arange(N) // K
            onehot = flat_e[:, None] == jnp.arange(E)[None, :]
            pos = jnp.cumsum(onehot, axis=0)[jnp.arange(N), flat_e] - 1
            valid = pos < C
            idx = jnp.where(valid, flat_e * C + pos, E * C)
            x_buf = jnp.zeros((E * C + 1, x.shape[1]), x.dtype).at[idx].set(x[tok])
            xb = x_buf[:E * C].reshape(E, C, -1)
            g = jnp.einsum('ecd,edf->ecf', xb, w_gate)
            u = jnp.einsum('ecd,edf->ecf', xb, w_up)
            h = jax.nn.silu(g) * u
            y = jnp.einsum('ecf,efd->ecd', h, w_down).reshape(E * C, -1)
            safe = jnp.where(valid, idx, 0)
            contrib = y[safe] * (flat_w * valid.astype(flat_w.dtype))[:, None]
            routed = jax.ops.segment_sum(contrib, tok, num_segments=T)
            routed = routed * ROUTED_SCALE
            gu = x @ ws_gate_up
            sg, su = (gu[:, :SF], gu[:, SF:])
            shared = jax.nn.silu(sg) * su @ ws_down
            return routed + shared
        key = jax.random.key(seed)
        ks = jax.random.split(key, 7)
        w = 0.02
        return {'hidden_states': jax.random.normal(ks[0], (B, S, D), jnp.float32), 'router_w': jax.random.normal(ks[1], (E, D), jnp.float32) * w, 'w_gate': jax.random.normal(ks[2], (E, D, F), jnp.float32) * w, 'w_up': jax.random.normal(ks[3], (E, D, F), jnp.float32) * w, 'w_down': jax.random.normal(ks[4], (E, F, D), jnp.float32) * w, 'ws_gate_up': jax.random.normal(ks[5], (D, 2 * SF), jnp.float32) * w, 'ws_down': jax.random.normal(ks[6], (SF, D), jnp.float32) * w}
    _L0_ffn_in = _L0_ffn_setup()

    def _L1_attn_setup():
        import jax, jax.numpy as jnp
        import numpy as np
        B, N, C, H, K = (4, 512, 128, 16, 2)
        D = C // H

        def _kernel(x):
            return jax.nn.silu(x) + 0.5
        key = jax.random.key(seed)
        ks = jax.random.split(key, 8)
        s = 0.02
        x = jax.random.normal(ks[0], (B, N, C), jnp.float32)
        Wq = jax.random.normal(ks[1], (C, C), jnp.float32) * s
        bq = jnp.zeros((C,), jnp.float32)
        Wk = jax.random.normal(ks[2], (K, C, C), jnp.float32) * s
        bk = jnp.zeros((K, C), jnp.float32)
        Wv = jax.random.normal(ks[3], (K, C, C), jnp.float32) * s
        bv = jnp.zeros((K, C), jnp.float32)
        Wo = jax.random.normal(ks[4], (C, C), jnp.float32) * s
        bo = jnp.zeros((C,), jnp.float32)
        ln_g = jnp.ones((C,), jnp.float32)
        ln_b = jnp.zeros((C,), jnp.float32)
        return dict(x=x, Wq=Wq, bq=bq, Wk=Wk, bk=bk, Wv=Wv, bv=bv, Wo=Wo, bo=bo, ln_g=ln_g, ln_b=ln_b)
    _L1_attn_in = _L1_attn_setup()

    def _L1_ffn_setup():
        import jax, jax.numpy as jnp
        import numpy as np
        H = 128
        I = 256
        E = 32
        B, S = (4, 256)

        def _grouped_mm(a, w, group_sizes):
            return jax.lax.ragged_dot(a, w, group_sizes)

        def _swiglu(x, gw, uw, dw):
            return jax.nn.silu(x @ gw) * (x @ uw) @ dw
        key = jax.random.key(seed)
        ks = jax.random.split(key, 8)
        scale = 0.02
        inp = {'hidden_states': jax.random.normal(ks[0], (B, S, H), dtype=jnp.float32), 'gate_w': jax.random.normal(ks[1], (H, E), dtype=jnp.float32) * scale, 'shared_gate_w': jax.random.normal(ks[2], (H, I), dtype=jnp.float32) * scale, 'shared_up_w': jax.random.normal(ks[3], (H, I), dtype=jnp.float32) * scale, 'shared_down_w': jax.random.normal(ks[4], (I, H), dtype=jnp.float32) * scale, 'routed_gate_w': jax.random.normal(ks[5], (E, H, I), dtype=jnp.float32) * scale, 'routed_up_w': jax.random.normal(ks[6], (E, H, I), dtype=jnp.float32) * scale, 'routed_down_w': jax.random.normal(ks[7], (E, I, H), dtype=jnp.float32) * scale}
        return inp
    _L1_ffn_in = _L1_ffn_setup()
    _d = {'L0_attn_x': _L0_attn_in['x'], 'L0_attn_ln1_g': _L0_attn_in['ln1_g'], 'L0_attn_ln1_b': _L0_attn_in['ln1_b'], 'L0_attn_ln2_g': _L0_attn_in['ln2_g'], 'L0_attn_ln2_b': _L0_attn_in['ln2_b'], 'L0_attn_wq': _L0_attn_in['wq'], 'L0_attn_bq': _L0_attn_in['bq'], 'L0_attn_wk': _L0_attn_in['wk'], 'L0_attn_bk': _L0_attn_in['bk'], 'L0_attn_wv': _L0_attn_in['wv'], 'L0_attn_bv': _L0_attn_in['bv'], 'L0_attn_wo': _L0_attn_in['wo'], 'L0_attn_w1': _L0_attn_in['w1'], 'L0_attn_b1': _L0_attn_in['b1'], 'L0_attn_w2': _L0_attn_in['w2'], 'L0_ffn_router_w': _L0_ffn_in['router_w'], 'L0_ffn_w_gate': _L0_ffn_in['w_gate'], 'L0_ffn_w_up': _L0_ffn_in['w_up'], 'L0_ffn_w_down': _L0_ffn_in['w_down'], 'L0_ffn_ws_gate_up': _L0_ffn_in['ws_gate_up'], 'L0_ffn_ws_down': _L0_ffn_in['ws_down'], 'L1_attn_Wq': _L1_attn_in['Wq'], 'L1_attn_bq': _L1_attn_in['bq'], 'L1_attn_Wk': _L1_attn_in['Wk'], 'L1_attn_bk': _L1_attn_in['bk'], 'L1_attn_Wv': _L1_attn_in['Wv'], 'L1_attn_bv': _L1_attn_in['bv'], 'L1_attn_Wo': _L1_attn_in['Wo'], 'L1_attn_bo': _L1_attn_in['bo'], 'L1_attn_ln_g': _L1_attn_in['ln_g'], 'L1_attn_ln_b': _L1_attn_in['ln_b'], 'L1_ffn_gate_w': _L1_ffn_in['gate_w'], 'L1_ffn_shared_gate_w': _L1_ffn_in['shared_gate_w'], 'L1_ffn_shared_up_w': _L1_ffn_in['shared_up_w'], 'L1_ffn_shared_down_w': _L1_ffn_in['shared_down_w'], 'L1_ffn_routed_gate_w': _L1_ffn_in['routed_gate_w'], 'L1_ffn_routed_up_w': _L1_ffn_in['routed_up_w'], 'L1_ffn_routed_down_w': _L1_ffn_in['routed_down_w']}
    _x0 = _d['L0_attn_x']
    _d['L0_attn_x'] = jax.random.normal(jax.random.fold_in(jax.random.key(seed), 1), (32, 256, 128), dtype=_x0.dtype)
    del _x0
    return _d

def reference(L0_attn_x, L0_attn_ln1_g, L0_attn_ln1_b, L0_attn_ln2_g, L0_attn_ln2_b, L0_attn_wq, L0_attn_bq, L0_attn_wk, L0_attn_bk, L0_attn_wv, L0_attn_bv, L0_attn_wo, L0_attn_w1, L0_attn_b1, L0_attn_w2, L0_ffn_router_w, L0_ffn_w_gate, L0_ffn_w_up, L0_ffn_w_down, L0_ffn_ws_gate_up, L0_ffn_ws_down, L1_attn_Wq, L1_attn_bq, L1_attn_Wk, L1_attn_bk, L1_attn_Wv, L1_attn_bv, L1_attn_Wo, L1_attn_bo, L1_attn_ln_g, L1_attn_ln_b, L1_ffn_gate_w, L1_ffn_shared_gate_w, L1_ffn_shared_up_w, L1_ffn_shared_down_w, L1_ffn_routed_gate_w, L1_ffn_routed_up_w, L1_ffn_routed_down_w):

    def _L0_attn_ref(x, ln1_g, ln1_b, ln2_g, ln2_b, wq, bq, wk, bk, wv, bv, wo, w1, b1, w2):
        import jax, jax.numpy as jnp
        import numpy as np
        import math
        B, S, H, L = (4, 128, 128, 2)
        DPH = 64
        NH = H // DPH
        ROT = 32
        EXP = 4
        MAX_FREQ = 10.0

        def _sinusoids(seq_len, rot=ROT, max_freq=MAX_FREQ):
            dim_exp = rot // 2
            freqs = 2.0 ** jnp.linspace(0.0, math.log2(max_freq / 2.0), dim_exp)
            coords = (1.0 + jnp.arange(seq_len, dtype=jnp.float32))[None, :, None]
            radians = (coords[..., None] * freqs * math.pi).reshape(1, seq_len, dim_exp)
            sinu = jnp.stack([jnp.cos(radians), jnp.sin(radians)], axis=-3)
            return jnp.tile(sinu, (1, 1, 1, 2))

        def _apply_rotary(qk, sinu):
            rot = sinu.shape[-1]
            sin = sinu[..., 0, :, None, :]
            cos = sinu[..., 1, :, None, :]
            r = qk[..., :rot]
            r2 = jnp.stack([-r[..., ::2], r[..., 1::2]], -1).reshape(r.shape)
            r = r * cos + r2 * sin
            return jnp.concatenate([r, qk[..., rot:]], -1)

        def _ln(x, g, b):
            m = x.mean(-1, keepdims=True)
            v = ((x - m) ** 2).mean(-1, keepdims=True)
            return (x - m) / jnp.sqrt(v + 1e-05) * g + b

        def _layer(x, sinu, ln1_g, ln1_b, ln2_g, ln2_b, wq, bq, wk, bk, wv, bv, wo, w1, b1, w2):
            b_, s_, h_ = x.shape
            xl = _ln(x, ln1_g, ln1_b)
            q = (xl @ wq + bq).reshape(b_, s_, NH, DPH)
            k = (xl @ wk + bk).reshape(b_, s_, NH, DPH)
            v = (xl @ wv + bv).reshape(b_, s_, NH, DPH)
            qk = _apply_rotary(jnp.concatenate([q, k], axis=-2), sinu)
            q, k = jnp.split(qk, 2, axis=-2)
            q = q / math.sqrt(DPH)
            probs = jax.nn.softmax(jnp.einsum('bqhd,bkhd->bhqk', q, k), axis=-1)
            att = jnp.einsum('bhqk,bkhd->bqhd', probs, v).reshape(b_, s_, h_)
            x = x + att @ wo
            xl2 = _ln(x, ln2_g, ln2_b)
            hid = xl2 @ w1 + b1
            hid = hid * jax.nn.sigmoid(1.702 * hid)
            return x + hid @ w2
        sinu = _sinusoids(x.shape[1])
        for i in range(ln1_g.shape[0]):
            x = _layer(x, sinu, ln1_g[i], ln1_b[i], ln2_g[i], ln2_b[i], wq[i], bq[i], wk[i], bk[i], wv[i], bv[i], wo[i], w1[i], b1[i], w2[i])
        return x

    def _L0_ffn_ref(hidden_states, router_w, w_gate, w_up, w_down, ws_gate_up, ws_down):
        import jax, jax.numpy as jnp
        import numpy as np
        B, S, D = (1, 256, 128)
        E, K, F = (64, 8, 96)
        SF = 96
        C = 64
        ROUTED_SCALE = 1.0

        def _moe_forward(x, router_w, w_gate, w_up, w_down, ws_gate_up, ws_down):
            T = x.shape[0]
            logits = x.astype(jnp.float32) @ router_w.T
            probs = jax.nn.softmax(logits, axis=-1)
            topk_w, topk_ids = jax.lax.top_k(probs, K)
            topk_w = topk_w / jnp.sum(topk_w, axis=-1, keepdims=True)
            topk_w = topk_w.astype(x.dtype)
            N = T * K
            flat_e = topk_ids.reshape(-1)
            flat_w = topk_w.reshape(-1)
            tok = jnp.arange(N) // K
            onehot = flat_e[:, None] == jnp.arange(E)[None, :]
            pos = jnp.cumsum(onehot, axis=0)[jnp.arange(N), flat_e] - 1
            valid = pos < C
            idx = jnp.where(valid, flat_e * C + pos, E * C)
            x_buf = jnp.zeros((E * C + 1, x.shape[1]), x.dtype).at[idx].set(x[tok])
            xb = x_buf[:E * C].reshape(E, C, -1)
            g = jnp.einsum('ecd,edf->ecf', xb, w_gate)
            u = jnp.einsum('ecd,edf->ecf', xb, w_up)
            h = jax.nn.silu(g) * u
            y = jnp.einsum('ecf,efd->ecd', h, w_down).reshape(E * C, -1)
            safe = jnp.where(valid, idx, 0)
            contrib = y[safe] * (flat_w * valid.astype(flat_w.dtype))[:, None]
            routed = jax.ops.segment_sum(contrib, tok, num_segments=T)
            routed = routed * ROUTED_SCALE
            gu = x @ ws_gate_up
            sg, su = (gu[:, :SF], gu[:, SF:])
            shared = jax.nn.silu(sg) * su @ ws_down
            return routed + shared
        b, s, d = hidden_states.shape
        x = hidden_states.reshape(-1, d)
        out = _moe_forward(x, router_w, w_gate, w_up, w_down, ws_gate_up, ws_down)
        return out.reshape(b, s, d)

    def _L1_attn_ref(x, Wq, bq, Wk, bk, Wv, bv, Wo, bo, ln_g, ln_b):
        import jax, jax.numpy as jnp
        import numpy as np
        B, N, C, H, K = (4, 512, 128, 16, 2)
        D = C // H

        def _kernel(x):
            return jax.nn.silu(x) + 0.5
        dtype = x.dtype
        Bn, Nn, Cn = x.shape
        q = x + x @ Wq.T + bq
        ks = x[None] + jnp.einsum('bnc,kdc->kbnd', x, Wk) + bk[:, None, None, :]
        vs = x[None] + jnp.einsum('bnc,kdc->kbnd', x, Wv) + bv[:, None, None, :]
        q = q.reshape(Bn, Nn, H, D).transpose(0, 2, 1, 3)
        ks = ks.reshape(K, Bn, Nn, H, D).transpose(0, 1, 3, 2, 4)
        vs = vs.reshape(K, Bn, Nn, H, D).transpose(0, 1, 3, 2, 4)
        q = _kernel(q)
        ks = _kernel(ks)
        q = q / (jnp.linalg.norm(q, axis=-1, keepdims=True) + 1e-06)
        ks = ks / (jnp.linalg.norm(ks, axis=-1, keepdims=True) + 1e-06)
        scale = Nn ** (-0.5)
        ks = ks.astype(jnp.float32) * scale
        vs = vs.astype(jnp.float32) * scale
        states = jnp.einsum('kbhnd,kbhne->kbhde', ks, vs)
        state = jnp.prod(states, axis=0)
        out = jnp.einsum('bhnd,bhde->bhne', q.astype(jnp.float32), state)
        out = out.astype(dtype)
        out = out.transpose(0, 2, 1, 3).reshape(Bn, Nn, Cn)
        mu = out.mean(axis=-1, keepdims=True)
        var = out.var(axis=-1, keepdims=True)
        out = (out - mu) * jax.lax.rsqrt(var + 1e-05) * ln_g + ln_b
        out = out @ Wo.T + bo
        return out

    def _L1_ffn_ref(hidden_states, gate_w, shared_gate_w, shared_up_w, shared_down_w, routed_gate_w, routed_up_w, routed_down_w):
        import jax, jax.numpy as jnp
        import numpy as np
        H = 128
        I = 256
        E = 32
        B, S = (4, 256)

        def _grouped_mm(a, w, group_sizes):
            return jax.lax.ragged_dot(a, w, group_sizes)

        def _swiglu(x, gw, uw, dw):
            return jax.nn.silu(x @ gw) * (x @ uw) @ dw
        b, s, h = hidden_states.shape
        x = hidden_states.reshape(-1, h)
        shared_out = _swiglu(x, shared_gate_w, shared_up_w, shared_down_w)
        logits = x @ gate_w
        topk_ids = jnp.argmax(logits, axis=-1)
        topk_val = jnp.max(logits, axis=-1)
        scores = jax.nn.sigmoid(topk_val)[:, None]
        xs = x * scores
        tokens_per_expert = jnp.zeros((E,), jnp.int32).at[topk_ids].add(1)
        order = jnp.argsort(topk_ids)
        sorted_x = xs[order]
        g = _grouped_mm(sorted_x, routed_gate_w, tokens_per_expert)
        u = _grouped_mm(sorted_x, routed_up_w, tokens_per_expert)
        d = _grouped_mm(jax.nn.silu(g) * u, routed_down_w, tokens_per_expert)
        inv = jnp.argsort(order)
        routed_out = d[inv]
        return (shared_out + routed_out).reshape(b, s, h)
    x = L0_attn_x
    xn = _layernorm(x, axis=-1)
    s = _L0_attn_ref(xn, L0_attn_ln1_g, L0_attn_ln1_b, L0_attn_ln2_g, L0_attn_ln2_b, L0_attn_wq, L0_attn_bq, L0_attn_wk, L0_attn_bk, L0_attn_wv, L0_attn_bv, L0_attn_wo, L0_attn_w1, L0_attn_b1, L0_attn_w2)
    g = _silu(_L0_ffn_ref(xn, L0_ffn_router_w, L0_ffn_w_gate, L0_ffn_w_up, L0_ffn_w_down, L0_ffn_ws_gate_up, L0_ffn_ws_down))
    x = x + s * g
    xn = _layernorm(x, axis=-1)
    s = _L1_attn_ref(xn, L1_attn_Wq, L1_attn_bq, L1_attn_Wk, L1_attn_bk, L1_attn_Wv, L1_attn_bv, L1_attn_Wo, L1_attn_bo, L1_attn_ln_g, L1_attn_ln_b)
    g = _silu(_L1_ffn_ref(xn, L1_ffn_gate_w, L1_ffn_shared_gate_w, L1_ffn_shared_up_w, L1_ffn_shared_down_w, L1_ffn_routed_gate_w, L1_ffn_routed_up_w, L1_ffn_routed_down_w))
    x = x + s * g
    return x

_drawn_inputs = setup_inputs


def setup_inputs(seed=0):
    import zlib

    import numpy as np

    out = dict(_drawn_inputs(seed))
    spreads = {'L0_attn_ln1_g': (1.0, 0.6),
     'L0_attn_ln1_b': (0.0, 0.8),
     'L0_attn_ln2_g': (1.0, 0.6),
     'L0_attn_ln2_b': (0.0, 0.8),
     'L0_attn_bq': (0.0, 0.8),
     'L0_attn_bk': (0.0, 0.8),
     'L0_attn_bv': (0.0, 0.8),
     'L0_attn_b1': (0.0, 0.8),
     'L1_attn_bq': (0.0, 0.8),
     'L1_attn_bk': (0.0, 0.8),
     'L1_attn_bv': (0.0, 0.8),
     'L1_attn_bo': (0.0, 0.8),
     'L1_attn_ln_g': (1.0, 0.6),
     'L1_attn_ln_b': (0.0, 0.8)}
    factors = {'L0_attn_wq': 8.0,
     'L0_attn_wk': 8.0,
     'L0_attn_wv': 8.0,
     'L0_attn_wo': 8.0,
     'L0_attn_w1': 8.0,
     'L0_attn_w2': 8.0,
     'L0_ffn_router_w': 8.0,
     'L0_ffn_w_gate': 8.0,
     'L0_ffn_w_up': 8.0,
     'L0_ffn_w_down': 8.0,
     'L0_ffn_ws_gate_up': 8.0,
     'L0_ffn_ws_down': 8.0,
     'L1_attn_Wq': 8.0,
     'L1_attn_Wk': 8.0,
     'L1_attn_Wv': 8.0,
     'L1_attn_Wo': 8.0,
     'L1_ffn_gate_w': 8.0,
     'L1_ffn_shared_gate_w': 8.0,
     'L1_ffn_shared_up_w': 8.0,
     'L1_ffn_shared_down_w': 8.0,
     'L1_ffn_routed_gate_w': 8.0,
     'L1_ffn_routed_up_w': 8.0,
     'L1_ffn_routed_down_w': 8.0}
    for name, (base, spread) in spreads.items():
        noise = np.random.default_rng([zlib.crc32(name.encode()), seed]).standard_normal(out[name].shape)
        drawn = base * np.exp(spread * noise) if base else spread * noise
        out[name] = jnp.asarray(drawn.astype(out[name].dtype))
    for name, factor in factors.items():
        out[name] = (out[name] * factor).astype(out[name].dtype)
    return out
```

```python
from contextlib import ExitStack

import concourse.bass as bass
from concourse import mybir

F32 = mybir.dt.float32
BF16 = mybir.dt.bfloat16
I32 = mybir.dt.int32
U32 = mybir.dt.uint32
ALU = mybir.AluOpType
ACT = mybir.ActivationFunctionType
X_AXIS = mybir.AxisListType.X

P = 128
C = 128
B = 32
S = 256
TOK = B * S
NT = TOK // P
TPU = S // P
HALF = B // 2
HT = NT // 2
DEPTH = 2
HEADS = 2
DH = C // HEADS
FC = 4
E0, CAP, F0 = 64, 64, 96
E1, F1 = 32, 256
LH, LD = 16, 8
NP = 5 * C
XW = C + E0
EPT = E0 // HALF
SORTED_TILES = NT + E1
IN_FLIGHT = 4
EPS = 1e-5
GELU = 1.702
NEG = -1e30

G1, B1, G2, B2, BQ, BK, BH = 0, 1, 2, 3, 4, 5, 6
NCOL = 6 + FC
C_ID, C_BLK, C_TRI, C_IOTA, C_TOKV, C_ONE, C_P = 0, 128, 256, 384, 416, 480, 608
C_TILE = 609
NCST = C_TILE + SORTED_TILES


def mixed_layers(nc, x, w0, cols, rows, rot, cst, ws, wsd, we0, wd0, w1, we1, out):
    xw = nc.dram_tensor("xw", (TOK, XW), F32, kind="Internal").ap()
    ffn0 = nc.dram_tensor("ffn0", (TOK + CAP, C), F32, kind="Internal").ap()
    x1d = nc.dram_tensor("x1d", (TOK, C), F32, kind="Internal").ap()
    shd = nc.dram_tensor("shd", (TOK, C), F32, kind="Internal").ap()
    xsd = nc.dram_tensor("xsd", (TOK, C), F32, kind="Internal").ap()
    srt = nc.dram_tensor("srt", (SORTED_TILES * P, C), F32, kind="Internal").ap()
    ysd = nc.dram_tensor("ysd", (SORTED_TILES * P, C), F32, kind="Internal").ap()

    def tiled(d):
        return d.rearrange("(t p) c -> p t c", p=P)

    x_t, xw_t, ffn0_t, x1_t, sh_t, xs_t = (tiled(d) for d in (x, xw, ffn0[0:TOK, :], x1d, shd, xsd))
    srt_t, ys_t, out_t = tiled(srt), tiled(ysd), tiled(out)

    ctx = ExitStack()
    with ctx:
        def sb(name, shape, dt=F32):
            return ctx.enter_context(nc.sbuf_tensor(name, shape, dt))

        def sem(name):
            return ctx.enter_context(nc.semaphore(name))

        def sems(stage, names):
            return {n: sem(f"{stage}_{n}") for n in names}

        ps = ctx.enter_context(nc.psum_tensor("ps", [P, 8, 512], F32))

        def bank(g, n):
            return ps[:, 4 * g + n, :]
        T, Q, S0, S1 = 0, 1, 2, 3

        X = sb("X", [P, NT, C])
        big = sb("big", [P, E1 * 768])
        keys = big[:, 0:HT * P]
        WE1 = big[:, :].rearrange("p (e f) -> p e f", e=E1)
        W0 = sb("W0", [P, DEPTH, 1536])

        def early(shape):
            return carve(big[:, :], early_at, shape)

        def late(shape):
            return carve(W0[:, :, :].rearrange("p d n -> p (d n)"), late_at, shape)
        early_at, late_at = [HT * P], [0]

        def carve(room, at, shape):
            n = 1
            for d in shape[1:]:
                n *= d
            at[0] += n
            assert at[0] <= room.shape[1]
            ap = room[0:shape[0], at[0] - n:at[0]]
            if len(shape) == 3:
                return ap.rearrange("p (a b) -> p a b", a=shape[1])
            if len(shape) == 4:
                return ap.rearrange("p (a b c) -> p a b c", a=shape[1], b=shape[2])
            return ap
        COL = sb("COL", [P, DEPTH * NCOL + 2])
        BHS = sb("BHS", [P, DEPTH, FC])
        ROW = sb("ROW", [P, DEPTH * C + NP + C])
        ROT = sb("ROT", [P, 2 * S])
        CST = sb("CST", [P, NCST])
        TRI = sb("TRI", [P, P], BF16)
        ONES = sb("ONES", [P, P], BF16)
        WS = sb("WS", [P, E0 + 2 * F0])
        WSD = sb("WSD", [F0, C])
        W1 = sb("W1", [P, 1568])
        MHALF = sb("MHALF", [P, 4])
        NG = 3 * LH * TPU
        PHALF = sb("PHALF", [P, NG])
        EPS6 = sb("EPS6", [P, NG])

        z0 = early([P, 2, TPU, C])
        z = sb("z", [P, 2, TPU, C])
        zT = sb("zT", [P, 2, S])
        xnT = early([P, 2, S])
        qk = sb("qk", [P, 2, 2, S])
        v = sb("v", [P, 2, TPU, C])
        pr = sb("pr", [P, 2, HEADS, TPU, S])
        pT = sb("pT", [P, 2, HEADS, TPU, S])
        att = sb("att", [P, 2, TPU, C])
        attT = sb("attT", [P, 2, S])
        st = sb("st", [P, 2, TPU, 6])
        mv = sb("mv", [P, 2, TPU, 2])
        ve = sb("ve", [P, 2, TPU])
        rs = sb("rs", [P, 2, TPU])
        nmx = sb("nmx", [P, 2, HEADS * TPU])
        sm = sb("sm", [P, 2, TPU, HEADS])
        rsm = sb("rsm", [P, 2, TPU, HEADS])
        xin = early([P, 2, TPU, C])
        ff = early([P, 2, TPU, C])

        ident = CST[:, C_ID:C_ID + P]

        def col(l, c):
            return COL[:, l * NCOL + c:l * NCOL + c + 1]

        def tiles(i, g):
            return bass.ds(TPU * i + HT * g, TPU)

        ld_small, prep, ld_w, zeroed = sem("ld_small"), sem("prep"), sem("ld_w"), sem("zeroed")
        zero = early([P, C])
        with nc.Block() as block:
            @block.sync
            def _(sp):
                for dst, src in ((CST, cst), (COL, cols), (ROW, rows), (ROT, rot), (WS, ws), (WSD, wsd), (W1, w1)):
                    sp.dma_start(dst[:, :], src).then_inc(ld_small, 16)
                sp.dma_start(W0[:, :, :].rearrange("p d n -> p (d n)"), w0).then_inc(ld_w, 16)
                sp.wait_ge(ld_small, 7 * 16)
                sp.wait_ge(ld_w, 16)

            @block.scalar
            def _(act):
                act.wait_ge(prep, 1)
                act.dma_start(srt_t, zero[:, :].unsqueeze(1).to_broadcast([P, SORTED_TILES, C])).then_inc(zeroed, 16)

            @block.gpsimd
            def _(pool):
                pool.memset(zero[:, :], 0.0).then_inc(prep, 1)
                pool.memset(MHALF[:, 0:2], -0.5)
                pool.memset(MHALF[:, 2:4], EPS)
                pool.memset(PHALF[:, :], 0.5)
                pool.memset(EPS6[:, :], 1e-6)

            @block.vector
            def _(dve):
                dve.wait_ge(ld_small, 7 * 16)
                dve.tensor_copy(TRI[:, :], CST[:, C_TRI:C_TRI + P])
                dve.tensor_copy(ONES[:, :], CST[:, C_ONE:C_ONE + P])
                for l in range(DEPTH):
                    dve.tensor_scalar(BHS[:, l, :], COL[:, l * NCOL + BH:l * NCOL + BH + FC], GELU, None, ALU.mult)
                for n in range(NP // C):
                    dve.tensor_tensor(W1[:, n * C:(n + 1) * C], W1[:, n * C:(n + 1) * C], ident, ALU.add)
                dve.wait_ge(ld_w, 16)
                for l in range(DEPTH):
                    dve.tensor_scalar(W0[:, l, 1024:1536], W0[:, l, 1024:1536], 1.0 / GELU, None, ALU.mult)

        LAYER = ["stats1", "rstd1", "z1", "zT1", "xl1", "qkv", "qkv_sb", "scores", "mx", "probs", "pT", "pT0", "pT1",
                 "pv", "att", "attTp", "attT", "wo", "stats2", "rstd2", "z2", "zT2", "xl2", "hid", "hT", "y", "xout"]

        layer_sems = sems("layer", LAYER)
        norm_sems = sems("norm", ["stats0", "rstd0", "xn", "xnTp", "xnT"])

        def rstd_step(pool, s, u, g, ready, done):
            pool.wait_ge(s[ready], u + 1)
            pool.tensor_tensor(ve[:, g, :], mv[:, g, :, 1], MHALF[:, 2:4], ALU.add)
            pool.drain()
            pool.tensor_tensor(rs[:, g, :], ve[:, g, :], MHALF[:, 0:2], ALU.pow).then_inc(s[done], 1)

        def stats_step(dve, g, src, done):
            for t in range(TPU):
                dve.bn_stats(st[:, g, t, :], src(t))
            dve.drain()
            for t in range(TPU):
                last = dve.bn_aggr(mv[:, g, t, :], st[:, g, t, :])
            last.then_inc(done, 1)

        def norm_step(dve, g, src, dst, done):
            for t in range(TPU):
                last = dve.tensor_scalar(dst(t), src(t), mv[:, g, t, 0:1], rs[:, g, t:t + 1], ALU.subtract, ALU.mult)
            last.then_inc(done, 1)

        def transpose_unit(pe, g, b, c0, src, done):
            for t in range(TPU):
                last = pe.transpose(bank(g, b)[:, c0 + t * P:c0 + (t + 1) * P], src[:, g, t, :], ident)
            last.then_inc(done, 1)

        def layer_tensor(pe, s, i, l, between=None, after_scores=None, logits_read=None, ff_read=None,
                         hidden_free=None):
            n0 = i + HALF * l
            wq, wk, wv, wo = (W0[:, l, n * C:(n + 1) * C] for n in range(4))
            for g in range(2):
                u = 2 * n0 + g
                pe.wait_ge(s["z1"], u + 1)
                transpose_unit(pe, g, T, 0, z, s["zT1"])
            for g in range(2):
                u = 2 * n0 + g
                pe.wait_ge(s["xl1"], u + 1)
                if logits_read:
                    pe.wait_ge(logits_read, 2 * i + g + 1)
                for n, w in enumerate((wq, wk)):
                    pe.matmul(bank(g, Q)[:, n * S:(n + 1) * S], w, zT[:, g, :], start=True, stop=True)
                for t in range(TPU):
                    last = pe.matmul(bank(g, T)[:, S + t * C:S + (t + 1) * C], zT[:, g, t * P:(t + 1) * P], wv,
                                     start=True, stop=True)
                last.then_inc(s["qkv"], 1)
            for g in range(2):
                u = 2 * n0 + g
                pe.wait_ge(s["qkv_sb"], u + 1)
                for t in range(TPU):
                    for h in range(HEADS):
                        d = slice(h * DH, (h + 1) * DH)
                        last = pe.matmul(bank(g, S0 + h)[:, t * S:(t + 1) * S], qk[d, g, 0, t * P:(t + 1) * P],
                                         qk[d, g, 1, :], start=True, stop=True)
                last.then_inc(s["scores"], 1)
            if after_scores:
                after_scores()
            for g in range(2):
                u = 2 * n0 + g
                pe.wait_ge(s["probs"], u + 1)
                for h in range(HEADS):
                    for t in range(TPU):
                        for k in range(TPU):
                            last = pe.transpose(bank(g, S0 + h)[:, k * S + t * P:k * S + (t + 1) * P],
                                                pr[:, g, h, t, k * P:(k + 1) * P], ident)
                    last.then_inc(s["pT"], 1)
            for g in range(2):
                u = 2 * n0 + g
                pe.wait_ge(s["pT0"], u + 1)
                for h in range(HEADS):
                    if h == 1:
                        pe.wait_ge(s["pT1"], u + 1)
                    for t in range(TPU):
                        for k in range(TPU):
                            last = pe.matmul(bank(g, Q)[:, t * C + h * DH:t * C + (h + 1) * DH],
                                             pT[:, g, h, k, t * P:(t + 1) * P], v[:, g, k, h * DH:(h + 1) * DH],
                                             start=(k == 0), stop=(k == TPU - 1))
                last.then_inc(s["pv"], 1)
            for g in range(2):
                u = 2 * n0 + g
                pe.wait_ge(s["att"], u + 1)
                transpose_unit(pe, g, T, 0, att, s["attTp"])
            for g in range(2):
                u = 2 * n0 + g
                pe.wait_ge(s["attT"], u + 1)
                for t in range(TPU):
                    last = pe.matmul(bank(g, Q)[:, S + t * C:S + (t + 1) * C], attT[:, g, t * P:(t + 1) * P], wo,
                                     start=True, stop=True)
                last.then_inc(s["wo"], 1)
            if between:
                between(0)
            for g in range(2):
                u = 2 * n0 + g
                pe.wait_ge(s["z2"], u + 1)
                transpose_unit(pe, g, T, 0, z, s["zT2"])
            if between:
                between(1)
            for g in range(2):
                u = 2 * n0 + g
                pe.wait_ge(s["xl2"], u + 1)
                if hidden_free:
                    pe.wait_ge(hidden_free, 2 * i + g + 1)
                for f in range(FC):
                    last = pe.matmul(bank(g, S0 + f // 2)[:, f % 2 * S:(f % 2 + 1) * S],
                                     W0[:, l, 512 + f * P:512 + (f + 1) * P], zT[:, g, :], start=True, stop=True)
                    if f % 2:
                        last.then_inc(s["hid"], 1)
            if hidden_free:
                between(2)
            for g in range(2):
                u = 2 * n0 + g
                pe.wait_ge(s["hT"], u + 1)
                if ff_read:
                    pe.wait_ge(ff_read, 2 * i + g + 1)
                for t in range(TPU):
                    for f in range(FC):
                        last = pe.matmul(bank(g, Q)[:, t * C:(t + 1) * C],
                                         pr[:, g, f // 2, f % 2, t * P:(t + 1) * P],
                                         W0[:, l, 1024 + f * C:1024 + (f + 1) * C], start=(f == 0), stop=(f == FC - 1))
                last.then_inc(s["y"], 1)
            if hidden_free:
                between(3)

        def affine_step(act, g, scale, bias, done):
            act.activation(zT[:, g, :], bank(g, T)[:, 0:S], ACT.Identity, bias=bias, scale=scale).then_inc(done, 1)

        def layer_scalar(act, s, i, l, after_norm=None, before_norm2=None, before_hidden=None):
            n0 = i + HALF * l
            for g in range(2):
                act.wait_ge(s["zT1"], 2 * n0 + g + 1)
                affine_step(act, g, col(l, G1), col(l, B1), s["xl1"])
            if after_norm:
                after_norm()
            for g in range(2):
                act.wait_ge(s["mx"], 2 * n0 + g + 1)
                for h in range(HEADS):
                    for t in range(TPU):
                        last = act.activation(pr[:, g, h, t, :], bank(g, S0 + h)[:, t * S:(t + 1) * S], ACT.Exp,
                                              bias=nmx[:, g, h * TPU + t:h * TPU + t + 1],
                                              accum_out=sm[:, g, t, h:h + 1])
                last.then_inc(s["probs"], 1)
            for g in range(2):
                act.wait_ge(s["pT"], HEADS * (2 * n0 + g) + 1)
                act.activation(pT[:, g, 0, :, :].rearrange("p k q -> p (k q)"), bank(g, S0), ACT.Copy)\
                   .then_inc(s["pT0"], 1)
            if before_norm2:
                before_norm2()
            for g in range(2):
                act.wait_ge(s["zT2"], 2 * n0 + g + 1)
                affine_step(act, g, col(l, G2), col(l, B2), s["xl2"])
            if before_hidden:
                before_hidden()
            for g in range(2):
                for f in range(FC):
                    if f % 2 == 0:
                        act.wait_ge(s["hid"], 2 * (2 * n0 + g) + f // 2 + 1)
                    last = act.activation(pr[:, g, f // 2, f % 2, :], bank(g, S0 + f // 2)[:, f % 2 * S:(f % 2 + 1) * S],
                                          ACT.Silu, bias=BHS[:, l, f:f + 1], scale=GELU)
                last.then_inc(s["hT"], 1)

        def layer_vector(dve, s, i, l, src, after_norm=None, after_scores=None, before_hidden=None, after_y=None):
            n0 = i + HALF * l
            for g in range(2):
                stats_step(dve, g, lambda t: src(g, t), s["stats1"])
            for g in range(2):
                dve.wait_ge(s["rstd1"], 2 * n0 + g + 1)
                norm_step(dve, g, lambda t: src(g, t), lambda t: z[:, g, t, :], s["z1"])
            if after_norm:
                after_norm()
            for g in range(2):
                dve.wait_ge(s["qkv"], 2 * n0 + g + 1)
                for n, c in enumerate((BQ, BK)):
                    dve.scalar_tensor_tensor(qk[:, g, n, :], bank(g, Q)[:, n * S:(n + 1) * S], col(l, c),
                                             ROT[:, n * S:(n + 1) * S], ALU.add, ALU.mult)
                dve.tensor_tensor(v[:, g, :, :], bank(g, T)[:, S:2 * S].rearrange("p (t c) -> p t c", t=TPU),
                                  ROW[:, l * C:(l + 1) * C].unsqueeze(1).to_broadcast([P, TPU, C]), ALU.add)\
                   .then_inc(s["qkv_sb"], 1)
            for g in range(2):
                dve.wait_ge(s["scores"], 2 * n0 + g + 1)
                dve.tensor_reduce(nmx[:, g, :], ps[:, 4 * g + S0:4 * g + S0 + 2, :].rearrange("p b (t k) -> p (b t) k", t=TPU),
                                  X_AXIS, ALU.max, negate=True).then_inc(s["mx"], 1)
            if after_scores:
                after_scores()
            for g in range(2):
                u = 2 * n0 + g
                dve.wait_ge(s["pT"], HEADS * u + 2)
                dve.tensor_copy(pT[:, g, 1, :, :].rearrange("p k q -> p (k q)"), bank(g, S1)).then_inc(s["pT1"], 1)
                dve.reciprocal(rsm[:, g, :, :], sm[:, g, :, :])
            dve.drain()
            for g in range(2):
                dve.wait_ge(s["pv"], 2 * n0 + g + 1)
                dve.tensor_tensor(att[:, g, :, :].rearrange("p t (h d) -> p (t h) d", h=HEADS),
                                  bank(g, Q)[:, 0:S].rearrange("p (a d) -> p a d", d=DH),
                                  rsm[:, g, :, :].rearrange("p t h -> p (t h)").unsqueeze(2)
                                  .to_broadcast([P, TPU * HEADS, DH]), ALU.mult).then_inc(s["att"], 1)
            for g in range(2):
                dve.wait_ge(s["attTp"], 2 * n0 + g + 1)
                dve.tensor_copy(attT[:, g, :], bank(g, T)[:, 0:S]).then_inc(s["attT"], 1)
            for g in range(2):
                dve.wait_ge(s["wo"], 2 * n0 + g + 1)
                for t in range(TPU):
                    dve.tensor_tensor(X[:, TPU * i + HT * g + t, :], bank(g, Q)[:, S + t * C:S + (t + 1) * C],
                                      src(g, t), ALU.add)
                dve.drain()
                stats_step(dve, g, lambda t: X[:, TPU * i + HT * g + t, :], s["stats2"])
            for g in range(2):
                dve.wait_ge(s["rstd2"], 2 * n0 + g + 1)
                norm_step(dve, g, lambda t: X[:, TPU * i + HT * g + t, :], lambda t: z[:, g, t, :], s["z2"])
            if before_hidden:
                before_hidden()
            for g in range(2):
                dve.wait_ge(s["y"], 2 * n0 + g + 1)
                for t in range(TPU):
                    n = TPU * i + HT * g + t
                    last = dve.tensor_tensor(X[:, n, :], bank(g, Q)[:, t * C:(t + 1) * C], X[:, n, :], ALU.add)
                last.then_inc(s["xout"], 1)
            if after_y:
                after_y()

        lg = early([P, 2, TPU, E0])
        rep = early([P, 2, TPU, E0])
        ex = early([P, 2, TPU, E0])
        mx8 = early([P, 2, TPU, 8])
        nl = early([P, 2, TPU])
        sw = early([P, 2, TPU])
        rsw = early([P, 2, TPU])
        wr = early([P, 2, TPU, E0])
        kk = early([P, TPU, 2, E0])
        hs = early([F0, 2, S])

        def stage1():
            s = dict(layer_sems)
            s.update(norm_sems)
            s.update(sems("s1", ["logits", "lg", "lmax", "lexp", "wrow", "key",
                                    "keyTp", "keyT", "gu", "sg", "hs", "down", "ff"]))
            in_sem = [sem(f"s1_xin{g}") for g in range(2)]
            xn_out = [sem(f"s1_xn_out{g}") for g in range(2)]
            w_out = [sem(f"s1_w_out{g}") for g in range(2)]
            ff_out = [sem(f"s1_ff_out{g}") for g in range(2)]
            with nc.Block() as block:
                @block.sync
                def _(sp):
                    for g in range(2):
                        sp.dma_start(xin[:, g, :, :], x_t[:, HT * g:HT * g + TPU, :]).then_inc(in_sem[g], 16)

                    def turn(i, last):
                        for g in range(2):
                            u = 2 * i + g
                            sp.wait_ge(s["xn"], u + 1)
                            if not last:
                                sp.dma_start(xin[:, g, :, :], x_t[:, tiles(i + 1, g), :]).then_inc(in_sem[g], 16)
                            sp.dma_start(xw_t[:, tiles(i, g), 0:C], z0[:, g, :, :]).then_inc(xn_out[g], 16)
                        for g in range(2):
                            u = 2 * i + g
                            sp.wait_ge(s["wrow"], u + 1)
                            sp.dma_start(xw_t[:, tiles(i, g), C:XW], wr[:, g, :, :]).then_inc(w_out[g], 16)
                        for g in range(2):
                            u = 2 * i + g
                            sp.wait_ge(s["ff"], u + 1)
                            sp.dma_start(ffn0_t[:, tiles(i, g), :], ff[:, g, :, :]).then_inc(ff_out[g], 16)

                    with sp.Fori(0, HALF - 1) as i:
                        turn(i, False)
                    turn(HALF - 1, True)
                    sp.wait_ge(zeroed, 16)
                    for g in range(2):
                        sp.wait_ge(xn_out[g], 16 * HALF)
                        sp.wait_ge(w_out[g], 16 * HALF)
                        sp.wait_ge(ff_out[g], 16 * HALF)

                @block.gpsimd
                def _(pool):
                    with pool.Fori(0, HALF) as i:
                        for g in range(2):
                            rstd_step(pool, s, 2 * i + g, g, "stats0", "rstd0")
                        for g in range(2):
                            rstd_step(pool, s, 2 * i + g, g, "stats1", "rstd1")
                        for g in range(2):
                            rstd_step(pool, s, 2 * i + g, g, "stats2", "rstd2")

                @block.tensor
                def _(pe):
                    with pe.Fori(0, HALF) as i:
                        for g in range(2):
                            pe.wait_ge(s["xn"], 2 * i + g + 1)
                            transpose_unit(pe, g, T, 0, z0, s["xnTp"])
                        for g in range(2):
                            pe.wait_ge(s["xnT"], 2 * i + g + 1)
                            for t in range(TPU):
                                last = pe.matmul(bank(g, Q)[:, t * E0:(t + 1) * E0],
                                                 xnT[:, g, t * P:(t + 1) * P], WS[:, 0:E0], start=True, stop=True)
                            last.then_inc(s["logits"], 1)

                        def key_transposes():
                            pe.wait_ge(s["key"], 2 * i + 2)
                            for t in range(TPU):
                                last = pe.transpose(bank(1, T)[:, t * P:(t + 1) * P],
                                                    kk[:, t, :, :].rearrange("p g e -> p (g e)"), ident)
                            last.then_inc(s["keyTp"], 1)

                        def shared(part):
                            for g in range(2):
                                if part == 0:
                                    for n in range(2):
                                        last = pe.matmul(bank(g, S0)[0:F0, n * S:(n + 1) * S],
                                                         WS[:, E0 + n * F0:E0 + (n + 1) * F0], xnT[:, g, :],
                                                         start=True, stop=True)
                                    last.then_inc(s["gu"], 1)
                                else:
                                    pe.wait_ge(s["hs"], 2 * i + g + 1)
                                    for t in range(TPU):
                                        last = pe.matmul(bank(g, Q)[:, t * C:(t + 1) * C],
                                                         hs[:, g, t * P:(t + 1) * P], WSD[:, :], start=True, stop=True)
                                    last.then_inc(s["down"], 1)

                        layer_tensor(pe, s, i, 0, between=shared, after_scores=key_transposes, logits_read=s["lg"],
                                     ff_read=s["ff"])

                @block.scalar
                def _(act):
                    with act.Fori(0, HALF) as i:
                        for g in range(2):
                            act.wait_ge(s["xnTp"], 2 * i + g + 1)
                            act.activation(xnT[:, g, :], bank(g, T)[:, 0:S], ACT.Copy).then_inc(s["xnT"], 1)

                        def router():
                            for g in range(2):
                                act.wait_ge(s["lmax"], 2 * i + g + 1)
                                for t in range(TPU):
                                    last = act.activation(ex[:, g, t, :], lg[:, g, t, :], ACT.Exp,
                                                          bias=nl[:, g, t:t + 1])
                                last.then_inc(s["lexp"], 1)

                        def shared():
                            act.wait_ge(s["keyTp"], i + 1)
                            act.activation(keys[:, bass.ds(S * i, S)], bank(1, T)[:, 0:S], ACT.Copy)\
                               .then_inc(s["keyT"], 1)

                        def silu():
                            for g in range(2):
                                act.wait_ge(s["gu"], 2 * i + g + 1)
                                act.activation(hs[:, g, :], bank(g, S0)[0:F0, 0:S], ACT.Silu).then_inc(s["sg"], 1)

                        layer_scalar(act, s, i, 0, after_norm=lambda: (router(), shared()), before_hidden=silu)

                @block.vector
                def _(dve):
                    with dve.Fori(0, HALF) as i:
                        for g in range(2):
                            dve.wait_ge(in_sem[g], 16 * (i + 1))
                            stats_step(dve, g, lambda t: xin[:, g, t, :], s["stats0"])
                        for g in range(2):
                            dve.wait_ge(s["rstd0"], 2 * i + g + 1)
                            norm_step(dve, g, lambda t: xin[:, g, t, :], lambda t: z0[:, g, t, :], s["xn"])
                        dve.drain()

                        def router():
                            for g in range(2):
                                dve.wait_ge(s["logits"], 2 * i + g + 1)
                                dve.tensor_copy(lg[:, g, :, :].rearrange("p t e -> p (t e)"),
                                                bank(g, Q)[:, 0:TPU * E0]).then_inc(s["lg"], 1)
                                dve.drain()
                                for t in range(TPU):
                                    dve.max(out=mx8[:, g, t, :], in_=lg[:, g, t, :])
                                dve.drain()
                                dve.tensor_scalar(nl[:, g, :], mx8[:, g, :, 0], -1.0, None, ALU.mult)\
                                   .then_inc(s["lmax"], 1)
                                for t in range(TPU):
                                    dve.match_replace(out=rep[:, g, t, :], in_to_replace=mx8[:, g, t, :],
                                                      in_values=lg[:, g, t, :], imm_value=NEG)
                                dve.drain()
                                for t in range(TPU):
                                    last = dve.tensor_scalar(kk[:, t, g, :], rep[:, g, t, :], NEG / 2,
                                                             CST[:, bass.ds(C_TOKV + TPU * i + HT * g + t, 1)],
                                                             ALU.is_lt, ALU.mult)
                                last.then_inc(s["key"], 1)

                        def weights():
                            for g in range(2):
                                dve.wait_ge(s["lexp"], 2 * i + g + 1)
                                for t in range(TPU):
                                    dve.scalar_tensor_tensor(ex[:, g, t, :], rep[:, g, t, :], NEG / 2, ex[:, g, t, :],
                                                             ALU.is_lt, ALU.mult, accum_out=sw[:, g, t:t + 1])
                            dve.drain()
                            dve.reciprocal(rsw[:, :, :], sw[:, :, :])
                            dve.drain()
                            for g in range(2):
                                dve.tensor_tensor(wr[:, g, :, :], ex[:, g, :, :],
                                                  rsw[:, g, :].unsqueeze(2).to_broadcast([P, TPU, E0]), ALU.mult)\
                                   .then_inc(s["wrow"], 1)

                        def shared():
                            for g in range(2):
                                dve.wait_ge(s["sg"], 2 * i + g + 1)
                                dve.tensor_tensor(hs[:, g, :], bank(g, S0)[0:F0, S:2 * S], hs[:, g, :], ALU.mult)\
                                   .then_inc(s["hs"], 1)
                            for g in range(2):
                                dve.wait_ge(s["down"], 2 * i + g + 1)
                                dve.tensor_copy(ff[:, g, :, :].rearrange("p t c -> p (t c)"), bank(g, Q)[:, 0:S])\
                                   .then_inc(s["ff"], 1)

                        layer_vector(dve, s, i, 0, lambda g, t: z0[:, g, t, :], after_norm=router,
                                     after_scores=weights, before_hidden=shared)
                        for g in range(2):
                            dve.wait_ge(xn_out[g], 16 * (i + 1))
                            dve.wait_ge(w_out[g], 16 * (i + 1))
                            dve.wait_ge(ff_out[g], 16 * (i + 1))
        stage1()

        gidx = sb("gidx", [CAP, E0], I32)
        sidx = sb("sidx", [CAP, E0], I32)

        def pick():
            lst = early([P, CAP])
            both = early([E0, 2 * CAP])
            fin = early([E0, CAP])
            kf = early([CAP, E0])
            tk = early([CAP, E0])
            em = early([CAP, E0])
            halves, moved, firsts, turned = sem("p_halves"), sem("p_moved"), sem("p_firsts"), sem("p_turned")
            with nc.Block() as block:
                @block.sync
                def _(sp):
                    sp.wait_ge(halves, 1)
                    sp.dma_start(both[:, CAP:2 * CAP], lst[E0:P, :]).then_inc(moved, 16)
                    sp.wait_ge(moved, 16)

                @block.tensor
                def _(pe):
                    pe.wait_ge(firsts, 1)
                    pe.transpose(bank(0, T)[0:CAP, 0:E0], fin[:, :], ident[0:E0, 0:E0]).then_inc(turned, 1)

                @block.vector
                def _(dve):
                    def largest(dst, src):
                        for r in range(CAP // 8):
                            dve.max(out=dst[:, 8 * r:8 * r + 8], in_=src)
                            dve.drain()
                            if r < CAP // 8 - 1:
                                dve.match_replace(out=src, in_to_replace=dst[:, 8 * r:8 * r + 8], in_values=src,
                                                  imm_value=0.0)
                                dve.drain()
                    largest(lst, keys)
                    dve.tensor_copy(both[:, 0:CAP], lst[0:E0, :]).then_inc(halves, 1)
                    dve.drain()
                    dve.wait_ge(moved, 16)
                    largest(fin, both[:, :])
                    dve.tensor_copy(em[:, :], CST[0:CAP, C_ONE:C_ONE + E0]).then_inc(firsts, 1)
                    dve.wait_ge(turned, 1)
                    dve.tensor_copy(kf[:, :], bank(0, T)[0:CAP, 0:E0])
                    dve.drain()
                    dve.tensor_scalar(tk[:, :], kf[:, :], -1.0, float(TOK), ALU.mult, ALU.add)
                    dve.tensor_scalar(em[:, :], kf[:, :], 0.0, CST[0:CAP, C_P:C_P + 1], ALU.is_equal, ALU.mult)
                    dve.drain()
                    dve.tensor_scalar(gidx[:, :], tk[:, :], float(TOK - 1), None, ALU.min)
                    dve.tensor_tensor(sidx[:, :], tk[:, :], em[:, :], ALU.add)
        pick()

        wg = early([P, EPT, 2 * F0])
        wdn = early([F0, EPT, C])
        gi = sb("gi", [CAP, EPT], I32)
        si = sb("si", [CAP, EPT], I32)
        sj = sb("sj", [CAP, EPT], I32)
        gj = sb("gj", [CAP, 1], I32)
        zero_i = sb("zero_i", [CAP, 1], I32)
        xe = early([CAP, EPT, XW])
        xeT = early([P, EPT, CAP])
        he = early([CAP, EPT, F0])
        heT = early([F0, EPT, CAP])
        ye = early([CAP, EPT, C])
        EG = EPT // 2

        def stage2():
            s = dict(layer_sems)
            s.update(sems("s2", ["xeTp", "xeT", "eg", "es", "eh", "ehTp", "ehT", "ey", "ye"]))
            we_in = sem("s2_we_in")
            rows_in = [sem(f"s2_rows_in{j}") for j in range(EPT)]
            added = sem("s2_added")
            with nc.Block() as block:
                @block.sync
                def _(sp):
                    def load_experts(i):
                        sp.dma_start(wg[:, :, :], we0[bass.ds(EPT * i, EPT), :, :].rearrange("e p f -> p e f"))\
                          .then_inc(we_in, 16)
                        sp.dma_start(wdn[:, :, :], wd0[bass.ds(EPT * i, EPT), :, :].rearrange("e p f -> p e f"))\
                          .then_inc(we_in, 16)
                    load_experts(0)
                    with sp.Fori(0, HALF - 1) as i:
                        sp.wait_ge(s["ey"], 2 * i + 2)
                        load_experts(i + 1)
                    sp.wait_ge(we_in, 32 * HALF)

                @block.gpsimd
                def _(pool):
                    pool.memset(zero_i[:, :], 0)
                    pool.drain()

                    def scatters(i):
                        for j in range(EPT):
                            pool.tensor_copy(si[:, j:j + 1], sidx[:, bass.ds(EPT * i + j, 1)])
                        pool.drain()
                        for j in range(EPT):
                            if j % EG == 0:
                                pool.wait_ge(s["ye"], 2 * i + j // EG + 1)
                            pool.tensor_tensor(sj[:, j:j + 1], si[:, j:j + 1], zero_i[:, :], ALU.add)
                            pool.drain()
                            pool.indirect_dma_start(out=ffn0[:, :],
                                                    out_offset=bass.IndirectOffsetOnAxis(ap=sj[:, j:j + 1], axis=0),
                                                    in_=ye[:, j, :], in_offset=None, bounds_check=TOK + CAP - 1,
                                                    compute_op=ALU.add).then_inc(added, 16)
                            pool.wait_ge(added, 16 * (EPT * i + j + 1))

                    def turn(i, first):
                        if not first:
                            pool.wait_ge(s["ye"], 2 * i)
                        pool.tensor_tensor(gj[:, :], zero_i[:, :], zero_i[:, :], ALU.add)
                        pool.tensor_copy(gi[:, :], gidx[:, bass.ds(EPT * i, EPT)])
                        pool.drain()
                        for j in range(EPT):
                            pool.indirect_dma_start(out=xe[:, j, :], out_offset=None, in_=xw[:, :],
                                                    in_offset=bass.IndirectOffsetOnAxis(ap=gi[:, j:j + 1], axis=0),
                                                    bounds_check=TOK - 1).then_inc(rows_in[j], 16)
                        for g in range(2):
                            rstd_step(pool, s, B + 2 * i + g, g, "stats1", "rstd1")
                        if not first:
                            scatters(i - 1)
                        for g in range(2):
                            rstd_step(pool, s, B + 2 * i + g, g, "stats2", "rstd2")

                    turn(0, True)
                    with pool.Fori(1, HALF) as i:
                        turn(i, False)
                    scatters(HALF - 1)

                @block.tensor
                def _(pe):
                    with pe.Fori(0, HALF) as i:
                        def experts(part):
                            for g in range(2):
                                u = 2 * i + g
                                for j in range(EG):
                                    n = EG * g + j
                                    if part == 0:
                                        pe.wait_ge(rows_in[n], 16 * (i + 1))
                                        last = pe.matmul(bank(g, S0)[:, j * CAP:(j + 1) * CAP], xe[:, n, 0:C],
                                                         ident[0:CAP, 0:CAP], start=True, stop=True)
                                    if part == 1:
                                        if j == 0:
                                            pe.wait_ge(s["xeT"], u + 1)
                                            pe.wait_ge(we_in, 32 * (i + 1))
                                        last = pe.matmul(bank(g, S1)[0:CAP, j * S:j * S + 2 * F0], xeT[:, n, :],
                                                         wg[:, n, :], start=True, stop=True)
                                    if part == 2:
                                        last = pe.matmul(bank(g, T)[0:F0, j * CAP:(j + 1) * CAP], he[:, n, :],
                                                         ident[0:CAP, 0:CAP], start=True, stop=True)
                                    if part == 3:
                                        if j == 0:
                                            pe.wait_ge(s["ehT"], u + 1)
                                        last = pe.matmul(bank(g, T)[0:CAP, S + j * C:S + (j + 1) * C], heT[:, n, :],
                                                         wdn[:, n, :], start=True, stop=True)
                                last.then_inc(s[("xeTp", "eg", "ehTp", "ey")[part]], 1)
                        layer_tensor(pe, s, i, 1, between=experts, hidden_free=s["eh"])

                @block.scalar
                def _(act):
                    with act.Fori(0, HALF) as i:
                        def rows():
                            for g in range(2):
                                act.wait_ge(s["xeTp"], 2 * i + g + 1)
                                act.activation(xeT[:, EG * g:EG * (g + 1), :].rearrange("p j c -> p (j c)"),
                                               bank(g, S0)[:, 0:EG * CAP], ACT.Copy).then_inc(s["xeT"], 1)

                        def silu():
                            for g in range(2):
                                act.wait_ge(s["eg"], 2 * i + g + 1)
                                act.activation(he[:, EG * g:EG * (g + 1), :],
                                               bank(g, S1)[0:CAP, :].rearrange("p (j f) -> p j f", j=EG)[:, :, 0:F0],
                                               ACT.Silu).then_inc(s["es"], 1)
                        layer_scalar(act, s, i, 1, before_norm2=rows, before_hidden=silu)

                @block.vector
                def _(dve):
                    with dve.Fori(0, HALF) as i:
                        def hidden():
                            for g in range(2):
                                e = slice(EG * g, EG * (g + 1))
                                dve.wait_ge(s["es"], 2 * i + g + 1)
                                dve.tensor_tensor(he[:, e, :],
                                                  bank(g, S1)[0:CAP, :].rearrange("p (j f) -> p j f", j=EG)
                                                  [:, :, F0:2 * F0], he[:, e, :], ALU.mult).then_inc(s["eh"], 1)
                            for g in range(2):
                                dve.wait_ge(s["ehTp"], 2 * i + g + 1)
                                dve.tensor_copy(heT[:, EG * g:EG * (g + 1), :].rearrange("p j c -> p (j c)"),
                                                bank(g, T)[0:F0, 0:EG * CAP]).then_inc(s["ehT"], 1)

                        def weighted():
                            for g in range(2):
                                dve.wait_ge(s["ey"], 2 * i + g + 1)
                                for j in range(EG):
                                    n = EG * g + j
                                    last = dve.tensor_scalar(ye[:, n, :], bank(g, T)[0:CAP, S + j * C:S + (j + 1) * C],
                                                             xe[:, n, bass.ds(EPT * i + C + n, 1)], None, ALU.mult)
                                last.then_inc(s["ye"], 1)

                        def from_x(g, t):
                            return X[:, TPU * i + HT * g + t, :]
                        layer_vector(dve, s, i, 1, from_x, before_hidden=hidden, after_y=weighted)
        stage2()

        EID = sb("EID", [P, NT])
        RNK = sb("RNK", [P, NT])
        SLOT = sb("SLOT", [P, NT], I32)
        TE = sb("TE", [1, SORTED_TILES], I32)
        cum = sb("cum", [P, 2, E1], BF16)

        def stage3():
            s = dict(norm_sems)
            s.update(sems("s3", ["gsil", "x1", "proj", "biased", "silu", "sq", "n2",
                            "nrm", "kn", "lg", "top", "tanh", "xs", "oh", "cum", "rank", "rankrd", "gu", "sgate",
                            "hmul", "down", "sh", "states", "state", "qTp", "qT", "lin", "stats2", "rstd2", "z2",
                            "zTp", "zT", "wo", "s1"]))
            xin3 = late([P, 2, TPU, C])
            gin = late([P, 2, TPU, C])
            x1b = late([P, 2, TPU, C])
            pj = [pr[:, g, :, :, :].rearrange("p a b c -> p (a b c)") for g in range(2)]
            qkp = [ctx.enter_context(nc.sbuf_tensor(f"qkp{g}", [P, TPU, 3 * C], F32)) for g in range(2)]
            sqb = [pj[g][:, 0:TPU * 3 * C].rearrange("p (t c) -> p t c", t=TPU) for g in range(2)]
            vv = [pT[:, g, :, :, :].rearrange("p a b c -> p (a b c)")[:, 0:TPU * 2 * C]
                  .rearrange("p (t c) -> p t c", t=TPU) for g in range(2)]
            hid = [pT[:, g, :, :, :].rearrange("p a b c -> p (a b c)")[:, 512:1024] for g in range(2)]
            xn = z
            xnT3 = attT
            qT = qk[:, :, 0, :]
            stt_ = [qk[:, g, 1, 0:C] for g in range(2)]
            st0 = [qk[:, g, 1, C:2 * C] for g in range(2)]
            z2 = v
            xsb = att
            shb = late([P, 2, TPU, C])
            n2 = late([P, 2, NG])
            rn = late([P, 2, NG])
            lg1 = late([P, 2, TPU, E1])
            m8 = late([P, 2, TPU, 8])
            i8 = sb("i8", [P, 2, TPU, 8], U32)
            ei = late([P, 2, TPU])
            th = late([P, 2, TPU])
            sc = late([P, 2, TPU])
            rk = late([P, 2, TPU])
            oh = sb("oh", [P, 2, TPU, E1], BF16)
            ct = sb("ct", [P, 2, E1], BF16)
            junk = late([P, 2, TPU, E1])
            W_WO, W_GATE, W_SG, W_SU, W_SD = 640, 768, 800, 1056, 1312
            in_x = [sem(f"s3_in_x{g}") for g in range(2)]
            in_g = [sem(f"s3_in_g{g}") for g in range(2)]
            o_x1 = [sem(f"s3_o_x1{g}") for g in range(2)]
            o_xs = [sem(f"s3_o_xs{g}") for g in range(2)]
            o_sh = [sem(f"s3_o_sh{g}") for g in range(2)]
            we1_in = sem("s3_we1")
            ls, lb = (COL[:, DEPTH * NCOL + n:DEPTH * NCOL + n + 1] for n in range(2))

            with nc.Block() as block:
                @block.sync
                def _(sp):
                    def load(i, g):
                        sp.dma_start(xin3[:, g, :, :], x_t[:, tiles(i, g), :]).then_inc(in_x[g], 16)
                        sp.dma_start(gin[:, g, :, :], ffn0_t[:, tiles(i, g), :]).then_inc(in_g[g], 16)

                    def turn(i, last):
                        for g in range(2):
                            sp.wait_ge(s["x1"], 2 * i + g + 1)
                            if not last:
                                load(i + 1, g)
                            sp.dma_start(x1_t[:, tiles(i, g), :], x1b[:, g, :, :]).then_inc(o_x1[g], 16)
                        for g in range(2):
                            sp.wait_ge(s["xs"], 2 * i + g + 1)
                            sp.dma_start(xs_t[:, tiles(i, g), :], xsb[:, g, :, :]).then_inc(o_xs[g], 16)
                        for g in range(2):
                            sp.wait_ge(s["sh"], 2 * i + g + 1)
                            sp.dma_start(sh_t[:, tiles(i, g), :], shb[:, g, :, :]).then_inc(o_sh[g], 16)

                    for g in range(2):
                        load(0, g)
                    sp.dma_start(big[:, :], we1, max_dma_last_dim=32768).then_inc(we1_in, 16)
                    with sp.Fori(0, HALF - 1) as i:
                        turn(i, False)
                    turn(HALF - 1, True)
                    sp.wait_ge(we1_in, 16)
                    for g in range(2):
                        sp.wait_ge(o_x1[g], 16 * HALF)
                        sp.wait_ge(o_xs[g], 16 * HALF)
                        sp.wait_ge(o_sh[g], 16 * HALF)

                @block.gpsimd
                def _(pool):
                    pool.memset(cum[:, :, :], 0.0)
                    pool.drain()
                    pool.tensor_tensor(ct[:, 0, :], cum[:, 0, :], cum[:, 1, :], ALU.add).then_inc(s["cum"], 1)
                    with pool.Fori(0, HALF) as i:
                        for g in range(2):
                            pool.wait_ge(s["gsil"], 2 * i + g + 1)
                            pool.tensor_tensor(gin[:, g, :, :], gin[:, g, :, :], X[:, tiles(i, g), :], ALU.mult)
                            pool.drain()
                            pool.tensor_tensor(x1b[:, g, :, :], gin[:, g, :, :], xin3[:, g, :, :], ALU.add)\
                                .then_inc(s["x1"], 1)
                        for g in range(2):
                            rstd_step(pool, s, B + 2 * i + g, g, "stats0", "rstd0")
                        for g in range(2):
                            u = 2 * i + g
                            pool.wait_ge(s["oh"], u + 1)
                            pool.tensor_tensor(ct[:, g, :], oh[:, g, 0, :], oh[:, g, 1, :], ALU.add)
                            pool.drain()
                            if g == 1:
                                pool.wait_ge(s["rank"], 2 * i + 1)
                            pool.tensor_tensor(cum[:, 1 - g, :], cum[:, g, :], ct[:, g, :], ALU.add)\
                                .then_inc(s["cum"], 1)
                        for g in range(2):
                            pool.wait_ge(s["n2"], 2 * i + g + 1)
                            pool.tensor_tensor(n2[:, g, :], n2[:, g, :], PHALF[:, :], ALU.pow)
                            pool.drain()
                            pool.tensor_tensor(n2[:, g, :], n2[:, g, :], EPS6[:, :], ALU.add).then_inc(s["nrm"], 1)
                        for g in range(2):
                            rstd_step(pool, s, 2 * i + g, g, "stats2", "rstd2")

                @block.tensor
                def _(pe):
                    with pe.Fori(0, HALF) as i:
                        for g in range(2):
                            pe.wait_ge(s["xn"], B + 2 * i + g + 1)
                            transpose_unit(pe, g, T, 0, xn, s["xnTp"])
                        for g in range(2):
                            pe.wait_ge(s["xnT"], B + 2 * i + g + 1)
                            for t in range(TPU):
                                xt = xnT3[:, g, t * P:(t + 1) * P]
                                pe.matmul(bank(g, (S0, Q)[t]), xt, W1[:, 0:4 * C], start=True, stop=True)
                                pe.matmul(bank(g, S1)[:, t * C:(t + 1) * C], xt, W1[:, 4 * C:5 * C],
                                          start=True, stop=True)
                                last = pe.matmul(bank(g, T)[:, S + t * E1:S + (t + 1) * E1], xt,
                                                 W1[:, W_GATE:W_GATE + E1], start=True, stop=True)
                            last.then_inc(s["proj"], 1)
                        for g in range(2):
                            u = 2 * i + g
                            pe.wait_ge(s["oh"], u + 1)
                            pe.wait_ge(s["cum"], u + 1)
                            for t in range(TPU):
                                r = bank(g, S1)[:, t * E1:(t + 1) * E1]
                                pe.matmul(r, TRI[:, :], oh[:, g, t, :], start=True, stop=False)
                                if t:
                                    pe.matmul(r, ONES[:, :], oh[:, g, 0, :], start=False, stop=False)
                                last = pe.matmul(r, ONES[:, :], cum[:, g, :], start=False, stop=True)
                            last.then_inc(s["rank"], 1)
                        for g in range(2):
                            pe.wait_ge(s["rankrd"], 2 * i + g + 1)
                            for n in range(2 * TPU):
                                w = W1[:, W_SG + n * P:W_SG + (n + 1) * P]
                                last = pe.matmul(bank(g, S0 + n // 2)[:, n % 2 * S:(n % 2 + 1) * S], w,
                                                 xnT3[:, g, :], start=True, stop=True)
                            last.then_inc(s["gu"], 1)
                        for g in range(2):
                            pe.wait_ge(s["kn"], 2 * i + g + 1)
                            for k in range(2):
                                for t in range(TPU):
                                    last = pe.matmul(bank(g, Q)[:, k * C:(k + 1) * C],
                                                     qkp[g][:, t, (k + 1) * C:(k + 2) * C],
                                                     vv[g][:, t, k * C:(k + 1) * C],
                                                     start=(t == 0), stop=(t == TPU - 1))
                            last.then_inc(s["states"], 1)
                            for t in range(TPU):
                                last = pe.transpose(bank(g, T)[:, t * P:(t + 1) * P], qkp[g][:, t, 0:C], ident)
                            last.then_inc(s["qTp"], 1)
                        for g in range(2):
                            pe.wait_ge(s["hmul"], 2 * i + g + 1)
                            for t in range(TPU):
                                for n in range(2):
                                    last = pe.matmul(bank(g, S0)[:, t * C:(t + 1) * C],
                                                     hid[g][:, n * S + t * P:n * S + (t + 1) * P],
                                                     W1[:, W_SD + n * C:W_SD + (n + 1) * C],
                                                     start=(n == 0), stop=(n == 1))
                            last.then_inc(s["down"], 1)
                        for g in range(2):
                            pe.wait_ge(s["qT"], 2 * i + g + 1)
                            pe.wait_ge(s["state"], 2 * i + g + 1)
                            for t in range(TPU):
                                last = pe.matmul(bank(g, Q)[:, S + t * C:S + (t + 1) * C], qT[:, g, t * P:(t + 1) * P],
                                                 stt_[g], start=True, stop=True)
                            last.then_inc(s["lin"], 1)
                        for g in range(2):
                            pe.wait_ge(s["z2"], 2 * i + g + 1)
                            transpose_unit(pe, g, T, 0, z2, s["zTp"])
                        for g in range(2):
                            pe.wait_ge(s["zT"], 2 * i + g + 1)
                            for t in range(TPU):
                                last = pe.matmul(bank(g, Q)[:, t * C:(t + 1) * C], zT[:, g, t * P:(t + 1) * P],
                                                 W1[:, W_WO:W_WO + C], start=True, stop=True)
                            last.then_inc(s["wo"], 1)

                @block.scalar
                def _(act):
                    with act.Fori(0, HALF) as i:
                        for g in range(2):
                            act.wait_ge(in_g[g], 16 * (i + 1))
                            act.wait_ge(in_x[g], 16 * (i + 1))
                            act.activation(gin[:, g, :, :], gin[:, g, :, :], ACT.Silu).then_inc(s["gsil"], 1)
                        for g in range(2):
                            act.wait_ge(s["xnTp"], B + 2 * i + g + 1)
                            act.activation(xnT3[:, g, :], bank(g, T)[:, 0:S], ACT.Copy).then_inc(s["xnT"], 1)
                        for g in range(2):
                            act.wait_ge(s["biased"], 2 * i + g + 1)
                            act.activation(qkp[g][:, :, :], qkp[g][:, :, :], ACT.Silu).then_inc(s["silu"], 1)
                            act.drain()
                            act.activation(sqb[g], qkp[g][:, :, :], ACT.Square, bias=PHALF[:, 0:1]).then_inc(s["sq"], 1)
                        for g in range(2):
                            act.wait_ge(s["top"], 2 * i + g + 1)
                            act.activation(th[:, g, :], m8[:, g, :, 0], ACT.Tanh, scale=0.5).then_inc(s["tanh"], 1)
                        for g in range(2):
                            act.wait_ge(s["gu"], 2 * i + g + 1)
                            act.activation(hid[g], bank(g, S0), ACT.Silu).then_inc(s["sgate"], 1)
                        for g in range(2):
                            act.wait_ge(s["qTp"], 2 * i + g + 1)
                            act.activation(qT[:, g, :], bank(g, T)[:, 0:S], ACT.Copy).then_inc(s["qT"], 1)
                        for g in range(2):
                            act.wait_ge(s["down"], 2 * i + g + 1)
                            act.activation(shb[:, g, :, :].rearrange("p t c -> p (t c)"), bank(g, S0)[:, 0:S], ACT.Copy)\
                               .then_inc(s["sh"], 1)
                        for g in range(2):
                            act.wait_ge(s["zTp"], 2 * i + g + 1)
                            affine_step(act, g, ls, lb, s["zT"])
                        for g in range(2):
                            act.wait_ge(o_x1[g], 16 * (i + 1))
                            act.wait_ge(o_xs[g], 16 * (i + 1))
                            act.wait_ge(o_sh[g], 16 * (i + 1))

                @block.vector
                def _(dve):
                    with dve.Fori(0, HALF) as i:
                        for g in range(2):
                            dve.wait_ge(s["x1"], 2 * i + g + 1)
                            stats_step(dve, g, lambda t: x1b[:, g, t, :], s["stats0"])
                        for g in range(2):
                            dve.wait_ge(s["rstd0"], B + 2 * i + g + 1)
                            norm_step(dve, g, lambda t: x1b[:, g, t, :], lambda t: xn[:, g, t, :], s["xn"])
                        for g in range(2):
                            dve.wait_ge(s["proj"], 2 * i + g + 1)
                            bias = ROW[:, DEPTH * C:DEPTH * C + NP]
                            for t in range(TPU):
                                b = bank(g, (S0, Q)[t])
                                last = dve.tensor_tensor(qkp[g][:, t, :], b[:, 0:3 * C], bias[:, 0:3 * C], ALU.add)
                            last.then_inc(s["biased"], 1)
                            for t in range(TPU):
                                b = bank(g, (S0, Q)[t])
                                dve.tensor_tensor(vv[g][:, t, 0:C], b[:, 3 * C:4 * C], bias[:, 3 * C:4 * C], ALU.add)
                            dve.tensor_tensor(vv[g][:, :, C:2 * C],
                                              bank(g, S1)[:, 0:S].rearrange("p (t c) -> p t c", t=TPU),
                                              bias[:, 4 * C:5 * C].unsqueeze(1).to_broadcast([P, TPU, C]), ALU.add)
                            dve.tensor_copy(lg1[:, g, :, :].rearrange("p t e -> p (t e)"),
                                            bank(g, T)[:, S:S + TPU * E1]).then_inc(s["lg"], 1)
                            dve.drain()
                            for t in range(TPU):
                                last = dve.max(out=m8[:, g, t, :], in_=lg1[:, g, t, :])
                            last.then_inc(s["top"], 1)
                            dve.drain()
                            for t in range(TPU):
                                dve.max_index(out=i8[:, g, t, :], in_max=m8[:, g, t, :], in_values=lg1[:, g, t, :])
                            dve.drain()
                            dve.tensor_copy(ei[:, g, :], i8[:, g, :, 0])
                            dve.drain()
                            for t in range(TPU):
                                last = dve.tensor_scalar(oh[:, g, t, :], CST[:, C_IOTA:C_IOTA + E1], ei[:, g, t:t + 1],
                                                         None, ALU.is_equal)
                            last.then_inc(s["oh"], 1)
                            dve.tensor_copy(EID[:, tiles(i, g)], ei[:, g, :])
                        for g in range(2):
                            dve.wait_ge(s["rank"], 2 * i + g + 1)
                            for t in range(TPU):
                                last = dve.scalar_tensor_tensor(junk[:, g, t, :], bank(g, S1)[:, t * E1:(t + 1) * E1],
                                                                1.0, oh[:, g, t, :], ALU.mult, ALU.mult,
                                                                accum_out=rk[:, g, t:t + 1])
                            last.then_inc(s["rankrd"], 1)
                        dve.drain()
                        for g in range(2):
                            dve.tensor_copy(RNK[:, tiles(i, g)], rk[:, g, :])
                        for g in range(2):
                            dve.wait_ge(s["sq"], 2 * i + g + 1)
                            dve.tensor_reduce(n2[:, g, :], sqb[g].rearrange("p t (h d) -> p (t h) d", d=LD), X_AXIS,
                                              ALU.add).then_inc(s["n2"], 1)
                        for g in range(2):
                            dve.wait_ge(s["tanh"], 2 * i + g + 1)
                            dve.tensor_scalar(sc[:, g, :], th[:, g, :], 0.5, 0.5, ALU.mult, ALU.add)
                        dve.drain()
                        for g in range(2):
                            for t in range(TPU):
                                last = dve.tensor_scalar(xsb[:, g, t, :], xn[:, g, t, :], sc[:, g, t:t + 1], None,
                                                         ALU.mult)
                            last.then_inc(s["xs"], 1)
                        for g in range(2):
                            dve.wait_ge(s["nrm"], 2 * i + g + 1)
                            dve.reciprocal(rn[:, g, :], n2[:, g, :])
                            dve.drain()
                            f = qkp[g][:, :, :].rearrange("p t (h d) -> p (t h) d", d=LD)
                            dve.scalar_tensor_tensor(f, f, 0.5, rn[:, g, :].unsqueeze(2).to_broadcast([P, NG, LD]),
                                                     ALU.add, ALU.mult).then_inc(s["kn"], 1)
                        for g in range(2):
                            dve.wait_ge(s["sgate"], 2 * i + g + 1)
                            dve.tensor_tensor(hid[g], bank(g, S1), hid[g], ALU.mult).then_inc(s["hmul"], 1)
                        for g in range(2):
                            dve.wait_ge(s["states"], 2 * i + g + 1)
                            dve.tensor_tensor(st0[g], bank(g, Q)[:, 0:C], CST[:, C_BLK:C_BLK + C], ALU.mult)
                            dve.drain()
                            dve.tensor_tensor(stt_[g], bank(g, Q)[:, C:2 * C], st0[g], ALU.mult).then_inc(s["state"], 1)
                        for g in range(2):
                            dve.wait_ge(s["lin"], 2 * i + g + 1)
                            stats_step(dve, g, lambda t: bank(g, Q)[:, S + t * C:S + (t + 1) * C], s["stats2"])
                        for g in range(2):
                            dve.wait_ge(s["rstd2"], 2 * i + g + 1)
                            norm_step(dve, g, lambda t: bank(g, Q)[:, S + t * C:S + (t + 1) * C],
                                      lambda t: z2[:, g, t, :], s["z2"])
                        for g in range(2):
                            dve.wait_ge(s["wo"], 2 * i + g + 1)
                            for t in range(TPU):
                                last = dve.tensor_tensor(X[:, TPU * i + HT * g + t, :], bank(g, Q)[:, t * C:(t + 1) * C],
                                                         ROW[:, DEPTH * C + NP:DEPTH * C + NP + C], ALU.add)
                            last.then_inc(s["s1"], 1)
        stage3()

        def place():
            placed = [sem(f"pl_placed{b}") for b in range(2)]
            loaded = [sem(f"pl_loaded{b}") for b in range(2)]
            counted, slots = sem("pl_counted"), sem("pl_slots")
            cnt = late([P, E1])
            ci = sb("ci", [P, E1], I32)
            nt = late([P, E1])
            end = late([P, E1])
            off = late([P, E1])
            eq = pr[:, :, :, :, :].rearrange("p g a b c -> p (g a b c)")[:, 0:NT * E1].rearrange("p (t e) -> p t e", e=E1)
            sl = late([P, NT])
            xb = sb("xb", [P, 2, C])
            ix = sb("ix", [P, 2], I32)
            iy = sb("iy", [P, 2], I32)
            zi = sb("zi", [P, 1], I32)
            with nc.Block() as block:
                @block.tensor
                def _(pe):
                    pe.matmul(bank(0, T)[:, 0:E1], ONES[:, :], cum[:, 0, :], start=True, stop=True).then_inc(counted, 1)

                @block.vector
                def _(dve):
                    dve.wait_ge(counted, 1)
                    dve.tensor_scalar(ci[:, :], bank(0, T)[:, 0:E1], float(P - 1), None, ALU.add)
                    dve.drain()
                    dve.tensor_scalar(ci[:, :], ci[:, :], P.bit_length() - 1, None, ALU.logical_shift_right)
                    dve.drain()
                    dve.tensor_copy(nt[:, :], ci[:, :])
                    dve.drain()
                    dve.tensor_tensor_scan(end[:, :], nt[:, :], CST[:, C_ONE:C_ONE + E1], 0.0, ALU.add, ALU.mult)
                    dve.drain()
                    dve.tensor_tensor(off[:, :], end[:, :], nt[:, :], ALU.subtract)
                    dve.drain()
                    dve.tensor_scalar(off[:, :], off[:, :], float(P), None, ALU.mult)
                    dve.tensor_tensor(eq, EID[:, :].unsqueeze(2).to_broadcast([P, NT, E1]),
                                      CST[:, C_IOTA:C_IOTA + E1].unsqueeze(1).to_broadcast([P, NT, E1]), ALU.is_equal)
                    dve.drain()
                    dve.tensor_tensor(eq, eq, off[:, :].unsqueeze(1).to_broadcast([P, NT, E1]), ALU.mult)
                    dve.drain()
                    dve.tensor_reduce(sl[:, :], eq, X_AXIS, ALU.add)
                    dve.drain()
                    dve.tensor_tensor(SLOT[:, :], sl[:, :], RNK[:, :], ALU.add).then_inc(slots, 1)
                    te = pT[0:1, :, :, :, :].rearrange("p g a b c -> p (g a b c)")
                    for h in range(3):
                        n = SORTED_TILES // 3
                        part = te[:, 0:n * E1].rearrange("p (t e) -> p t e", e=E1)
                        t0 = C_TILE + h * n
                        dve.tensor_tensor(part, end[0:1, :].unsqueeze(1).to_broadcast([1, n, E1]),
                                          CST[0:1, t0:t0 + n].unsqueeze(2).to_broadcast([1, n, E1]), ALU.is_le)
                        dve.drain()
                        dve.tensor_reduce(tef[:, h * n:(h + 1) * n], part, X_AXIS, ALU.add)
                        dve.drain()
                    dve.tensor_scalar(TE[:, :], tef[:, :], float(E1 - 1), None, ALU.min)

                @block.sync
                def _(sp):
                    for b in range(2):
                        sp.dma_start(xb[:, b, :], xs_t[:, b, :]).then_inc(loaded[b], 16)
                    with sp.Fori(0, NT // 2 - 1) as j:
                        for b in range(2):
                            sp.wait_ge(placed[b], 16 * (j + 1))
                            sp.dma_start(xb[:, b, :], xs_t[:, 2 * j + 2 + b, :]).then_inc(loaded[b], 16)
                    for b in range(2):
                        sp.wait_ge(placed[b], 16 * (NT // 2))

                @block.gpsimd
                def _(pool):
                    pool.memset(zi[:, :], 0)
                    pool.drain()
                    pool.wait_ge(slots, 1)
                    with pool.Fori(0, NT // 2) as j:
                        pool.tensor_copy(ix[:, :], SLOT[:, bass.ds(2 * j, 2)])
                        pool.drain()
                        for b in range(2):
                            pool.wait_ge(loaded[b], 16 * (j + 1))
                            pool.tensor_tensor(iy[:, b:b + 1], ix[:, b:b + 1], zi[:, :], ALU.add)
                            pool.drain()
                            pool.indirect_dma_start(out=srt[:, :],
                                                    out_offset=bass.IndirectOffsetOnAxis(ap=iy[:, b:b + 1], axis=0),
                                                    in_=xb[:, b, :], in_offset=None,
                                                    bounds_check=SORTED_TILES * P - 1).then_inc(placed[b], 16)
                        for b in range(2):
                            pool.wait_ge(placed[b], 16 * (j + 1))

        tef = late([1, SORTED_TILES])
        place()

        row_in = [sem(f"row_in{k}") for k in range(IN_FLIGHT)]

        def stage4():
            n_t = IN_FLIGHT
            s = sems("s4", ["xTp", "xT", "gu", "silu", "h", "hTp", "hT", "yp", "y"])
            row_out = [sem(f"s4_out{k}") for k in range(n_t)]

            def four(buf, shape):
                flat = buf[:, :, :, :].rearrange("p g a b -> p (g a b)")
                return [flat[:, k * shape:(k + 1) * shape] for k in range(n_t)]
            xt = four(v, C)
            xT = [zT[:, k // 2, k % 2 * P:(k % 2 + 1) * P] for k in range(n_t)]
            yb = four(att, C)
            hb = [pr[:, k // 2, k % 2, :, :].rearrange("p a b -> p (a b)")[:, 0:F1] for k in range(n_t)]
            hT = [pT[:, k // 2, k % 2, :, :].rearrange("p a b -> p (a b)")[:, 0:F1] for k in range(n_t)]

            def gu(k):
                return ps[:, 2 * k, :]

            def misc(k):
                return ps[:, 2 * k + 1, :]
            turns = SORTED_TILES // n_t
            with nc.Block() as block:
                @block.sync
                def _(sp):
                    for k in range(n_t):
                        sp.dma_start(xt[k], srt_t[:, k, :]).then_inc(row_in[k], 16)

                    def turn(i, last):
                        for k in range(n_t):
                            if not last:
                                sp.wait_ge(s["xTp"], n_t * i + k + 1)
                                sp.dma_start(xt[k], srt_t[:, n_t * i + n_t + k, :]).then_inc(row_in[k], 16)
                        for k in range(n_t):
                            sp.wait_ge(s["y"], n_t * i + k + 1)
                            sp.dma_start(ys_t[:, n_t * i + k, :], yb[k]).then_inc(row_out[k], 16)
                    with sp.Fori(0, turns - 1) as i:
                        turn(i, False)
                    turn(turns - 1, True)
                    for k in range(n_t):
                        sp.wait_ge(row_out[k], 16 * turns)

                @block.tensor
                def _(pe):
                    with pe.Fori(0, turns) as i:
                        for k in range(n_t):
                            pe.wait_ge(row_in[k], 16 * (i + 1))
                            pe.transpose(misc(k)[:, 0:P], xt[k], ident).then_inc(s["xTp"], 1)
                        e = [pe.value_load(TE[0:1, bass.ds(n_t * i + k, 1)], min_val=0, max_val=E1 - 1)
                             for k in range(n_t)]
                        for k in range(n_t):
                            pe.wait_ge(s["xT"], n_t * i + k + 1)
                            pe.matmul(gu(k), xT[k], WE1[:, e[k], 0:2 * F1], start=True, stop=True).then_inc(s["gu"], 1)
                        for k in range(n_t):
                            pe.wait_ge(s["h"], n_t * i + k + 1)
                            for f in range(2):
                                last = pe.transpose(misc(k)[:, (f + 1) * P:(f + 2) * P], hb[k][:, f * P:(f + 1) * P],
                                                    ident)
                            last.then_inc(s["hTp"], 1)
                        for k in range(n_t):
                            pe.wait_ge(s["hT"], n_t * i + k + 1)
                            for f in range(2):
                                last = pe.matmul(gu(k)[:, 0:C], hT[k][:, f * P:(f + 1) * P],
                                                 WE1[:, e[k], 2 * F1 + f * C:2 * F1 + (f + 1) * C],
                                                 start=(f == 0), stop=(f == 1))
                            last.then_inc(s["yp"], 1)

                @block.scalar
                def _(act):
                    with act.Fori(0, turns) as i:
                        for k in range(n_t):
                            act.wait_ge(s["xTp"], n_t * i + k + 1)
                            act.activation(xT[k], misc(k)[:, 0:P], ACT.Copy).then_inc(s["xT"], 1)
                        for k in range(n_t):
                            act.wait_ge(s["gu"], n_t * i + k + 1)
                            act.activation(hb[k], gu(k)[:, 0:F1], ACT.Silu).then_inc(s["silu"], 1)
                        for k in range(n_t):
                            act.wait_ge(s["yp"], n_t * i + k + 1)
                            act.activation(yb[k], gu(k)[:, 0:C], ACT.Copy).then_inc(s["y"], 1)
                        for k in range(n_t):
                            act.wait_ge(row_out[k], 16 * (i + 1))

                @block.vector
                def _(dve):
                    with dve.Fori(0, turns) as i:
                        for k in range(n_t):
                            dve.wait_ge(s["silu"], n_t * i + k + 1)
                            dve.tensor_tensor(hb[k], gu(k)[:, F1:2 * F1], hb[k], ALU.mult).then_inc(s["h"], 1)
                        for k in range(n_t):
                            dve.wait_ge(s["hTp"], n_t * i + k + 1)
                            dve.tensor_copy(hT[k], misc(k)[:, P:3 * P]).then_inc(s["hT"], 1)
        stage4()

        def stage5():
            n_t = IN_FLIGHT
            s = sems("s5", ["sum", "silu", "res"])
            got = [sem(f"s5_got{k}") for k in range(n_t)]
            ld = sem("s5_ld")
            stored = sem("s5_stored")

            def four(buf):
                return buf[:, :, :, :].rearrange("p g a b -> p (g a) b")
            yg, a1, a2 = four(v), four(z), four(att)
            ob = qk[:, 0, :, :].rearrange("p n (b c) -> p (n b) c", c=C)
            turns = NT // n_t
            with nc.Block() as block:
                @block.sync
                def _(sp):
                    def load(i):
                        sp.dma_start(a1, x1_t[:, bass.ds(n_t * i, n_t), :]).then_inc(ld, 16)
                        sp.dma_start(a2, sh_t[:, bass.ds(n_t * i, n_t), :]).then_inc(ld, 16)

                    def turn(i, last):
                        sp.wait_ge(s["res"], i + 1)
                        if not last:
                            load(i + 1)
                        sp.dma_start(out_t[:, bass.ds(n_t * i, n_t), :], ob).then_inc(stored, 16)
                    load(0)
                    with sp.Fori(0, turns - 1) as i:
                        turn(i, False)
                    turn(turns - 1, True)
                    sp.wait_ge(stored, 16 * turns)

                @block.gpsimd
                def _(pool):
                    def turn(i, first):
                        if not first:
                            pool.wait_ge(s["sum"], i)
                        pool.tensor_tensor(iw[:, :], iw[:, :], iw[:, :], ALU.subtract)
                        pool.tensor_copy(iv[:, :], SLOT[:, bass.ds(n_t * i, n_t)])
                        pool.drain()
                        for k in range(n_t):
                            pool.indirect_dma_start(out=yg[:, k, :], out_offset=None, in_=ysd[:, :],
                                                    in_offset=bass.IndirectOffsetOnAxis(ap=iv[:, k:k + 1], axis=0),
                                                    bounds_check=SORTED_TILES * P - 1).then_inc(got[k], 16)
                    pool.memset(iw[:, :], 0)
                    pool.drain()
                    turn(0, True)
                    with pool.Fori(1, turns) as i:
                        turn(i, False)

                @block.scalar
                def _(act):
                    with act.Fori(0, turns) as i:
                        act.wait_ge(s["sum"], i + 1)
                        act.activation(a2, a2, ACT.Silu).then_inc(s["silu"], 1)

                @block.vector
                def _(dve):
                    def turn(i, first):
                        for k in range(n_t):
                            dve.wait_ge(got[k], 16 * (i + 1))
                        dve.wait_ge(ld, 32 * (i + 1))
                        dve.tensor_tensor(a2, a2, yg, ALU.add).then_inc(s["sum"], 1)
                        dve.wait_ge(s["silu"], i + 1)
                        dve.tensor_tensor(a2, a2, X[:, bass.ds(n_t * i, n_t), :], ALU.mult)
                        dve.drain()
                        if not first:
                            dve.wait_ge(stored, 16 * i)
                        dve.tensor_tensor(ob, a2, a1, ALU.add).then_inc(s["res"], 1)
                    turn(0, True)
                    with dve.Fori(1, turns) as i:
                        turn(i, False)
        iv = sb("iv", [P, IN_FLIGHT], I32)
        iw = sb("iw", [P, 1], I32)
        stage5()


def pack(inputs):
    import numpy as np
    a = {k: np.asarray(v) for k, v in inputs.items()}
    f = np.float32
    d = {}
    d["x"] = a["L0_attn_x"].reshape(TOK, C)
    w = []
    for l in range(DEPTH):
        w += [a["L0_attn_wq"][l], a["L0_attn_wk"][l], a["L0_attn_wv"][l], a["L0_attn_wo"][l], a["L0_attn_w1"][l],
              a["L0_attn_w2"][l].reshape(FC, P, C).transpose(1, 0, 2).reshape(P, FC * C)]
    d["w0"] = np.concatenate(w, axis=1)
    c = []
    for l in range(DEPTH):
        c += [a[f"L0_attn_{n}"][l][:, None] for n in ("ln1_g", "ln1_b", "ln2_g", "ln2_b", "bq", "bk")]
        c.append(a["L0_attn_b1"][l].reshape(FC, P).T)
    c += [a["L1_attn_ln_g"][:, None], a["L1_attn_ln_b"][:, None]]
    d["cols"] = np.concatenate(c, axis=1)
    r = np.concatenate([a["L0_attn_bv"].reshape(-1), a["L1_attn_bq"], a["L1_attn_bk"].reshape(-1),
                        a["L1_attn_bv"].reshape(-1), a["L1_attn_bo"]])
    d["rows"] = np.broadcast_to(r[None, :], (P, r.size))
    freq = np.array([float.fromhex(h) for h in (
        "0x1.0p+0", "0x1.1cfed8p+0", "0x1.3d466cp+0", "0x1.6135f6p+0", "0x1.89377ap+0", "0x1.b5c0fcp+0",
        "0x1.e755dep+0", "0x1.0f4432p+1", "0x1.2dfdb2p+1", "0x1.503210p+1", "0x1.764638p+1", "0x1.a0aa7ap+1",
        "0x1.cfdbe8p+1", "0x1.0232dcp+2", "0x1.1f7176p+2", "0x1.3ffffep+2")], f)
    rad = ((np.arange(1, S + 1, dtype=f)[None, :] * freq[:, None]) * f(np.pi)).astype(np.float64)
    rad = np.concatenate([rad, rad])
    sign = np.where(np.arange(2 * freq.size) % 2 == 0, -1.0, 1.0)[:, None]
    head = np.concatenate([np.sin(rad) + sign * np.cos(rad), np.ones((DH - 2 * freq.size, S))])
    rk = np.concatenate([head] * HEADS)
    d["rot"] = np.concatenate([rk * DH ** -0.5, rk], axis=1).astype(f)
    k = np.zeros((P, NCST), f)
    p = np.arange(P)
    k[:, C_ID:C_ID + P] = np.eye(P)
    k[:, C_BLK:C_BLK + P] = (p[:, None] // LD == p[None, :] // LD) * (1.0 / S) ** 2
    k[:, C_TRI:C_TRI + P] = p[:, None] < p[None, :]
    k[:, C_IOTA:C_IOTA + E1] = np.arange(E1)
    k[:, C_TOKV:C_TOKV + NT] = TOK - P * np.arange(NT)[None, :] - p[:, None]
    k[:, C_ONE:C_ONE + P] = 1.0
    k[:, C_P] = p
    k[:, C_TILE:] = np.arange(SORTED_TILES)
    d["cst"] = k
    d["ws"] = np.concatenate([a["L0_ffn_router_w"].T, a["L0_ffn_ws_gate_up"]], axis=1)
    d["wsd"] = a["L0_ffn_ws_down"]
    d["we0"] = np.concatenate([a["L0_ffn_w_gate"], a["L0_ffn_w_up"]], axis=2)
    d["wd0"] = a["L0_ffn_w_down"]
    d["w1"] = np.concatenate([a["L1_attn_Wq"].T, a["L1_attn_Wk"][0].T, a["L1_attn_Wk"][1].T, a["L1_attn_Wv"][0].T,
                              a["L1_attn_Wv"][1].T, a["L1_attn_Wo"].T, a["L1_ffn_gate_w"], a["L1_ffn_shared_gate_w"],
                              a["L1_ffn_shared_up_w"],
                              a["L1_ffn_shared_down_w"].reshape(2, P, C).transpose(1, 0, 2).reshape(P, 2 * C)], axis=1)
    e = np.concatenate([a["L1_ffn_routed_gate_w"], a["L1_ffn_routed_up_w"],
                        a["L1_ffn_routed_down_w"].reshape(E1, 2, P, C).transpose(0, 2, 1, 3).reshape(E1, P, 2 * C)],
                       axis=2)
    d["we1"] = e.transpose(1, 0, 2).reshape(P, E1 * 768)
    return {n: np.ascontiguousarray(v) for n, v in d.items()}


_ARGS = ["x", "w0", "cols", "rows", "rot", "cst", "ws", "wsd", "we0", "wd0", "w1", "we1"]


def kernel(**inputs):
    import concourse.bacc as _bacc
    from concourse import mybir as _mybir
    from concourse.bass_utils import run_bass_kernel_spmd as _run

    arrays = pack(inputs)
    nc = _bacc.Bacc("TRN2", target_bir_lowering=False, num_devices=1)
    args = [nc.dram_tensor(n, arrays[n].shape, _mybir.dt.from_np(arrays[n].dtype), kind="ExternalInput").ap()
            for n in _ARGS]
    out = nc.dram_tensor("out", (TOK, C), F32, kind="ExternalOutput").ap()
    mixed_layers(nc, *args, out)
    r = _run(nc, [arrays], core_ids=[0])
    return r.results[0]["out"].reshape(B, S, C)
```

```python
from contextlib import ExitStack

import concourse.bass as bass
from concourse import mybir

F32 = mybir.dt.float32
BF16 = mybir.dt.bfloat16
I32 = mybir.dt.int32
U32 = mybir.dt.uint32
ALU = mybir.AluOpType
ACT = mybir.ActivationFunctionType
X_AXIS = mybir.AxisListType.X

P = 128
C = 128
B = 32
S = 256
TOK = B * S
NT = TOK // P
TPU = S // P
HALF = B // 2
HT = NT // 2
DEPTH = 2
HEADS = 2
DH = C // HEADS
FC = 4
E0, CAP, F0 = 64, 64, 96
E1, F1 = 32, 256
LH, LD = 16, 8
NP = 5 * C
XW = C + E0
EPT = E0 // HALF
SORTED_TILES = NT + E1
IN_FLIGHT = 4
EPS = 1e-5
GELU = 1.702
NEG = -1e30

G1, B1, G2, B2, BQ, BK, BH = 0, 1, 2, 3, 4, 5, 6
NCOL = 6 + FC
C_ID, C_BLK, C_TRI, C_IOTA, C_TOKV, C_ONE, C_P = 0, 128, 256, 384, 416, 480, 608
C_TILE = 609
NCST = C_TILE + SORTED_TILES


def mixed_layers(nc, x, w0, cols, rows, rot, cst, ws, wsd, we0, wd0, w1, we1, out):
    xw = nc.dram_tensor("xw", (TOK, XW), F32, kind="Internal").ap()
    ffn0 = nc.dram_tensor("ffn0", (TOK + CAP, C), F32, kind="Internal").ap()
    x1d = nc.dram_tensor("x1d", (TOK, C), F32, kind="Internal").ap()
    shd = nc.dram_tensor("shd", (TOK, C), F32, kind="Internal").ap()
    xsd = nc.dram_tensor("xsd", (TOK, C), F32, kind="Internal").ap()
    srt = nc.dram_tensor("srt", (SORTED_TILES * P, C), F32, kind="Internal").ap()
    ysd = nc.dram_tensor("ysd", (SORTED_TILES * P, C), F32, kind="Internal").ap()

    def tiled(d):
        return d.rearrange("(t p) c -> p t c", p=P)

    x_t, xw_t, ffn0_t, x1_t, sh_t, xs_t = (tiled(d) for d in (x, xw, ffn0[0:TOK, :], x1d, shd, xsd))
    srt_t, ys_t, out_t = tiled(srt), tiled(ysd), tiled(out)

    ctx = ExitStack()
    with ctx:
        def sb(name, shape, dt=F32):
            return ctx.enter_context(nc.sbuf_tensor(name, shape, dt))

        def sem(name):
            return ctx.enter_context(nc.semaphore(name))

        def sems(stage, names):
            return {n: sem(f"{stage}_{n}") for n in names}

        ps = ctx.enter_context(nc.psum_tensor("ps", [P, 8, 512], F32))

        def bank(g, n):
            return ps[:, 4 * g + n, :]
        T, Q, S0, S1 = 0, 1, 2, 3

        X = sb("X", [P, NT, C])
        big = sb("big", [P, E1 * 768])
        keys = big[:, 0:HT * P]
        WE1 = big[:, :].rearrange("p (e f) -> p e f", e=E1)
        W0 = sb("W0", [P, DEPTH, 1536])

        def early(shape):
            return carve(big[:, :], early_at, shape)

        def late(shape):
            return carve(W0[:, :, :].rearrange("p d n -> p (d n)"), late_at, shape)
        early_at, late_at = [HT * P], [0]

        def carve(room, at, shape):
            n = 1
            for d in shape[1:]:
                n *= d
            at[0] += n
            assert at[0] <= room.shape[1]
            ap = room[0:shape[0], at[0] - n:at[0]]
            if len(shape) == 3:
                return ap.rearrange("p (a b) -> p a b", a=shape[1])
            if len(shape) == 4:
                return ap.rearrange("p (a b c) -> p a b c", a=shape[1], b=shape[2])
            return ap
        COL = sb("COL", [P, DEPTH * NCOL + 2])
        BHS = sb("BHS", [P, DEPTH, FC])
        ROW = sb("ROW", [P, DEPTH * C + NP + C])
        ROT = sb("ROT", [P, 2 * S])
        CST = sb("CST", [P, NCST])
        TRI = sb("TRI", [P, P], BF16)
        ONES = sb("ONES", [P, P], BF16)
        WS = sb("WS", [P, E0 + 2 * F0])
        WSD = sb("WSD", [F0, C])
        W1 = sb("W1", [P, 1568])
        MHALF = sb("MHALF", [P, 4])
        NG = 3 * LH * TPU
        PHALF = sb("PHALF", [P, 1])

        z0 = early([P, 2, TPU, C])
        z = sb("z", [P, 2, TPU, C])
        zT = sb("zT", [P, 2, S])
        xnT = early([P, 2, S])
        qk = sb("qk", [P, 2, 2, S])
        v = sb("v", [P, 2, TPU, C])
        pr = sb("pr", [P, 2, HEADS, TPU, S])
        pT = sb("pT", [P, 2, HEADS, TPU, S])
        att = sb("att", [P, 2, TPU, C])
        attT = sb("attT", [P, 2, S])
        st = sb("st", [P, 2, TPU, 6])
        mv = sb("mv", [P, 2, TPU, 2])
        ve = sb("ve", [P, 2, TPU])
        rs = sb("rs", [P, 2, TPU])
        nmx = sb("nmx", [P, 2, HEADS * TPU])
        sm = sb("sm", [P, 2, TPU, HEADS])
        rsm = sb("rsm", [P, 2, TPU, HEADS])
        xin = early([P, 2, TPU, C])
        ff = early([P, 2, TPU, C])

        ident = CST[:, C_ID:C_ID + P]

        def col(l, c):
            return COL[:, l * NCOL + c:l * NCOL + c + 1]

        def tiles(i, g):
            return bass.ds(TPU * i + HT * g, TPU)

        ld_small, prep, ld_w, zeroed = sem("ld_small"), sem("prep"), sem("ld_w"), sem("zeroed")
        zero = early([P, C])
        with nc.Block() as block:
            @block.sync
            def _(sp):
                for dst, src in ((CST, cst), (COL, cols), (ROW, rows), (ROT, rot), (WS, ws), (WSD, wsd), (W1, w1)):
                    sp.dma_start(dst[:, :], src).then_inc(ld_small, 16)
                sp.dma_start(W0[:, :, :].rearrange("p d n -> p (d n)"), w0).then_inc(ld_w, 16)
                sp.wait_ge(ld_small, 7 * 16)
                sp.wait_ge(ld_w, 16)

            @block.scalar
            def _(act):
                act.wait_ge(prep, 1)
                act.dma_start(srt_t, zero[:, :].unsqueeze(1).to_broadcast([P, SORTED_TILES, C])).then_inc(zeroed, 16)

            @block.gpsimd
            def _(pool):
                pool.memset(zero[:, :], 0.0).then_inc(prep, 1)
                pool.memset(MHALF[:, 0:2], -0.5)
                pool.memset(MHALF[:, 2:4], EPS)
                pool.memset(PHALF[:, :], 0.5)

            @block.vector
            def _(dve):
                dve.wait_ge(ld_small, 7 * 16)
                dve.tensor_copy(TRI[:, :], CST[:, C_TRI:C_TRI + P])
                dve.tensor_copy(ONES[:, :], CST[:, C_ONE:C_ONE + P])
                for l in range(DEPTH):
                    dve.tensor_scalar(BHS[:, l, :], COL[:, l * NCOL + BH:l * NCOL + BH + FC], GELU, None, ALU.mult)
                for n in range(NP // C):
                    dve.tensor_tensor(W1[:, n * C:(n + 1) * C], W1[:, n * C:(n + 1) * C], ident, ALU.add)
                dve.wait_ge(ld_w, 16)
                for l in range(DEPTH):
                    dve.tensor_scalar(W0[:, l, 1024:1536], W0[:, l, 1024:1536], 1.0 / GELU, None, ALU.mult)

        LAYER = ["stats1", "rstd1", "z1", "zT1", "xl1", "qkv", "qkv_sb", "scores", "mx", "probs", "pT", "pT_A", "pT_B",
                 "pv", "att", "attTp", "attT", "wo", "stats2", "rstd2", "z2", "zT2", "xl2", "hid", "hT", "y", "xout"]

        layer_sems = sems("layer", LAYER)
        norm_sems = sems("norm", ["stats0", "rstd0", "xn", "xnTp", "xnT"])

        norm_bufs = (st, mv, ve, rs)

        def rstd_step(pool, s, u, g, ready, done, bufs=norm_bufs):
            _, mv, ve, rs = bufs
            pool.wait_ge(s[ready], u + 1)
            pool.tensor_tensor(ve[:, g, :], mv[:, g, :, 1], MHALF[:, 2:4], ALU.add)
            pool.drain()
            pool.tensor_tensor(rs[:, g, :], ve[:, g, :], MHALF[:, 0:2], ALU.pow).then_inc(s[done], 1)

        def stats_step(dve, g, src, done, bufs=norm_bufs):
            st, mv, _, _ = bufs
            for t in range(TPU):
                dve.bn_stats(st[:, g, t, :], src(t))
            dve.drain()
            for t in range(TPU):
                last = dve.bn_aggr(mv[:, g, t, :], st[:, g, t, :])
            last.then_inc(done, 1)

        def norm_step(dve, g, src, dst, done, bufs=norm_bufs):
            _, mv, _, rs = bufs
            for t in range(TPU):
                last = dve.tensor_scalar(dst(t), src(t), mv[:, g, t, 0:1], rs[:, g, t:t + 1], ALU.subtract, ALU.mult)
            last.then_inc(done, 1)

        def transpose_unit(pe, g, b, c0, src, done):
            for t in range(TPU):
                last = pe.transpose(bank(g, b)[:, c0 + t * P:c0 + (t + 1) * P], src[:, g, t, :], ident)
            last.then_inc(done, 1)

        def front_tensor(pe, s, i, l):
            for g in range(2):
                pe.wait_ge(s["z1"], 2 * (i + HALF * l) + g + 1)
                transpose_unit(pe, g, T, 0, z, s["zT1"])

        def layer_tensor(pe, s, i, l, after_att, after_wo, after_norm2, after_hidden, after_y, after_scores=None,
                         logits_read=None, hidden_free=None, ff_read=None):
            n0 = i + HALF * l
            wq, wk, wv, wo = (W0[:, l, n * C:(n + 1) * C] for n in range(4))
            for g in range(2):
                u = 2 * n0 + g
                pe.wait_ge(s["xl1"], u + 1)
                for n, w in enumerate((wq, wk)):
                    pe.matmul(bank(g, Q)[:, n * S:(n + 1) * S], w, zT[:, g, :], start=True, stop=True)
                for t in range(TPU):
                    last = pe.matmul(bank(g, T)[:, S + t * C:S + (t + 1) * C], zT[:, g, t * P:(t + 1) * P], wv,
                                     start=True, stop=True)
                last.then_inc(s["qkv"], 1)
            for g in range(2):
                u = 2 * n0 + g
                pe.wait_ge(s["qkv_sb"], u + 1)
                if logits_read:
                    pe.wait_ge(logits_read, 2 * i + g + 1)
                for h in range(HEADS):
                    d = slice(h * DH, (h + 1) * DH)
                    for t in range(TPU):
                        last = pe.matmul(bank(g, S0 + h)[:, t * S:(t + 1) * S], qk[d, g, 0, t * P:(t + 1) * P],
                                         qk[d, g, 1, :], start=True, stop=True)
                    last.then_inc(s["scores"], 1)
            if after_scores:
                after_scores()
            for g in range(2):
                u = 2 * n0 + g
                for h in range(HEADS):
                    pe.wait_ge(s["probs"], HEADS * u + h + 1)
                    for t in range(TPU):
                        for k in range(TPU):
                            last = pe.transpose(bank(g, S0 + h)[:, k * S + t * P:k * S + (t + 1) * P],
                                                pr[:, g, h, t, k * P:(k + 1) * P], ident)
                    last.then_inc(s["pT"], 1)
            for g in range(2):
                for h in range(HEADS):
                    pe.wait_ge(s[("pT_A", "pT_B")[g]], HEADS * n0 + h + 1)
                    for t in range(TPU):
                        for k in range(TPU):
                            last = pe.matmul(bank(g, Q)[:, t * C + h * DH:t * C + (h + 1) * DH],
                                             pT[:, g, h, k, t * P:(t + 1) * P], v[:, g, k, h * DH:(h + 1) * DH],
                                             start=(k == 0), stop=(k == TPU - 1))
                last.then_inc(s["pv"], 1)
            for g in range(2):
                u = 2 * n0 + g
                pe.wait_ge(s["att"], u + 1)
                transpose_unit(pe, g, T, 0, att, s["attTp"])
                after_att(g)
            for g in range(2):
                u = 2 * n0 + g
                pe.wait_ge(s["attT"], u + 1)
                for t in range(TPU):
                    last = pe.matmul(bank(g, Q)[:, S + t * C:S + (t + 1) * C], attT[:, g, t * P:(t + 1) * P], wo,
                                     start=True, stop=True)
                last.then_inc(s["wo"], 1)
            after_wo()
            for g in range(2):
                u = 2 * n0 + g
                pe.wait_ge(s["z2"], u + 1)
                transpose_unit(pe, g, T, 0, z, s["zT2"])
            after_norm2()
            for g in range(2):
                u = 2 * n0 + g
                pe.wait_ge(s["xl2"], u + 1)
                if hidden_free:
                    pe.wait_ge(hidden_free, 2 * i + g + 1)
                for f in range(FC):
                    last = pe.matmul(bank(g, S0 + f // 2)[:, f % 2 * S:(f % 2 + 1) * S],
                                     W0[:, l, 512 + f * P:512 + (f + 1) * P], zT[:, g, :], start=True, stop=True)
                    if f % 2:
                        last.then_inc(s["hid"], 1)
            after_hidden()
            for g in range(2):
                u = 2 * n0 + g
                pe.wait_ge(s["hT"], u + 1)
                if ff_read:
                    pe.wait_ge(ff_read, 2 * i + g + 1)
                for t in range(TPU):
                    for f in range(FC):
                        last = pe.matmul(bank(g, Q)[:, t * C:(t + 1) * C],
                                         pr[:, g, f // 2, f % 2, t * P:(t + 1) * P],
                                         W0[:, l, 1024 + f * C:1024 + (f + 1) * C], start=(f == 0), stop=(f == FC - 1))
                last.then_inc(s["y"], 1)
            after_y()
            for g in range(2):
                pe.wait_ge(s["xout"], 2 * n0 + g + 1)

        def affine_step(act, g, scale, bias, done):
            act.activation(zT[:, g, :], bank(g, T)[:, 0:S], ACT.Identity, bias=bias, scale=scale).then_inc(done, 1)

        def front_scalar(act, s, i, l):
            for g in range(2):
                act.wait_ge(s["zT1"], 2 * (i + HALF * l) + g + 1)
                affine_step(act, g, col(l, G1), col(l, B1), s["xl1"])

        def layer_scalar(act, s, i, l, before_norm2, before_scores=None):
            n0 = i + HALF * l
            if before_scores:
                before_scores()
            for g in range(2):
                for h in range(HEADS):
                    act.wait_ge(s["mx"], HEADS * (2 * n0 + g) + h + 1)
                    for t in range(TPU):
                        last = act.activation(pr[:, g, h, t, :], bank(g, S0 + h)[:, t * S:(t + 1) * S], ACT.Exp,
                                              bias=nmx[:, g, h * TPU + t:h * TPU + t + 1],
                                              accum_out=sm[:, g, t, h:h + 1])
                    last.then_inc(s["probs"], 1)
            for h in range(HEADS):
                act.wait_ge(s["pT"], HEADS * (2 * n0 + 1) + h + 1)
                act.activation(pT[:, 1, h, :, :].rearrange("p k q -> p (k q)"), bank(1, S0 + h), ACT.Copy)\
                   .then_inc(s["pT_B"], 1)
            before_norm2()
            for g in range(2):
                act.wait_ge(s["zT2"], 2 * n0 + g + 1)
                affine_step(act, g, col(l, G2), col(l, B2), s["xl2"])
            for g in range(2):
                for f in range(FC):
                    if f % 2 == 0:
                        act.wait_ge(s["hid"], 2 * (2 * n0 + g) + f // 2 + 1)
                    last = act.activation(pr[:, g, f // 2, f % 2, :], bank(g, S0 + f // 2)[:, f % 2 * S:(f % 2 + 1) * S],
                                          ACT.Silu, bias=BHS[:, l, f:f + 1], scale=GELU)
                last.then_inc(s["hT"], 1)

        def front_vector(dve, s, i, l, src):
            for g in range(2):
                stats_step(dve, g, lambda t: src(i, g, t), s["stats1"])
            for g in range(2):
                dve.wait_ge(s["rstd1"], 2 * (i + HALF * l) + g + 1)
                norm_step(dve, g, lambda t: src(i, g, t), lambda t: z[:, g, t, :], s["z1"])

        def layer_vector(dve, s, i, l, src, before_hidden, ahead, after_y, after_scores=None):
            n0 = i + HALF * l
            for g in range(2):
                dve.wait_ge(s["qkv"], 2 * n0 + g + 1)
                for n, c in enumerate((BQ, BK)):
                    dve.scalar_tensor_tensor(qk[:, g, n, :], bank(g, Q)[:, n * S:(n + 1) * S], col(l, c),
                                             ROT[:, n * S:(n + 1) * S], ALU.add, ALU.mult)
                dve.tensor_tensor(v[:, g, :, :], bank(g, T)[:, S:2 * S].rearrange("p (t c) -> p t c", t=TPU),
                                  ROW[:, l * C:(l + 1) * C].unsqueeze(1).to_broadcast([P, TPU, C]), ALU.add)\
                   .then_inc(s["qkv_sb"], 1)
            for g in range(2):
                for h in range(HEADS):
                    dve.wait_ge(s["scores"], HEADS * (2 * n0 + g) + h + 1)
                    dve.tensor_reduce(nmx[:, g, h * TPU:(h + 1) * TPU],
                                      bank(g, S0 + h).rearrange("p (t k) -> p t k", t=TPU),
                                      X_AXIS, ALU.max, negate=True).then_inc(s["mx"], 1)
            if after_scores:
                after_scores()
            for h in range(HEADS):
                dve.wait_ge(s["pT"], HEADS * 2 * n0 + h + 1)
                dve.tensor_copy(pT[:, 0, h, :, :].rearrange("p k q -> p (k q)"), bank(0, S0 + h))\
                   .then_inc(s["pT_A"], 1)
            dve.wait_ge(s["probs"], HEADS * (2 * n0 + 2))
            dve.reciprocal(rsm[:, :, :, :], sm[:, :, :, :])
            dve.drain()
            for g in range(2):
                dve.wait_ge(s["pv"], 2 * n0 + g + 1)
                dve.tensor_tensor(att[:, g, :, :].rearrange("p t (h d) -> p (t h) d", h=HEADS),
                                  bank(g, Q)[:, 0:S].rearrange("p (a d) -> p a d", d=DH),
                                  rsm[:, g, :, :].rearrange("p t h -> p (t h)").unsqueeze(2)
                                  .to_broadcast([P, TPU * HEADS, DH]), ALU.mult).then_inc(s["att"], 1)
            for g in range(2):
                dve.wait_ge(s["attTp"], 2 * n0 + g + 1)
                dve.tensor_copy(attT[:, g, :], bank(g, T)[:, 0:S]).then_inc(s["attT"], 1)
            for g in range(2):
                dve.wait_ge(s["wo"], 2 * n0 + g + 1)
                for t in range(TPU):
                    dve.tensor_tensor(X[:, TPU * i + HT * g + t, :], bank(g, Q)[:, S + t * C:S + (t + 1) * C],
                                      src(i, g, t), ALU.add)
                dve.drain()
                stats_step(dve, g, lambda t: X[:, TPU * i + HT * g + t, :], s["stats2"])
            for g in range(2):
                dve.wait_ge(s["rstd2"], 2 * n0 + g + 1)
                norm_step(dve, g, lambda t: X[:, TPU * i + HT * g + t, :], lambda t: z[:, g, t, :], s["z2"])
            before_hidden()
            for g in range(2):
                dve.wait_ge(s["zT2"], 2 * n0 + g + 1)
            ahead()
            for g in range(2):
                dve.wait_ge(s["y"], 2 * n0 + g + 1)
                for t in range(TPU):
                    n = TPU * i + HT * g + t
                    last = dve.tensor_tensor(X[:, n, :], bank(g, Q)[:, t * C:(t + 1) * C], X[:, n, :], ALU.add)
                last.then_inc(s["xout"], 1)
            after_y()

        lg = early([P, 2, TPU, E0])
        rep = early([P, 2, TPU, E0])
        ex = early([P, 2, TPU, E0])
        mx8 = early([P, 2, TPU, 8])
        nl = early([P, 2, TPU])
        sw = early([P, 2, TPU])
        rsw = early([P, 2, TPU])
        wr = early([P, 2, TPU, E0])
        kk = early([P, TPU, 2, E0])
        hs = early([F0, 2, S])

        def stage1():
            s = dict(layer_sems)
            s.update(norm_sems)
            s.update(sems("s1", ["logits", "lg", "lmax", "lexp", "wrow", "key",
                                    "keyTp", "keyT", "gu", "sg", "hs", "down", "ff"]))
            in_sem = [sem(f"s1_xin{g}") for g in range(2)]
            xn_out = [sem(f"s1_xn_out{g}") for g in range(2)]
            w_out = [sem(f"s1_w_out{g}") for g in range(2)]
            ff_out = [sem(f"s1_ff_out{g}") for g in range(2)]
            with nc.Block() as block:
                @block.sync
                def _(sp):
                    for g in range(2):
                        sp.dma_start(xin[:, g, :, :], x_t[:, HT * g:HT * g + TPU, :]).then_inc(in_sem[g], 16)

                    def turn(i, last):
                        for g in range(2):
                            u = 2 * i + g
                            sp.wait_ge(s["xn"], u + 1)
                            if not last:
                                sp.dma_start(xin[:, g, :, :], x_t[:, tiles(i + 1, g), :]).then_inc(in_sem[g], 16)
                            sp.dma_start(xw_t[:, tiles(i, g), 0:C], z0[:, g, :, :]).then_inc(xn_out[g], 16)
                        for g in range(2):
                            u = 2 * i + g
                            sp.wait_ge(s["wrow"], u + 1)
                            sp.dma_start(xw_t[:, tiles(i, g), C:XW], wr[:, g, :, :]).then_inc(w_out[g], 16)
                        for g in range(2):
                            u = 2 * i + g
                            sp.wait_ge(s["ff"], u + 1)
                            sp.dma_start(ffn0_t[:, tiles(i, g), :], ff[:, g, :, :]).then_inc(ff_out[g], 16)

                    with sp.Fori(0, HALF - 1) as i:
                        turn(i, False)
                    turn(HALF - 1, True)
                    sp.wait_ge(zeroed, 16)
                    for g in range(2):
                        sp.wait_ge(xn_out[g], 16 * HALF)
                        sp.wait_ge(w_out[g], 16 * HALF)
                        sp.wait_ge(ff_out[g], 16 * HALF)

                @block.gpsimd
                def _(pool):
                    def ahead(i):
                        for n in ("0", "1"):
                            for g in range(2):
                                rstd_step(pool, s, 2 * i + g, g, "stats" + n, "rstd" + n)

                    def turn(i, last):
                        for g in range(2):
                            rstd_step(pool, s, 2 * i + g, g, "stats2", "rstd2")
                        if not last:
                            ahead(i + 1)
                    ahead(0)
                    with pool.Fori(0, HALF - 1) as i:
                        turn(i, False)
                    turn(HALF - 1, True)

                @block.tensor
                def _(pe):
                    def turn_rows(i):
                        for g in range(2):
                            pe.wait_ge(s["xn"], 2 * i + g + 1)
                            transpose_unit(pe, g, T, 0, z0, s["xnTp"])

                    def ahead(i):
                        for g in range(2):
                            pe.wait_ge(s["xnT"], 2 * i + g + 1)
                            for t in range(TPU):
                                last = pe.matmul(bank(g, S0)[:, t * E0:(t + 1) * E0],
                                                 xnT[:, g, t * P:(t + 1) * P], WS[:, 0:E0], start=True, stop=True)
                            last.then_inc(s["logits"], 1)
                        front_tensor(pe, s, i, 0)

                    def turn(i, final):
                        def key_transposes():
                            pe.wait_ge(s["key"], 2 * i + 2)
                            for t in range(TPU):
                                last = pe.transpose(bank(1, T)[:, t * P:(t + 1) * P],
                                                    kk[:, t, :, :].rearrange("p g e -> p (g e)"), ident)
                            last.then_inc(s["keyTp"], 1)

                        def shared(g):
                            for n in range(2):
                                last = pe.matmul(bank(g, S0)[0:F0, n * S:(n + 1) * S],
                                                 WS[:, E0 + n * F0:E0 + (n + 1) * F0], xnT[:, g, :],
                                                 start=True, stop=True)
                            last.then_inc(s["gu"], 1)

                        def shared_down():
                            for g in range(2):
                                pe.wait_ge(s["hs"], 2 * i + g + 1)
                                for t in range(TPU):
                                    last = pe.matmul(bank(g, Q)[:, t * C:(t + 1) * C],
                                                     hs[:, g, t * P:(t + 1) * P], WSD[:, :], start=True, stop=True)
                                last.then_inc(s["down"], 1)

                        layer_tensor(pe, s, i, 0, after_scores=key_transposes, after_att=shared, after_wo=lambda: None,
                                     after_norm2=shared_down,
                                     after_hidden=lambda: None if final else turn_rows(i + 1),
                                     after_y=lambda: None if final else ahead(i + 1),
                                     logits_read=s["lg"], ff_read=s["ff"])
                    turn_rows(0)
                    ahead(0)
                    with pe.Fori(0, HALF - 1) as i:
                        turn(i, False)
                    turn(HALF - 1, True)

                @block.scalar
                def _(act):
                    def ahead(i):
                        for g in range(2):
                            act.wait_ge(s["xnTp"], 2 * i + g + 1)
                            act.activation(xnT[:, g, :], bank(g, T)[:, 0:S], ACT.Copy).then_inc(s["xnT"], 1)
                        front_scalar(act, s, i, 0)

                    def turn(i, final):
                        def router():
                            for g in range(2):
                                act.wait_ge(s["lmax"], 2 * i + g + 1)
                                for t in range(TPU):
                                    last = act.activation(ex[:, g, t, :], lg[:, g, t, :], ACT.Exp,
                                                          bias=nl[:, g, t:t + 1])
                                last.then_inc(s["lexp"], 1)
                            act.wait_ge(s["keyTp"], i + 1)
                            act.activation(keys[:, bass.ds(S * i, S)], bank(1, T)[:, 0:S], ACT.Copy)\
                               .then_inc(s["keyT"], 1)

                        def silu():
                            for g in range(2):
                                act.wait_ge(s["gu"], 2 * i + g + 1)
                                act.activation(hs[:, g, :], bank(g, S0)[0:F0, 0:S], ACT.Silu).then_inc(s["sg"], 1)

                        layer_scalar(act, s, i, 0, before_scores=router, before_norm2=silu)
                        if not final:
                            ahead(i + 1)
                    ahead(0)
                    with act.Fori(0, HALF - 1) as i:
                        turn(i, False)
                    turn(HALF - 1, True)

                @block.vector
                def _(dve):
                    def from_z0(i, g, t):
                        return z0[:, g, t, :]

                    def stats(i):
                        for g in range(2):
                            dve.wait_ge(in_sem[g], 16 * (i + 1))
                            stats_step(dve, g, lambda t: xin[:, g, t, :], s["stats0"])

                    def norms(i):
                        for g in range(2):
                            dve.wait_ge(s["rstd0"], 2 * i + g + 1)
                            norm_step(dve, g, lambda t: xin[:, g, t, :], lambda t: z0[:, g, t, :], s["xn"])
                        dve.drain()
                        front_vector(dve, s, i, 0, from_z0)

                    def router(i):
                        for g in range(2):
                            dve.wait_ge(s["logits"], 2 * i + g + 1)
                            dve.tensor_copy(lg[:, g, :, :].rearrange("p t e -> p (t e)"),
                                            bank(g, S0)[:, 0:TPU * E0]).then_inc(s["lg"], 1)
                            dve.drain()
                            for t in range(TPU):
                                dve.max(out=mx8[:, g, t, :], in_=lg[:, g, t, :])
                            dve.drain()
                            dve.tensor_scalar(nl[:, g, :], mx8[:, g, :, 0], -1.0, None, ALU.mult)\
                               .then_inc(s["lmax"], 1)
                            for t in range(TPU):
                                dve.match_replace(out=rep[:, g, t, :], in_to_replace=mx8[:, g, t, :],
                                                  in_values=lg[:, g, t, :], imm_value=NEG)
                            dve.drain()
                            for t in range(TPU):
                                last = dve.tensor_scalar(kk[:, t, g, :], rep[:, g, t, :], NEG / 2,
                                                         CST[:, bass.ds(C_TOKV + TPU * i + HT * g + t, 1)],
                                                         ALU.is_lt, ALU.mult)
                            last.then_inc(s["key"], 1)

                    def turn(i, final):
                        def weights():
                            for g in range(2):
                                dve.wait_ge(s["lexp"], 2 * i + g + 1)
                                for t in range(TPU):
                                    dve.scalar_tensor_tensor(ex[:, g, t, :], rep[:, g, t, :], NEG / 2, ex[:, g, t, :],
                                                             ALU.is_lt, ALU.mult, accum_out=sw[:, g, t:t + 1])
                            dve.drain()
                            dve.reciprocal(rsw[:, :, :], sw[:, :, :])
                            dve.drain()
                            for g in range(2):
                                dve.tensor_tensor(wr[:, g, :, :], ex[:, g, :, :],
                                                  rsw[:, g, :].unsqueeze(2).to_broadcast([P, TPU, E0]), ALU.mult)\
                                   .then_inc(s["wrow"], 1)

                        def shared():
                            for g in range(2):
                                dve.wait_ge(s["sg"], 2 * i + g + 1)
                                dve.tensor_tensor(hs[:, g, :], bank(g, S0)[0:F0, S:2 * S], hs[:, g, :], ALU.mult)\
                                   .then_inc(s["hs"], 1)

                        def ahead():
                            if not final:
                                stats(i + 1)
                            for g in range(2):
                                dve.wait_ge(s["down"], 2 * i + g + 1)
                                dve.tensor_copy(ff[:, g, :, :].rearrange("p t c -> p (t c)"), bank(g, Q)[:, 0:S])\
                                   .then_inc(s["ff"], 1)
                            if not final:
                                for g in range(2):
                                    dve.wait_ge(xn_out[g], 16 * (i + 1))
                                norms(i + 1)

                        layer_vector(dve, s, i, 0, from_z0, after_scores=weights, before_hidden=shared, ahead=ahead,
                                     after_y=lambda: None)
                        for g in range(2):
                            dve.wait_ge(w_out[g], 16 * (i + 1))
                            dve.wait_ge(ff_out[g], 16 * (i + 1))
                        if not final:
                            router(i + 1)
                    stats(0)
                    norms(0)
                    router(0)
                    with dve.Fori(0, HALF - 1) as i:
                        turn(i, False)
                    turn(HALF - 1, True)
        stage1()

        gidx = sb("gidx", [CAP, E0], I32)
        sidx = sb("sidx", [CAP, E0], I32)

        def pick():
            lst = early([P, CAP])
            both = early([E0, 2 * CAP])
            fin = early([E0, CAP])
            kf = early([CAP, E0])
            tk = early([CAP, E0])
            em = early([CAP, E0])
            halves, moved, firsts, turned = sem("p_halves"), sem("p_moved"), sem("p_firsts"), sem("p_turned")
            with nc.Block() as block:
                @block.sync
                def _(sp):
                    sp.wait_ge(halves, 1)
                    sp.dma_start(both[:, CAP:2 * CAP], lst[E0:P, :]).then_inc(moved, 16)
                    sp.wait_ge(moved, 16)

                @block.tensor
                def _(pe):
                    pe.wait_ge(firsts, 1)
                    pe.transpose(bank(0, T)[0:CAP, 0:E0], fin[:, :], ident[0:E0, 0:E0]).then_inc(turned, 1)

                @block.vector
                def _(dve):
                    def largest(dst, src):
                        for r in range(CAP // 8):
                            dve.max(out=dst[:, 8 * r:8 * r + 8], in_=src)
                            dve.drain()
                            if r < CAP // 8 - 1:
                                dve.match_replace(out=src, in_to_replace=dst[:, 8 * r:8 * r + 8], in_values=src,
                                                  imm_value=0.0)
                                dve.drain()
                    largest(lst, keys)
                    dve.tensor_copy(both[:, 0:CAP], lst[0:E0, :]).then_inc(halves, 1)
                    dve.drain()
                    dve.wait_ge(moved, 16)
                    largest(fin, both[:, :])
                    dve.tensor_copy(em[:, :], CST[0:CAP, C_ONE:C_ONE + E0]).then_inc(firsts, 1)
                    dve.wait_ge(turned, 1)
                    dve.tensor_copy(kf[:, :], bank(0, T)[0:CAP, 0:E0])
                    dve.drain()
                    dve.tensor_scalar(tk[:, :], kf[:, :], -1.0, float(TOK), ALU.mult, ALU.add)
                    dve.tensor_scalar(em[:, :], kf[:, :], 0.0, CST[0:CAP, C_P:C_P + 1], ALU.is_equal, ALU.mult)
                    dve.drain()
                    dve.tensor_scalar(gidx[:, :], tk[:, :], float(TOK - 1), None, ALU.min)
                    dve.tensor_tensor(sidx[:, :], tk[:, :], em[:, :], ALU.add)
        pick()

        wg = early([P, EPT, 2 * F0])
        wdn = early([F0, EPT, C])
        gi = sb("gi", [CAP, EPT], I32)
        si = sb("si", [CAP, EPT], I32)
        sj = sb("sj", [CAP, EPT], I32)
        gj = sb("gj", [CAP, 1], I32)
        zero_i = sb("zero_i", [CAP, 1], I32)
        xe = early([CAP, EPT, XW])
        xeT = early([P, EPT, CAP])
        he = early([CAP, EPT, F0])
        heT = early([F0, EPT, CAP])
        ye = early([CAP, EPT, C])
        EG = EPT // 2

        def stage2():
            s = dict(layer_sems)
            s.update(sems("s2", ["xeTp", "xeT", "eg", "es", "eh", "ehTp", "ehT", "ey", "ye"]))
            we_in = sem("s2_we_in")
            rows_in = [sem(f"s2_rows_in{j}") for j in range(EPT)]
            added = sem("s2_added")
            with nc.Block() as block:
                @block.sync
                def _(sp):
                    def load_experts(i):
                        sp.dma_start(wg[:, :, :], we0[bass.ds(EPT * i, EPT), :, :].rearrange("e p f -> p e f"))\
                          .then_inc(we_in, 16)
                        sp.dma_start(wdn[:, :, :], wd0[bass.ds(EPT * i, EPT), :, :].rearrange("e p f -> p e f"))\
                          .then_inc(we_in, 16)
                    load_experts(0)
                    with sp.Fori(0, HALF - 1) as i:
                        sp.wait_ge(s["ey"], 2 * i + 2)
                        load_experts(i + 1)
                    sp.wait_ge(we_in, 32 * HALF)

                @block.gpsimd
                def _(pool):
                    pool.memset(zero_i[:, :], 0)
                    pool.drain()

                    def scatters(i):
                        for j in range(EPT):
                            pool.tensor_copy(si[:, j:j + 1], sidx[:, bass.ds(EPT * i + j, 1)])
                        pool.drain()
                        for j in range(EPT):
                            if j % EG == 0:
                                pool.wait_ge(s["ye"], 2 * i + j // EG + 1)
                            pool.tensor_tensor(sj[:, j:j + 1], si[:, j:j + 1], zero_i[:, :], ALU.add)
                            pool.drain()
                            pool.indirect_dma_start(out=ffn0[:, :],
                                                    out_offset=bass.IndirectOffsetOnAxis(ap=sj[:, j:j + 1], axis=0),
                                                    in_=ye[:, j, :], in_offset=None, bounds_check=TOK + CAP - 1,
                                                    compute_op=ALU.add).then_inc(added, 16)
                            pool.wait_ge(added, 16 * (EPT * i + j + 1))

                    def ahead(i):
                        for g in range(2):
                            rstd_step(pool, s, B + 2 * i + g, g, "stats1", "rstd1")

                    def turn(i, first, final):
                        if not first:
                            pool.wait_ge(s["ye"], 2 * i)
                        pool.tensor_tensor(gj[:, :], zero_i[:, :], zero_i[:, :], ALU.add)
                        pool.tensor_copy(gi[:, :], gidx[:, bass.ds(EPT * i, EPT)])
                        pool.drain()
                        for j in range(EPT):
                            pool.indirect_dma_start(out=xe[:, j, :], out_offset=None, in_=xw[:, :],
                                                    in_offset=bass.IndirectOffsetOnAxis(ap=gi[:, j:j + 1], axis=0),
                                                    bounds_check=TOK - 1).then_inc(rows_in[j], 16)
                        if not first:
                            scatters(i - 1)
                        for g in range(2):
                            rstd_step(pool, s, B + 2 * i + g, g, "stats2", "rstd2")
                        if not final:
                            ahead(i + 1)

                    ahead(0)
                    turn(0, True, False)
                    with pool.Fori(1, HALF - 1) as i:
                        turn(i, False, False)
                    turn(HALF - 1, False, True)
                    scatters(HALF - 1)

                @block.tensor
                def _(pe):
                    def turn(i, final):
                        def experts(part, units=(0, 1)):
                            for g in units:
                                u = 2 * i + g
                                for j in range(EG):
                                    n = EG * g + j
                                    if part == 0:
                                        pe.wait_ge(rows_in[n], 16 * (i + 1))
                                        last = pe.matmul(bank(g, S0)[:, j * CAP:(j + 1) * CAP], xe[:, n, 0:C],
                                                         ident[0:CAP, 0:CAP], start=True, stop=True)
                                    if part == 1:
                                        if j == 0:
                                            pe.wait_ge(s["xeT"], u + 1)
                                            pe.wait_ge(we_in, 32 * (i + 1))
                                        last = pe.matmul(bank(g, S1)[0:CAP, j * S:j * S + 2 * F0], xeT[:, n, :],
                                                         wg[:, n, :], start=True, stop=True)
                                    if part == 2:
                                        last = pe.matmul(bank(g, T)[0:F0, j * CAP:(j + 1) * CAP], he[:, n, :],
                                                         ident[0:CAP, 0:CAP], start=True, stop=True)
                                    if part == 3:
                                        last = pe.matmul(bank(g, T)[0:CAP, S + j * C:S + (j + 1) * C], heT[:, n, :],
                                                         wdn[:, n, :], start=True, stop=True)
                                last.then_inc(s[("xeTp", "eg", "ehTp", "ey")[part]], 1)

                        def after_y():
                            for g in range(2):
                                pe.wait_ge(s["ehT"], 2 * i + g + 1)
                            if not final:
                                front_tensor(pe, s, i + 1, 1)
                                for g in range(2):
                                    pe.wait_ge(s["xl1"], B + 2 * i + 2 + g + 1)
                            experts(3)
                        layer_tensor(pe, s, i, 1, after_att=lambda g: experts(0, (g,)), after_wo=lambda: experts(1),
                                     after_norm2=lambda: None, after_hidden=lambda: experts(2), after_y=after_y,
                                     hidden_free=s["eh"])
                        for g in range(2):
                            pe.wait_ge(s["ye"], 2 * i + g + 1)
                    front_tensor(pe, s, 0, 1)
                    with pe.Fori(0, HALF - 1) as i:
                        turn(i, False)
                    turn(HALF - 1, True)

                @block.scalar
                def _(act):
                    def turn(i, final):
                        def rows():
                            for g in range(2):
                                act.wait_ge(s["xeTp"], 2 * i + g + 1)
                                act.activation(xeT[:, EG * g:EG * (g + 1), :].rearrange("p j c -> p (j c)"),
                                               bank(g, S0)[:, 0:EG * CAP], ACT.Copy).then_inc(s["xeT"], 1)

                        def silu():
                            for g in range(2):
                                act.wait_ge(s["eg"], 2 * i + g + 1)
                                act.activation(he[:, EG * g:EG * (g + 1), :],
                                               bank(g, S1)[0:CAP, :].rearrange("p (j f) -> p j f", j=EG)[:, :, 0:F0],
                                               ACT.Silu).then_inc(s["es"], 1)
                        layer_scalar(act, s, i, 1, before_norm2=lambda: (rows(), silu()))
                        if not final:
                            front_scalar(act, s, i + 1, 1)
                    front_scalar(act, s, 0, 1)
                    with act.Fori(0, HALF - 1) as i:
                        turn(i, False)
                    turn(HALF - 1, True)

                @block.vector
                def _(dve):
                    def from_x(i, g, t):
                        return X[:, TPU * i + HT * g + t, :]

                    def turn(i, final):
                        def hidden():
                            for g in range(2):
                                e = slice(EG * g, EG * (g + 1))
                                dve.wait_ge(s["es"], 2 * i + g + 1)
                                dve.tensor_tensor(he[:, e, :],
                                                  bank(g, S1)[0:CAP, :].rearrange("p (j f) -> p j f", j=EG)
                                                  [:, :, F0:2 * F0], he[:, e, :], ALU.mult).then_inc(s["eh"], 1)
                            for g in range(2):
                                dve.wait_ge(s["ehTp"], 2 * i + g + 1)
                                dve.tensor_copy(heT[:, EG * g:EG * (g + 1), :].rearrange("p j c -> p (j c)"),
                                                bank(g, T)[0:F0, 0:EG * CAP]).then_inc(s["ehT"], 1)

                        def weighted():
                            for g in range(2):
                                dve.wait_ge(s["ey"], 2 * i + g + 1)
                                for j in range(EG):
                                    n = EG * g + j
                                    last = dve.tensor_scalar(ye[:, n, :], bank(g, T)[0:CAP, S + j * C:S + (j + 1) * C],
                                                             xe[:, n, bass.ds(EPT * i + C + n, 1)], None, ALU.mult)
                                last.then_inc(s["ye"], 1)

                        layer_vector(dve, s, i, 1, from_x, before_hidden=hidden, after_y=weighted,
                                     ahead=lambda: None if final else front_vector(dve, s, i + 1, 1, from_x))
                    front_vector(dve, s, 0, 1, from_x)
                    with dve.Fori(0, HALF - 1) as i:
                        turn(i, False)
                    turn(HALF - 1, True)
        stage2()

        EID = sb("EID", [P, NT])
        RNK = sb("RNK", [P, NT])
        SLOT = sb("SLOT", [P, NT], I32)
        TE = sb("TE", [1, SORTED_TILES], I32)
        cum = sb("cum", [P, 2, E1], BF16)

        def stage3():
            s = dict(norm_sems)
            s.update(sems("s3", ["gsil", "x1", "proj", "biased", "silu", "sq", "n2",
                            "nrm", "kn", "lg", "top", "tanh", "xs", "oh", "cum", "rank", "rankrd", "gu", "sgate",
                            "hmul", "down", "sh", "states", "state", "qTp", "qT", "lin", "stats2", "rstd2", "z2",
                            "zTp", "zT", "wo", "s1"]))
            in_bufs = (late([P, 2, TPU, 6]), late([P, 2, TPU, 2]), late([P, 2, TPU]), late([P, 2, TPU]))
            xin3 = late([P, 2, TPU, C])
            gin = late([P, 2, TPU, C])
            x1b = late([P, 2, TPU, C])
            pj = [pr[:, g, :, :, :].rearrange("p a b c -> p (a b c)") for g in range(2)]
            qkp = [ctx.enter_context(nc.sbuf_tensor(f"qkp{g}", [P, TPU, 3 * C], F32)) for g in range(2)]
            sqb = [pj[g][:, 0:TPU * 3 * C].rearrange("p (t c) -> p t c", t=TPU) for g in range(2)]
            vv = [pT[:, g, :, :, :].rearrange("p a b c -> p (a b c)")[:, 0:TPU * 2 * C]
                  .rearrange("p (t c) -> p t c", t=TPU) for g in range(2)]
            hid = [pT[:, g, :, :, :].rearrange("p a b c -> p (a b c)")[:, 512:1024] for g in range(2)]
            xn = z
            xnT3 = attT
            qT = qk[:, :, 0, :]
            stt_ = [qk[:, g, 1, 0:C] for g in range(2)]
            st0 = [qk[:, g, 1, C:2 * C] for g in range(2)]
            z2 = v
            xsb = att
            shb = late([P, 2, TPU, C])
            n2 = late([P, 2, NG])
            rn = late([P, 2, NG])
            lg1 = late([P, 2, TPU, E1])
            m8 = late([P, 2, TPU, 8])
            i8 = sb("i8", [P, 2, TPU, 8], U32)
            ei = late([P, 2, TPU])
            th = late([P, 2, TPU])
            sc = late([P, 2, TPU])
            rk = late([P, 2, TPU])
            oh = sb("oh", [P, 2, TPU, E1], BF16)
            ct = sb("ct", [P, 2, E1], BF16)
            junk = late([P, 2, TPU, E1])
            RANKS = S + TPU * E1
            W_WO, W_GATE, W_SG, W_SU, W_SD = 640, 768, 800, 1056, 1312
            in_x = [sem(f"s3_in_x{g}") for g in range(2)]
            in_g = [sem(f"s3_in_g{g}") for g in range(2)]
            o_x1 = [sem(f"s3_o_x1{g}") for g in range(2)]
            o_xs = [sem(f"s3_o_xs{g}") for g in range(2)]
            o_sh = [sem(f"s3_o_sh{g}") for g in range(2)]
            we1_in = sem("s3_we1")
            ls, lb = (COL[:, DEPTH * NCOL + n:DEPTH * NCOL + n + 1] for n in range(2))

            with nc.Block() as block:
                @block.sync
                def _(sp):
                    def load(i, g):
                        sp.dma_start(xin3[:, g, :, :], x_t[:, tiles(i, g), :]).then_inc(in_x[g], 16)
                        sp.dma_start(gin[:, g, :, :], ffn0_t[:, tiles(i, g), :]).then_inc(in_g[g], 16)

                    def turn(i, last):
                        for g in range(2):
                            sp.wait_ge(s["x1"], 2 * i + g + 1)
                            if not last:
                                load(i + 1, g)
                            sp.dma_start(x1_t[:, tiles(i, g), :], x1b[:, g, :, :]).then_inc(o_x1[g], 16)
                        for g in range(2):
                            sp.wait_ge(s["xs"], 2 * i + g + 1)
                            sp.dma_start(xs_t[:, tiles(i, g), :], xsb[:, g, :, :]).then_inc(o_xs[g], 16)
                        for g in range(2):
                            sp.wait_ge(s["sh"], 2 * i + g + 1)
                            sp.dma_start(sh_t[:, tiles(i, g), :], shb[:, g, :, :]).then_inc(o_sh[g], 16)

                    for g in range(2):
                        load(0, g)
                    sp.dma_start(big[:, :], we1, max_dma_last_dim=32768).then_inc(we1_in, 16)
                    with sp.Fori(0, HALF - 1) as i:
                        turn(i, False)
                    turn(HALF - 1, True)
                    sp.wait_ge(we1_in, 16)
                    for g in range(2):
                        sp.wait_ge(o_x1[g], 16 * HALF)
                        sp.wait_ge(o_xs[g], 16 * HALF)
                        sp.wait_ge(o_sh[g], 16 * HALF)

                @block.gpsimd
                def _(pool):
                    pool.memset(cum[:, :, :], 0.0)
                    pool.drain()
                    pool.tensor_tensor(ct[:, 0, :], cum[:, 0, :], cum[:, 1, :], ALU.add).then_inc(s["cum"], 1)

                    def ahead(i):
                        for g in range(2):
                            pool.wait_ge(s["gsil"], 2 * i + g + 1)
                            pool.tensor_tensor(gin[:, g, :, :], gin[:, g, :, :], X[:, tiles(i, g), :], ALU.mult)
                            pool.drain()
                            pool.tensor_tensor(x1b[:, g, :, :], gin[:, g, :, :], xin3[:, g, :, :], ALU.add)\
                                .then_inc(s["x1"], 1)
                        for g in range(2):
                            rstd_step(pool, s, B + 2 * i + g, g, "stats0", "rstd0", in_bufs)

                    def turn(i, final):
                        for g in range(2):
                            u = 2 * i + g
                            pool.wait_ge(s["oh"], u + 1)
                            pool.tensor_tensor(ct[:, g, :], oh[:, g, 0, :], oh[:, g, 1, :], ALU.add)
                            pool.drain()
                            if g == 1:
                                pool.wait_ge(s["rank"], 2 * i + 1)
                            pool.tensor_tensor(cum[:, 1 - g, :], cum[:, g, :], ct[:, g, :], ALU.add)\
                                .then_inc(s["cum"], 1)
                        if not final:
                            ahead(i + 1)
                        for g in range(2):
                            rstd_step(pool, s, 2 * i + g, g, "stats2", "rstd2")
                    ahead(0)
                    with pool.Fori(0, HALF - 1) as i:
                        turn(i, False)
                    turn(HALF - 1, True)

                @block.tensor
                def _(pe):
                    def ahead(i):
                        for g in range(2):
                            pe.wait_ge(s["xn"], B + 2 * i + g + 1)
                            transpose_unit(pe, g, T, 0, xn, s["xnTp"])

                    def turn(i, final):
                        for g in range(2):
                            for t in range(TPU):
                                xt = xnT3[:, g, t * P:(t + 1) * P]
                                pe.matmul(bank(g, (S0, Q)[t]), xt, W1[:, 0:4 * C], start=True, stop=True)
                                pe.matmul(bank(g, S1)[:, t * C:(t + 1) * C], xt, W1[:, 4 * C:5 * C],
                                          start=True, stop=True)
                                last = pe.matmul(bank(g, T)[:, S + t * E1:S + (t + 1) * E1], xt,
                                                 W1[:, W_GATE:W_GATE + E1], start=True, stop=True)
                            last.then_inc(s["proj"], 1)
                        for g in range(2):
                            u = 2 * i + g
                            pe.wait_ge(s["lg"], u + 1)
                            for n in range(2 * TPU):
                                w = W1[:, W_SG + n * P:W_SG + (n + 1) * P]
                                last = pe.matmul(bank(g, S0 + n // 2)[:, n % 2 * S:(n % 2 + 1) * S], w,
                                                 xnT3[:, g, :], start=True, stop=True)
                            last.then_inc(s["gu"], 1)
                            pe.wait_ge(s["oh"], u + 1)
                            pe.wait_ge(s["cum"], u + 1)
                            for t in range(TPU):
                                r = bank(g, T)[:, RANKS + t * E1:RANKS + (t + 1) * E1]
                                pe.matmul(r, TRI[:, :], oh[:, g, t, :], start=True, stop=False)
                                if t:
                                    pe.matmul(r, ONES[:, :], oh[:, g, 0, :], start=False, stop=False)
                                last = pe.matmul(r, ONES[:, :], cum[:, g, :], start=False, stop=True)
                            last.then_inc(s["rank"], 1)
                        for g in range(2):
                            pe.wait_ge(s["kn"], 2 * i + g + 1)
                            for k in range(2):
                                for t in range(TPU):
                                    last = pe.matmul(bank(g, Q)[:, k * C:(k + 1) * C],
                                                     qkp[g][:, t, (k + 1) * C:(k + 2) * C],
                                                     vv[g][:, t, k * C:(k + 1) * C],
                                                     start=(t == 0), stop=(t == TPU - 1))
                            last.then_inc(s["states"], 1)
                            for t in range(TPU):
                                last = pe.transpose(bank(g, T)[:, t * P:(t + 1) * P], qkp[g][:, t, 0:C], ident)
                            last.then_inc(s["qTp"], 1)
                        for g in range(2):
                            pe.wait_ge(s["hmul"], 2 * i + g + 1)
                            for t in range(TPU):
                                for n in range(2):
                                    last = pe.matmul(bank(g, S0)[:, t * C:(t + 1) * C],
                                                     hid[g][:, n * S + t * P:n * S + (t + 1) * P],
                                                     W1[:, W_SD + n * C:W_SD + (n + 1) * C],
                                                     start=(n == 0), stop=(n == 1))
                            last.then_inc(s["down"], 1)
                        for g in range(2):
                            pe.wait_ge(s["qT"], 2 * i + g + 1)
                            pe.wait_ge(s["state"], 2 * i + g + 1)
                            for t in range(TPU):
                                last = pe.matmul(bank(g, Q)[:, S + t * C:S + (t + 1) * C], qT[:, g, t * P:(t + 1) * P],
                                                 stt_[g], start=True, stop=True)
                            last.then_inc(s["lin"], 1)
                        if not final:
                            ahead(i + 1)
                            for g in range(2):
                                pe.wait_ge(s["xnT"], B + 2 * (i + 1) + g + 1)
                        for g in range(2):
                            pe.wait_ge(s["z2"], 2 * i + g + 1)
                            transpose_unit(pe, g, T, 0, z2, s["zTp"])
                        for g in range(2):
                            pe.wait_ge(s["zT"], 2 * i + g + 1)
                            for t in range(TPU):
                                last = pe.matmul(bank(g, Q)[:, t * C:(t + 1) * C], zT[:, g, t * P:(t + 1) * P],
                                                 W1[:, W_WO:W_WO + C], start=True, stop=True)
                            last.then_inc(s["wo"], 1)
                        for g in range(2):
                            pe.wait_ge(s["s1"], 2 * i + g + 1)
                    ahead(0)
                    for g in range(2):
                        pe.wait_ge(s["xnT"], B + g + 1)
                    with pe.Fori(0, HALF - 1) as i:
                        turn(i, False)
                    turn(HALF - 1, True)

                @block.scalar
                def _(act):
                    def gate(i):
                        for g in range(2):
                            act.wait_ge(in_g[g], 16 * (i + 1))
                            act.wait_ge(in_x[g], 16 * (i + 1))
                            act.activation(gin[:, g, :, :], gin[:, g, :, :], ACT.Silu).then_inc(s["gsil"], 1)

                    def rows(i):
                        for g in range(2):
                            act.wait_ge(s["xnTp"], B + 2 * i + g + 1)
                            act.activation(xnT3[:, g, :], bank(g, T)[:, 0:S], ACT.Copy).then_inc(s["xnT"], 1)

                    def turn(i, final):
                        for g in range(2):
                            act.wait_ge(s["biased"], 2 * i + g + 1)
                            act.activation(qkp[g][:, :, :], qkp[g][:, :, :], ACT.Silu).then_inc(s["silu"], 1)
                            act.drain()
                            act.activation(sqb[g], qkp[g][:, :, :], ACT.Square, bias=PHALF[:, 0:1]).then_inc(s["sq"], 1)
                        for g in range(2):
                            act.wait_ge(s["top"], 2 * i + g + 1)
                            act.activation(th[:, g, :], m8[:, g, :, 0], ACT.Tanh, scale=0.5).then_inc(s["tanh"], 1)
                        act.wait_ge(s["n2"], 2 * i + 2)
                        act.activation(n2[:, :, :], n2[:, :, :], ACT.Sqrt).then_inc(s["nrm"], 1)
                        for g in range(2):
                            act.wait_ge(s["gu"], 2 * i + g + 1)
                            act.activation(hid[g], bank(g, S0), ACT.Silu).then_inc(s["sgate"], 1)
                        if not final:
                            for g in range(2):
                                act.wait_ge(o_x1[g], 16 * (i + 1))
                            gate(i + 1)
                        for g in range(2):
                            act.wait_ge(s["qTp"], 2 * i + g + 1)
                            act.activation(qT[:, g, :], bank(g, T)[:, 0:S], ACT.Copy).then_inc(s["qT"], 1)
                        for g in range(2):
                            act.wait_ge(s["down"], 2 * i + g + 1)
                            act.activation(shb[:, g, :, :].rearrange("p t c -> p (t c)"), bank(g, S0)[:, 0:S], ACT.Copy)\
                               .then_inc(s["sh"], 1)
                        if not final:
                            rows(i + 1)
                        for g in range(2):
                            act.wait_ge(s["zTp"], 2 * i + g + 1)
                            affine_step(act, g, ls, lb, s["zT"])
                        for g in range(2):
                            act.wait_ge(o_xs[g], 16 * (i + 1))
                            act.wait_ge(o_sh[g], 16 * (i + 1))
                    gate(0)
                    rows(0)
                    with act.Fori(0, HALF - 1) as i:
                        turn(i, False)
                    turn(HALF - 1, True)

                @block.vector
                def _(dve):
                    def stats(i):
                        for g in range(2):
                            dve.wait_ge(s["x1"], 2 * i + g + 1)
                            stats_step(dve, g, lambda t: x1b[:, g, t, :], s["stats0"], in_bufs)

                    def norms(i):
                        for g in range(2):
                            dve.wait_ge(s["rstd0"], B + 2 * i + g + 1)
                            norm_step(dve, g, lambda t: x1b[:, g, t, :], lambda t: xn[:, g, t, :], s["xn"], in_bufs)

                    def turn(i, final):
                        for g in range(2):
                            dve.wait_ge(s["proj"], 2 * i + g + 1)
                            bias = ROW[:, DEPTH * C:DEPTH * C + NP]
                            for t in range(TPU):
                                b = bank(g, (S0, Q)[t])
                                last = dve.tensor_tensor(qkp[g][:, t, :], b[:, 0:3 * C], bias[:, 0:3 * C], ALU.add)
                            last.then_inc(s["biased"], 1)
                            for t in range(TPU):
                                b = bank(g, (S0, Q)[t])
                                dve.tensor_tensor(vv[g][:, t, 0:C], b[:, 3 * C:4 * C], bias[:, 3 * C:4 * C], ALU.add)
                            dve.tensor_tensor(vv[g][:, :, C:2 * C],
                                              bank(g, S1)[:, 0:S].rearrange("p (t c) -> p t c", t=TPU),
                                              bias[:, 4 * C:5 * C].unsqueeze(1).to_broadcast([P, TPU, C]), ALU.add)
                            dve.tensor_copy(lg1[:, g, :, :].rearrange("p t e -> p (t e)"),
                                            bank(g, T)[:, S:S + TPU * E1]).then_inc(s["lg"], 1)
                            dve.drain()
                            for t in range(TPU):
                                last = dve.max(out=m8[:, g, t, :], in_=lg1[:, g, t, :])
                            last.then_inc(s["top"], 1)
                            dve.drain()
                            for t in range(TPU):
                                dve.max_index(out=i8[:, g, t, :], in_max=m8[:, g, t, :], in_values=lg1[:, g, t, :])
                            dve.drain()
                            dve.tensor_copy(ei[:, g, :], i8[:, g, :, 0])
                            dve.drain()
                            for t in range(TPU):
                                last = dve.tensor_scalar(oh[:, g, t, :], CST[:, C_IOTA:C_IOTA + E1], ei[:, g, t:t + 1],
                                                         None, ALU.is_equal)
                            last.then_inc(s["oh"], 1)
                            dve.tensor_copy(EID[:, tiles(i, g)], ei[:, g, :])
                        for g in range(2):
                            dve.wait_ge(s["sq"], 2 * i + g + 1)
                            dve.tensor_reduce(n2[:, g, :], sqb[g].rearrange("p t (h d) -> p (t h) d", d=LD), X_AXIS,
                                              ALU.add).then_inc(s["n2"], 1)
                        for g in range(2):
                            dve.wait_ge(s["rank"], 2 * i + g + 1)
                            for t in range(TPU):
                                last = dve.scalar_tensor_tensor(junk[:, g, t, :], bank(g, T)[:, RANKS + t * E1:RANKS + (t + 1) * E1],
                                                                1.0, oh[:, g, t, :], ALU.mult, ALU.mult,
                                                                accum_out=rk[:, g, t:t + 1])
                            last.then_inc(s["rankrd"], 1)
                        dve.drain()
                        for g in range(2):
                            dve.tensor_copy(RNK[:, tiles(i, g)], rk[:, g, :])
                        for g in range(2):
                            dve.wait_ge(s["tanh"], 2 * i + g + 1)
                            dve.tensor_scalar(sc[:, g, :], th[:, g, :], 0.5, 0.5, ALU.mult, ALU.add)
                        dve.drain()
                        for g in range(2):
                            for t in range(TPU):
                                last = dve.tensor_scalar(xsb[:, g, t, :], xn[:, g, t, :], sc[:, g, t:t + 1], None,
                                                         ALU.mult)
                            last.then_inc(s["xs"], 1)
                        dve.wait_ge(s["nrm"], i + 1)
                        dve.tensor_scalar(n2[:, :, :], n2[:, :, :], 1e-6, None, ALU.add)
                        dve.drain()
                        dve.reciprocal(rn[:, :, :], n2[:, :, :])
                        dve.drain()
                        for g in range(2):
                            f = qkp[g][:, :, :].rearrange("p t (h d) -> p (t h) d", d=LD)
                            dve.scalar_tensor_tensor(f, f, 0.5, rn[:, g, :].unsqueeze(2).to_broadcast([P, NG, LD]),
                                                     ALU.add, ALU.mult).then_inc(s["kn"], 1)
                        for g in range(2):
                            dve.wait_ge(s["sgate"], 2 * i + g + 1)
                            dve.tensor_tensor(hid[g], bank(g, S1), hid[g], ALU.mult).then_inc(s["hmul"], 1)
                        for g in range(2):
                            dve.wait_ge(s["states"], 2 * i + g + 1)
                            dve.tensor_tensor(st0[g], bank(g, Q)[:, 0:C], CST[:, C_BLK:C_BLK + C], ALU.mult)
                            dve.drain()
                            dve.tensor_tensor(stt_[g], bank(g, Q)[:, C:2 * C], st0[g], ALU.mult).then_inc(s["state"], 1)
                        if not final:
                            stats(i + 1)
                        for g in range(2):
                            dve.wait_ge(s["lin"], 2 * i + g + 1)
                            stats_step(dve, g, lambda t: bank(g, Q)[:, S + t * C:S + (t + 1) * C], s["stats2"])
                        if not final:
                            norms(i + 1)
                        for g in range(2):
                            dve.wait_ge(s["rstd2"], 2 * i + g + 1)
                            norm_step(dve, g, lambda t: bank(g, Q)[:, S + t * C:S + (t + 1) * C],
                                      lambda t: z2[:, g, t, :], s["z2"])
                        for g in range(2):
                            dve.wait_ge(s["wo"], 2 * i + g + 1)
                            for t in range(TPU):
                                last = dve.tensor_tensor(X[:, TPU * i + HT * g + t, :], bank(g, Q)[:, t * C:(t + 1) * C],
                                                         ROW[:, DEPTH * C + NP:DEPTH * C + NP + C], ALU.add)
                            last.then_inc(s["s1"], 1)
                    stats(0)
                    norms(0)
                    with dve.Fori(0, HALF - 1) as i:
                        turn(i, False)
                    turn(HALF - 1, True)
        stage3()

        def place():
            placed = [sem(f"pl_placed{b}") for b in range(2)]
            loaded = [sem(f"pl_loaded{b}") for b in range(2)]
            counted, slots = sem("pl_counted"), sem("pl_slots")
            cnt = late([P, E1])
            ci = sb("ci", [P, E1], I32)
            nt = late([P, E1])
            end = late([P, E1])
            off = late([P, E1])
            eq = pr[:, :, :, :, :].rearrange("p g a b c -> p (g a b c)")[:, 0:NT * E1].rearrange("p (t e) -> p t e", e=E1)
            sl = late([P, NT])
            xb = sb("xb", [P, 2, C])
            ix = sb("ix", [P, 2], I32)
            iy = sb("iy", [P, 2], I32)
            zi = sb("zi", [P, 1], I32)
            with nc.Block() as block:
                @block.tensor
                def _(pe):
                    pe.matmul(bank(0, T)[:, 0:E1], ONES[:, :], cum[:, 0, :], start=True, stop=True).then_inc(counted, 1)

                @block.vector
                def _(dve):
                    dve.wait_ge(counted, 1)
                    dve.tensor_scalar(ci[:, :], bank(0, T)[:, 0:E1], float(P - 1), None, ALU.add)
                    dve.drain()
                    dve.tensor_scalar(ci[:, :], ci[:, :], P.bit_length() - 1, None, ALU.logical_shift_right)
                    dve.drain()
                    dve.tensor_copy(nt[:, :], ci[:, :])
                    dve.drain()
                    dve.tensor_tensor_scan(end[:, :], nt[:, :], CST[:, C_ONE:C_ONE + E1], 0.0, ALU.add, ALU.mult)
                    dve.drain()
                    dve.tensor_tensor(off[:, :], end[:, :], nt[:, :], ALU.subtract)
                    dve.drain()
                    dve.tensor_scalar(off[:, :], off[:, :], float(P), None, ALU.mult)
                    dve.tensor_tensor(eq, EID[:, :].unsqueeze(2).to_broadcast([P, NT, E1]),
                                      CST[:, C_IOTA:C_IOTA + E1].unsqueeze(1).to_broadcast([P, NT, E1]), ALU.is_equal)
                    dve.drain()
                    dve.tensor_tensor(eq, eq, off[:, :].unsqueeze(1).to_broadcast([P, NT, E1]), ALU.mult)
                    dve.drain()
                    dve.tensor_reduce(sl[:, :], eq, X_AXIS, ALU.add)
                    dve.drain()
                    dve.tensor_tensor(SLOT[:, :], sl[:, :], RNK[:, :], ALU.add).then_inc(slots, 1)
                    te = pT[0:1, :, :, :, :].rearrange("p g a b c -> p (g a b c)")
                    for h in range(3):
                        n = SORTED_TILES // 3
                        part = te[:, 0:n * E1].rearrange("p (t e) -> p t e", e=E1)
                        t0 = C_TILE + h * n
                        dve.tensor_tensor(part, end[0:1, :].unsqueeze(1).to_broadcast([1, n, E1]),
                                          CST[0:1, t0:t0 + n].unsqueeze(2).to_broadcast([1, n, E1]), ALU.is_le)
                        dve.drain()
                        dve.tensor_reduce(tef[:, h * n:(h + 1) * n], part, X_AXIS, ALU.add)
                        dve.drain()
                    dve.tensor_scalar(TE[:, :], tef[:, :], float(E1 - 1), None, ALU.min)

                @block.sync
                def _(sp):
                    for b in range(2):
                        sp.dma_start(xb[:, b, :], xs_t[:, b, :]).then_inc(loaded[b], 16)
                    with sp.Fori(0, NT // 2 - 1) as j:
                        for b in range(2):
                            sp.wait_ge(placed[b], 16 * (j + 1))
                            sp.dma_start(xb[:, b, :], xs_t[:, 2 * j + 2 + b, :]).then_inc(loaded[b], 16)
                    for b in range(2):
                        sp.wait_ge(placed[b], 16 * (NT // 2))

                @block.gpsimd
                def _(pool):
                    pool.memset(zi[:, :], 0)
                    pool.drain()
                    pool.wait_ge(slots, 1)
                    with pool.Fori(0, NT // 2) as j:
                        pool.tensor_copy(ix[:, :], SLOT[:, bass.ds(2 * j, 2)])
                        pool.drain()
                        for b in range(2):
                            pool.wait_ge(loaded[b], 16 * (j + 1))
                            pool.tensor_tensor(iy[:, b:b + 1], ix[:, b:b + 1], zi[:, :], ALU.add)
                            pool.drain()
                            pool.indirect_dma_start(out=srt[:, :],
                                                    out_offset=bass.IndirectOffsetOnAxis(ap=iy[:, b:b + 1], axis=0),
                                                    in_=xb[:, b, :], in_offset=None,
                                                    bounds_check=SORTED_TILES * P - 1).then_inc(placed[b], 16)
                        for b in range(2):
                            pool.wait_ge(placed[b], 16 * (j + 1))

        tef = late([1, SORTED_TILES])
        place()

        row_in = [sem(f"row_in{k}") for k in range(IN_FLIGHT)]

        def stage4():
            n_t = IN_FLIGHT
            s = sems("s4", ["xTp", "xT", "gu", "silu", "h", "hTp", "hT", "yp", "y"])
            row_out = [sem(f"s4_out{k}") for k in range(n_t)]

            def four(buf, shape):
                flat = buf[:, :, :, :].rearrange("p g a b -> p (g a b)")
                return [flat[:, k * shape:(k + 1) * shape] for k in range(n_t)]
            xt = four(v, C)
            xT = [zT[:, k // 2, k % 2 * P:(k % 2 + 1) * P] for k in range(n_t)]
            yb = four(att, C)
            hb = [pr[:, k // 2, k % 2, :, :].rearrange("p a b -> p (a b)")[:, 0:F1] for k in range(n_t)]
            hT = [pT[:, k // 2, k % 2, :, :].rearrange("p a b -> p (a b)")[:, 0:F1] for k in range(n_t)]

            def gu(k):
                return ps[:, 2 * k, :]

            def misc(k):
                return ps[:, 2 * k + 1, :]
            turns = SORTED_TILES // n_t
            with nc.Block() as block:
                @block.sync
                def _(sp):
                    for k in range(n_t):
                        sp.dma_start(xt[k], srt_t[:, k, :]).then_inc(row_in[k], 16)

                    def turn(i, last):
                        for k in range(n_t):
                            if not last:
                                sp.wait_ge(s["xTp"], n_t * i + k + 1)
                                sp.dma_start(xt[k], srt_t[:, n_t * i + n_t + k, :]).then_inc(row_in[k], 16)
                        for k in range(n_t):
                            sp.wait_ge(s["y"], n_t * i + k + 1)
                            sp.dma_start(ys_t[:, n_t * i + k, :], yb[k]).then_inc(row_out[k], 16)
                    with sp.Fori(0, turns - 1) as i:
                        turn(i, False)
                    turn(turns - 1, True)
                    for k in range(n_t):
                        sp.wait_ge(row_out[k], 16 * turns)

                @block.tensor
                def _(pe):
                    with pe.Fori(0, turns) as i:
                        for k in range(n_t):
                            pe.wait_ge(row_in[k], 16 * (i + 1))
                            pe.transpose(misc(k)[:, 0:P], xt[k], ident).then_inc(s["xTp"], 1)
                        e = [pe.value_load(TE[0:1, bass.ds(n_t * i + k, 1)], min_val=0, max_val=E1 - 1)
                             for k in range(n_t)]
                        for k in range(n_t):
                            pe.wait_ge(s["xT"], n_t * i + k + 1)
                            pe.matmul(gu(k), xT[k], WE1[:, e[k], 0:2 * F1], start=True, stop=True).then_inc(s["gu"], 1)
                        for k in range(n_t):
                            pe.wait_ge(s["h"], n_t * i + k + 1)
                            for f in range(2):
                                last = pe.transpose(misc(k)[:, (f + 1) * P:(f + 2) * P], hb[k][:, f * P:(f + 1) * P],
                                                    ident)
                            last.then_inc(s["hTp"], 1)
                        for k in range(n_t):
                            pe.wait_ge(s["hT"], n_t * i + k + 1)
                            for f in range(2):
                                last = pe.matmul(gu(k)[:, 0:C], hT[k][:, f * P:(f + 1) * P],
                                                 WE1[:, e[k], 2 * F1 + f * C:2 * F1 + (f + 1) * C],
                                                 start=(f == 0), stop=(f == 1))
                            last.then_inc(s["yp"], 1)

                @block.scalar
                def _(act):
                    with act.Fori(0, turns) as i:
                        for k in range(n_t):
                            act.wait_ge(s["xTp"], n_t * i + k + 1)
                            act.activation(xT[k], misc(k)[:, 0:P], ACT.Copy).then_inc(s["xT"], 1)
                        for k in range(n_t):
                            act.wait_ge(s["gu"], n_t * i + k + 1)
                            act.activation(hb[k], gu(k)[:, 0:F1], ACT.Silu).then_inc(s["silu"], 1)
                        for k in range(n_t):
                            act.wait_ge(s["yp"], n_t * i + k + 1)
                            act.activation(yb[k], gu(k)[:, 0:C], ACT.Copy).then_inc(s["y"], 1)
                        for k in range(n_t):
                            act.wait_ge(row_out[k], 16 * (i + 1))

                @block.vector
                def _(dve):
                    with dve.Fori(0, turns) as i:
                        for k in range(n_t):
                            dve.wait_ge(s["silu"], n_t * i + k + 1)
                            dve.tensor_tensor(hb[k], gu(k)[:, F1:2 * F1], hb[k], ALU.mult).then_inc(s["h"], 1)
                        for k in range(n_t):
                            dve.wait_ge(s["hTp"], n_t * i + k + 1)
                            dve.tensor_copy(hT[k], misc(k)[:, P:3 * P]).then_inc(s["hT"], 1)
        stage4()

        def stage5():
            n_t = IN_FLIGHT
            s = sems("s5", ["sum", "silu", "res"])
            got = [sem(f"s5_got{k}") for k in range(n_t)]
            ld = sem("s5_ld")
            stored = sem("s5_stored")

            def four(buf):
                return buf[:, :, :, :].rearrange("p g a b -> p (g a) b")
            yg, a1, a2 = four(v), four(z), four(att)
            ob = qk[:, 0, :, :].rearrange("p n (b c) -> p (n b) c", c=C)
            turns = NT // n_t
            with nc.Block() as block:
                @block.sync
                def _(sp):
                    def load(i):
                        sp.dma_start(a1, x1_t[:, bass.ds(n_t * i, n_t), :]).then_inc(ld, 16)
                        sp.dma_start(a2, sh_t[:, bass.ds(n_t * i, n_t), :]).then_inc(ld, 16)

                    def turn(i, last):
                        sp.wait_ge(s["res"], i + 1)
                        if not last:
                            load(i + 1)
                        sp.dma_start(out_t[:, bass.ds(n_t * i, n_t), :], ob).then_inc(stored, 16)
                    load(0)
                    with sp.Fori(0, turns - 1) as i:
                        turn(i, False)
                    turn(turns - 1, True)
                    sp.wait_ge(stored, 16 * turns)

                @block.gpsimd
                def _(pool):
                    def turn(i, first):
                        if not first:
                            pool.wait_ge(s["sum"], i)
                        pool.tensor_tensor(iw[:, :], iw[:, :], iw[:, :], ALU.subtract)
                        pool.tensor_copy(iv[:, :], SLOT[:, bass.ds(n_t * i, n_t)])
                        pool.drain()
                        for k in range(n_t):
                            pool.indirect_dma_start(out=yg[:, k, :], out_offset=None, in_=ysd[:, :],
                                                    in_offset=bass.IndirectOffsetOnAxis(ap=iv[:, k:k + 1], axis=0),
                                                    bounds_check=SORTED_TILES * P - 1).then_inc(got[k], 16)
                    pool.memset(iw[:, :], 0)
                    pool.drain()
                    turn(0, True)
                    with pool.Fori(1, turns) as i:
                        turn(i, False)

                @block.scalar
                def _(act):
                    with act.Fori(0, turns) as i:
                        act.wait_ge(s["sum"], i + 1)
                        act.activation(a2, a2, ACT.Silu).then_inc(s["silu"], 1)

                @block.vector
                def _(dve):
                    def turn(i, first):
                        for k in range(n_t):
                            dve.wait_ge(got[k], 16 * (i + 1))
                        dve.wait_ge(ld, 32 * (i + 1))
                        dve.tensor_tensor(a2, a2, yg, ALU.add).then_inc(s["sum"], 1)
                        dve.wait_ge(s["silu"], i + 1)
                        dve.tensor_tensor(a2, a2, X[:, bass.ds(n_t * i, n_t), :], ALU.mult)
                        dve.drain()
                        if not first:
                            dve.wait_ge(stored, 16 * i)
                        dve.tensor_tensor(ob, a2, a1, ALU.add).then_inc(s["res"], 1)
                    turn(0, True)
                    with dve.Fori(1, turns) as i:
                        turn(i, False)
        iv = sb("iv", [P, IN_FLIGHT], I32)
        iw = sb("iw", [P, 1], I32)
        stage5()


def pack(inputs):
    import numpy as np
    a = {k: np.asarray(v) for k, v in inputs.items()}
    f = np.float32
    d = {}
    d["x"] = a["L0_attn_x"].reshape(TOK, C)
    w = []
    for l in range(DEPTH):
        w += [a["L0_attn_wq"][l], a["L0_attn_wk"][l], a["L0_attn_wv"][l], a["L0_attn_wo"][l], a["L0_attn_w1"][l],
              a["L0_attn_w2"][l].reshape(FC, P, C).transpose(1, 0, 2).reshape(P, FC * C)]
    d["w0"] = np.concatenate(w, axis=1)
    c = []
    for l in range(DEPTH):
        c += [a[f"L0_attn_{n}"][l][:, None] for n in ("ln1_g", "ln1_b", "ln2_g", "ln2_b", "bq", "bk")]
        c.append(a["L0_attn_b1"][l].reshape(FC, P).T)
    c += [a["L1_attn_ln_g"][:, None], a["L1_attn_ln_b"][:, None]]
    d["cols"] = np.concatenate(c, axis=1)
    r = np.concatenate([a["L0_attn_bv"].reshape(-1), a["L1_attn_bq"], a["L1_attn_bk"].reshape(-1),
                        a["L1_attn_bv"].reshape(-1), a["L1_attn_bo"]])
    d["rows"] = np.broadcast_to(r[None, :], (P, r.size))
    freq = np.array([float.fromhex(h) for h in (
        "0x1.0p+0", "0x1.1cfed8p+0", "0x1.3d466cp+0", "0x1.6135f6p+0", "0x1.89377ap+0", "0x1.b5c0fcp+0",
        "0x1.e755dep+0", "0x1.0f4432p+1", "0x1.2dfdb2p+1", "0x1.503210p+1", "0x1.764638p+1", "0x1.a0aa7ap+1",
        "0x1.cfdbe8p+1", "0x1.0232dcp+2", "0x1.1f7176p+2", "0x1.3ffffep+2")], f)
    rad = ((np.arange(1, S + 1, dtype=f)[None, :] * freq[:, None]) * f(np.pi)).astype(np.float64)
    rad = np.concatenate([rad, rad])
    sign = np.where(np.arange(2 * freq.size) % 2 == 0, -1.0, 1.0)[:, None]
    head = np.concatenate([np.sin(rad) + sign * np.cos(rad), np.ones((DH - 2 * freq.size, S))])
    rk = np.concatenate([head] * HEADS)
    d["rot"] = np.concatenate([rk * DH ** -0.5, rk], axis=1).astype(f)
    k = np.zeros((P, NCST), f)
    p = np.arange(P)
    k[:, C_ID:C_ID + P] = np.eye(P)
    k[:, C_BLK:C_BLK + P] = (p[:, None] // LD == p[None, :] // LD) * (1.0 / S) ** 2
    k[:, C_TRI:C_TRI + P] = p[:, None] < p[None, :]
    k[:, C_IOTA:C_IOTA + E1] = np.arange(E1)
    k[:, C_TOKV:C_TOKV + NT] = TOK - P * np.arange(NT)[None, :] - p[:, None]
    k[:, C_ONE:C_ONE + P] = 1.0
    k[:, C_P] = p
    k[:, C_TILE:] = np.arange(SORTED_TILES)
    d["cst"] = k
    d["ws"] = np.concatenate([a["L0_ffn_router_w"].T, a["L0_ffn_ws_gate_up"]], axis=1)
    d["wsd"] = a["L0_ffn_ws_down"]
    d["we0"] = np.concatenate([a["L0_ffn_w_gate"], a["L0_ffn_w_up"]], axis=2)
    d["wd0"] = a["L0_ffn_w_down"]
    d["w1"] = np.concatenate([a["L1_attn_Wq"].T, a["L1_attn_Wk"][0].T, a["L1_attn_Wk"][1].T, a["L1_attn_Wv"][0].T,
                              a["L1_attn_Wv"][1].T, a["L1_attn_Wo"].T, a["L1_ffn_gate_w"], a["L1_ffn_shared_gate_w"],
                              a["L1_ffn_shared_up_w"],
                              a["L1_ffn_shared_down_w"].reshape(2, P, C).transpose(1, 0, 2).reshape(P, 2 * C)], axis=1)
    e = np.concatenate([a["L1_ffn_routed_gate_w"], a["L1_ffn_routed_up_w"],
                        a["L1_ffn_routed_down_w"].reshape(E1, 2, P, C).transpose(0, 2, 1, 3).reshape(E1, P, 2 * C)],
                       axis=2)
    d["we1"] = e.transpose(1, 0, 2).reshape(P, E1 * 768)
    return {n: np.ascontiguousarray(v) for n, v in d.items()}


_ARGS = ["x", "w0", "cols", "rows", "rot", "cst", "ws", "wsd", "we0", "wd0", "w1", "we1"]


def kernel(**inputs):
    import concourse.bacc as _bacc
    from concourse import mybir as _mybir
    from concourse.bass_utils import run_bass_kernel_spmd as _run

    arrays = pack(inputs)
    nc = _bacc.Bacc("TRN2", target_bir_lowering=False, num_devices=1)
    args = [nc.dram_tensor(n, arrays[n].shape, _mybir.dt.from_np(arrays[n].dtype), kind="ExternalInput").ap()
            for n in _ARGS]
    out = nc.dram_tensor("out", (TOK, C), F32, kind="ExternalOutput").ap()
    mixed_layers(nc, *args, out)
    r = _run(nc, [arrays], core_ids=[0])
    return r.results[0]["out"].reshape(B, S, C)
```

```python
from contextlib import ExitStack

import concourse.bass as bass
from concourse import mybir

F32 = mybir.dt.float32
BF16 = mybir.dt.bfloat16
I32 = mybir.dt.int32
U32 = mybir.dt.uint32
ALU = mybir.AluOpType
ACT = mybir.ActivationFunctionType
X_AXIS = mybir.AxisListType.X

P = 128
C = 128
B = 32
S = 256
TOK = B * S
NT = TOK // P
TPU = S // P
HALF = B // 2
HT = NT // 2
DEPTH = 2
HEADS = 2
DH = C // HEADS
FC = 4
E0, CAP, F0 = 64, 64, 96
E1, F1 = 32, 256
LH, LD = 16, 8
NP = 5 * C
XW = C + E0
EPT = E0 // HALF
SORTED_TILES = NT + E1
IN_FLIGHT = 4
PER_LOAD = 2
EPS = 1e-5
GELU = 1.702
NEG = -1e30

G1, B1, G2, B2, BQ, BK, BH = 0, 1, 2, 3, 4, 5, 6
NCOL = 6 + FC
C_ID, C_BLK, C_TRI, C_IOTA, C_TOKV, C_ONE, C_P = 0, 128, 256, 384, 416, 480, 608
C_TILE = 609
NCST = C_TILE + SORTED_TILES


def mixed_layers(nc, x, w0, cols, rows, rot, cst, ws, wsd, we0, wd0, w1, we1, out):
    xw = nc.dram_tensor("xw", (TOK, XW), F32, kind="Internal").ap()
    ffn0 = nc.dram_tensor("ffn0", (TOK + CAP, C), F32, kind="Internal").ap()
    x1d = nc.dram_tensor("x1d", (TOK, C), F32, kind="Internal").ap()
    shd = nc.dram_tensor("shd", (TOK, C), F32, kind="Internal").ap()
    xsd = nc.dram_tensor("xsd", (TOK, C), F32, kind="Internal").ap()
    srt = nc.dram_tensor("srt", (SORTED_TILES * P, C), F32, kind="Internal").ap()
    ysd = nc.dram_tensor("ysd", (SORTED_TILES * P, C), F32, kind="Internal").ap()

    def tiled(d):
        return d.rearrange("(t p) c -> p t c", p=P)

    x_t, xw_t, ffn0_t, x1_t, sh_t, xs_t = (tiled(d) for d in (x, xw, ffn0[0:TOK, :], x1d, shd, xsd))
    srt_t, ys_t, out_t = tiled(srt), tiled(ysd), tiled(out)

    ctx = ExitStack()
    with ctx:
        def sb(name, shape, dt=F32):
            return ctx.enter_context(nc.sbuf_tensor(name, shape, dt))

        def sem(name):
            return ctx.enter_context(nc.semaphore(name))

        def sems(stage, names):
            return {n: sem(f"{stage}_{n}") for n in names}

        ps = ctx.enter_context(nc.psum_tensor("ps", [P, 8, 512], F32))

        def bank(g, n):
            return ps[:, 4 * g + n, :]
        T, Q, S0, S1 = 0, 1, 2, 3

        X = sb("X", [P, NT, C])
        big = sb("big", [P, E1 * 768])
        keys = big[:, 0:HT * P]
        WE1 = big[:, :].rearrange("p (e f) -> p e f", e=E1)
        W0 = sb("W0", [P, DEPTH, 1536])

        def early(shape):
            return carve(big[:, :], early_at, shape)

        def late(shape):
            return carve(W0[:, :, :].rearrange("p d n -> p (d n)"), late_at, shape)
        early_at, late_at = [HT * P], [0]

        def carve(room, at, shape):
            n = 1
            for d in shape[1:]:
                n *= d
            at[0] += n
            assert at[0] <= room.shape[1]
            ap = room[0:shape[0], at[0] - n:at[0]]
            if len(shape) == 3:
                return ap.rearrange("p (a b) -> p a b", a=shape[1])
            if len(shape) == 4:
                return ap.rearrange("p (a b c) -> p a b c", a=shape[1], b=shape[2])
            return ap
        COL = sb("COL", [P, DEPTH * NCOL + 2])
        BHS = sb("BHS", [P, DEPTH, FC])
        ROW = sb("ROW", [P, DEPTH * C + NP + C])
        ROT = sb("ROT", [P, 2 * S])
        CST = sb("CST", [P, NCST])
        TRI = sb("TRI", [P, P], BF16)
        ONES = sb("ONES", [P, P], BF16)
        WS = sb("WS", [P, E0 + 2 * F0])
        WSD = sb("WSD", [F0, C])
        W1 = sb("W1", [P, 1568])
        MHALF = sb("MHALF", [P, 4])
        NG = 3 * LH * TPU
        PHALF = sb("PHALF", [P, 1])

        z0 = early([P, 2, TPU, C])
        z = sb("z", [P, 2, TPU, C])
        zT = sb("zT", [P, 2, S])
        xnT = early([P, 2, S])
        qk = sb("qk", [P, 2, 2, S])
        v = sb("v", [P, 2, TPU, C])
        pr = sb("pr", [P, 2, HEADS, TPU, S])
        pT = sb("pT", [P, 2, HEADS, TPU, S])
        att = sb("att", [P, 2, TPU, C])
        attT = sb("attT", [P, 2, S])
        st = sb("st", [P, 2, TPU, 6])
        mv = sb("mv", [P, 2, TPU, 2])
        ve = sb("ve", [P, 2, TPU])
        rs = sb("rs", [P, 2, TPU])
        nmx = sb("nmx", [P, 2, HEADS * TPU])
        sm = sb("sm", [P, 2, TPU, HEADS])
        rsm = sb("rsm", [P, 2, TPU, HEADS])
        xin = early([P, 2, TPU, C])
        ff = early([P, 2, TPU, C])

        ident = CST[:, C_ID:C_ID + P]

        def col(l, c):
            return COL[:, l * NCOL + c:l * NCOL + c + 1]

        def tiles(i, g):
            return bass.ds(TPU * i + HT * g, TPU)

        ld_small, ld_w, ld_late, zeroed = sem("ld_small"), sem("ld_w"), sem("ld_late"), sem("zeroed")
        in_sem = [sem(f"s1_xin{g}") for g in range(2)]
        zero = early([P, C])
        with nc.Block() as block:
            @block.sync
            def _(sp):
                for dst, src in ((COL, cols), (CST, cst), (ROW, rows), (ROT, rot), (WS, ws), (WSD, wsd)):
                    sp.dma_start(dst[:, :], src).then_inc(ld_small, 16)
                for g in range(2):
                    sp.dma_start(xin[:, g, :, :], x_t[:, HT * g:HT * g + TPU, :]).then_inc(in_sem[g], 16)
                sp.wait_ge(ld_small, 6 * 16)
                sp.wait_ge(ld_w, 16)

            @block.scalar
            def _(act):
                act.dma_start(W0[:, 0, :], w0[:, 0:1536]).then_inc(ld_w, 16)
                act.dma_start(W0[:, 1, :], w0[:, 1536:3072]).then_inc(ld_late, 16)
                act.dma_start(W1[:, :], w1).then_inc(ld_late, 16)

            @block.gpsimd
            def _(pool):
                pool.memset(zero[:, :], 0.0)
                pool.memset(MHALF[:, 0:2], -0.5)
                pool.memset(MHALF[:, 2:4], EPS)
                pool.memset(PHALF[:, :], 0.5)

            @block.vector
            def _(dve):
                dve.wait_ge(ld_small, 6 * 16)
                dve.tensor_copy(TRI[:, :], CST[:, C_TRI:C_TRI + P])
                dve.tensor_copy(ONES[:, :], CST[:, C_ONE:C_ONE + P])
                for l in range(DEPTH):
                    dve.tensor_scalar(BHS[:, l, :], COL[:, l * NCOL + BH:l * NCOL + BH + FC], GELU, None, ALU.mult)
                dve.wait_ge(ld_w, 16)
                dve.tensor_scalar(W0[:, 0, 1024:1536], W0[:, 0, 1024:1536], 1.0 / GELU, None, ALU.mult)

        LAYER = ["stats1", "rstd1", "z1", "zT1", "xl1", "qkv", "qkv_sb", "scores", "mx", "probs", "pT", "pT_A", "pT_B",
                 "pv", "att", "attTp", "attT", "wo", "stats2", "rstd2", "z2", "zT2", "xl2", "hid", "hT", "y", "xout"]

        layer_sems = sems("layer", LAYER)
        norm_sems = sems("norm", ["stats0", "rstd0", "xn", "xnTp", "xnT"])

        norm_bufs = (st, mv, ve, rs)

        def rstd_step(pool, s, u, g, ready, done, bufs=norm_bufs):
            _, mv, ve, rs = bufs
            pool.wait_ge(s[ready], u + 1)
            pool.tensor_tensor(ve[:, g, :], mv[:, g, :, 1], MHALF[:, 2:4], ALU.add)
            pool.drain()
            pool.tensor_tensor(rs[:, g, :], ve[:, g, :], MHALF[:, 0:2], ALU.pow).then_inc(s[done], 1)

        def stats_step(dve, g, src, done, bufs=norm_bufs):
            st, mv, _, _ = bufs
            for t in range(TPU):
                dve.bn_stats(st[:, g, t, :], src(t))
            dve.drain()
            for t in range(TPU):
                last = dve.bn_aggr(mv[:, g, t, :], st[:, g, t, :])
            last.then_inc(done, 1)

        def norm_step(dve, g, src, dst, done, bufs=norm_bufs):
            _, mv, _, rs = bufs
            for t in range(TPU):
                last = dve.tensor_scalar(dst(t), src(t), mv[:, g, t, 0:1], rs[:, g, t:t + 1], ALU.subtract, ALU.mult)
            last.then_inc(done, 1)

        def transpose_unit(pe, g, b, c0, src, done):
            for t in range(TPU):
                last = pe.transpose(bank(g, b)[:, c0 + t * P:c0 + (t + 1) * P], src[:, g, t, :], ident)
            last.then_inc(done, 1)

        def front_tensor(pe, s, i, l):
            for g in range(2):
                pe.wait_ge(s["z1"], 2 * (i + HALF * l) + g + 1)
                transpose_unit(pe, g, T, 0, z, s["zT1"])

        def layer_tensor(pe, s, i, l, after_att, after_wo, after_norm2, after_hidden, after_y, score_free, first,
                         hidden_free=None, ff_read=None):
            n0 = i + HALF * l
            wq, wk, wv, wo = (W0[:, l, n * C:(n + 1) * C] for n in range(4))
            for g in range(2):
                u = 2 * n0 + g
                pe.wait_ge(s["xl1"], u + 1)
                if not first:
                    pe.wait_ge(s["xout"], u - 1)
                for n, w in enumerate((wq, wk)):
                    pe.matmul(bank(g, Q)[:, n * S:(n + 1) * S], w, zT[:, g, :], start=True, stop=True)
                for t in range(TPU):
                    last = pe.matmul(bank(g, T)[:, S + t * C:S + (t + 1) * C], zT[:, g, t * P:(t + 1) * P], wv,
                                     start=True, stop=True)
                last.then_inc(s["qkv"], 1)
            for g in range(2):
                u = 2 * n0 + g
                pe.wait_ge(s["qkv_sb"], u + 1)
                score_free(g)
                for h in range(HEADS):
                    d = slice(h * DH, (h + 1) * DH)
                    for t in range(TPU):
                        last = pe.matmul(bank(g, S0 + h)[:, t * S:(t + 1) * S], qk[d, g, 0, t * P:(t + 1) * P],
                                         qk[d, g, 1, :], start=True, stop=True)
                    last.then_inc(s["scores"], 1)
            for g in range(2):
                u = 2 * n0 + g
                for h in range(HEADS):
                    pe.wait_ge(s["probs"], HEADS * u + h + 1)
                    for t in range(TPU):
                        for k in range(TPU):
                            last = pe.transpose(bank(g, S0 + h)[:, k * S + t * P:k * S + (t + 1) * P],
                                                pr[:, g, h, t, k * P:(k + 1) * P], ident)
                    last.then_inc(s["pT"], 1)
            for g in range(2):
                for h in range(HEADS):
                    pe.wait_ge(s[("pT_A", "pT_B")[g]], HEADS * n0 + h + 1)
                    for t in range(TPU):
                        for k in range(TPU):
                            last = pe.matmul(bank(g, Q)[:, t * C + h * DH:t * C + (h + 1) * DH],
                                             pT[:, g, h, k, t * P:(t + 1) * P], v[:, g, k, h * DH:(h + 1) * DH],
                                             start=(k == 0), stop=(k == TPU - 1))
                last.then_inc(s["pv"], 1)
            for g in range(2):
                u = 2 * n0 + g
                pe.wait_ge(s["att"], u + 1)
                transpose_unit(pe, g, T, 0, att, s["attTp"])
                after_att(g)
            for g in range(2):
                u = 2 * n0 + g
                pe.wait_ge(s["attT"], u + 1)
                for t in range(TPU):
                    last = pe.matmul(bank(g, Q)[:, S + t * C:S + (t + 1) * C], attT[:, g, t * P:(t + 1) * P], wo,
                                     start=True, stop=True)
                last.then_inc(s["wo"], 1)
            after_wo()
            for g in range(2):
                u = 2 * n0 + g
                pe.wait_ge(s["z2"], u + 1)
                transpose_unit(pe, g, T, 0, z, s["zT2"])
            after_norm2()
            for g in range(2):
                u = 2 * n0 + g
                pe.wait_ge(s["xl2"], u + 1)
                if hidden_free:
                    pe.wait_ge(hidden_free, 2 * i + g + 1)
                for f in range(FC):
                    last = pe.matmul(bank(g, S0 + f // 2)[:, f % 2 * S:(f % 2 + 1) * S],
                                     W0[:, l, 512 + f * P:512 + (f + 1) * P], zT[:, g, :], start=True, stop=True)
                    if f % 2:
                        last.then_inc(s["hid"], 1)
            after_hidden()
            for g in range(2):
                u = 2 * n0 + g
                pe.wait_ge(s["hT"], u + 1)
                if ff_read:
                    pe.wait_ge(ff_read, 2 * i + g + 1)
                for t in range(TPU):
                    for f in range(FC):
                        last = pe.matmul(bank(g, Q)[:, t * C:(t + 1) * C],
                                         pr[:, g, f // 2, f % 2, t * P:(t + 1) * P],
                                         W0[:, l, 1024 + f * C:1024 + (f + 1) * C], start=(f == 0), stop=(f == FC - 1))
                last.then_inc(s["y"], 1)
            after_y()

        def affine_step(act, g, scale, bias, done):
            act.activation(zT[:, g, :], bank(g, T)[:, 0:S], ACT.Identity, bias=bias, scale=scale).then_inc(done, 1)

        def front_scalar(act, s, i, l):
            for g in range(2):
                act.wait_ge(s["zT1"], 2 * (i + HALF * l) + g + 1)
                affine_step(act, g, col(l, G1), col(l, B1), s["xl1"])

        def layer_scalar(act, s, i, l, before_norm2):
            n0 = i + HALF * l
            for g in range(2):
                for h in range(HEADS):
                    act.wait_ge(s["mx"], HEADS * (2 * n0 + g) + h + 1)
                    for t in range(TPU):
                        last = act.activation(pr[:, g, h, t, :], bank(g, S0 + h)[:, t * S:(t + 1) * S], ACT.Exp,
                                              bias=nmx[:, g, h * TPU + t:h * TPU + t + 1],
                                              accum_out=sm[:, g, t, h:h + 1])
                    last.then_inc(s["probs"], 1)
            for h in range(HEADS):
                act.wait_ge(s["pT"], HEADS * (2 * n0 + 1) + h + 1)
                act.activation(pT[:, 1, h, :, :].rearrange("p k q -> p (k q)"), bank(1, S0 + h), ACT.Copy)\
                   .then_inc(s["pT_B"], 1)
            before_norm2()
            for g in range(2):
                act.wait_ge(s["zT2"], 2 * n0 + g + 1)
                affine_step(act, g, col(l, G2), col(l, B2), s["xl2"])
            for g in range(2):
                for f in range(FC):
                    if f % 2 == 0:
                        act.wait_ge(s["hid"], 2 * (2 * n0 + g) + f // 2 + 1)
                    last = act.activation(pr[:, g, f // 2, f % 2, :], bank(g, S0 + f // 2)[:, f % 2 * S:(f % 2 + 1) * S],
                                          ACT.Silu, bias=BHS[:, l, f:f + 1], scale=GELU)
                last.then_inc(s["hT"], 1)

        def front_vector(dve, s, i, l, src):
            for g in range(2):
                stats_step(dve, g, lambda t: src(i, g, t), s["stats1"])
            for g in range(2):
                dve.wait_ge(s["rstd1"], 2 * (i + HALF * l) + g + 1)
                norm_step(dve, g, lambda t: src(i, g, t), lambda t: z[:, g, t, :], s["z1"])

        def by_tile(ap):
            return ap.rearrange("p (t c) -> p t c", t=TPU)

        def layer_vector(dve, s, i, l, unit_src, before_hidden, ahead, after_y, after_probs=None):
            n0 = i + HALF * l
            for g in range(2):
                dve.wait_ge(s["qkv"], 2 * n0 + g + 1)
                for n, c in enumerate((BQ, BK)):
                    dve.scalar_tensor_tensor(qk[:, g, n, :], bank(g, Q)[:, n * S:(n + 1) * S], col(l, c),
                                             ROT[:, n * S:(n + 1) * S], ALU.add, ALU.mult)
                dve.tensor_tensor(v[:, g, :, :], bank(g, T)[:, S:2 * S].rearrange("p (t c) -> p t c", t=TPU),
                                  ROW[:, l * C:(l + 1) * C].unsqueeze(1).to_broadcast([P, TPU, C]), ALU.add)\
                   .then_inc(s["qkv_sb"], 1)
            for g in range(2):
                for h in range(HEADS):
                    dve.wait_ge(s["scores"], HEADS * (2 * n0 + g) + h + 1)
                    dve.tensor_reduce(nmx[:, g, h * TPU:(h + 1) * TPU],
                                      bank(g, S0 + h).rearrange("p (t k) -> p t k", t=TPU),
                                      X_AXIS, ALU.max, negate=True).then_inc(s["mx"], 1)
            for h in range(HEADS):
                dve.wait_ge(s["pT"], HEADS * 2 * n0 + h + 1)
                dve.tensor_copy(pT[:, 0, h, :, :].rearrange("p k q -> p (k q)"), bank(0, S0 + h))\
                   .then_inc(s["pT_A"], 1)
            dve.wait_ge(s["probs"], HEADS * (2 * n0 + 2))
            dve.reciprocal(rsm[:, :, :, :], sm[:, :, :, :])
            if after_probs:
                after_probs()
            dve.drain()
            for g in range(2):
                dve.wait_ge(s["pv"], 2 * n0 + g + 1)
                dve.tensor_tensor(att[:, g, :, :].rearrange("p t (h d) -> p (t h) d", h=HEADS),
                                  bank(g, Q)[:, 0:S].rearrange("p (a d) -> p a d", d=DH),
                                  rsm[:, g, :, :].rearrange("p t h -> p (t h)").unsqueeze(2)
                                  .to_broadcast([P, TPU * HEADS, DH]), ALU.mult).then_inc(s["att"], 1)
            for g in range(2):
                dve.wait_ge(s["attTp"], 2 * n0 + g + 1)
                dve.tensor_copy(attT[:, g, :], bank(g, T)[:, 0:S]).then_inc(s["attT"], 1)
            for g in range(2):
                dve.wait_ge(s["wo"], 2 * n0 + g + 1)
                dve.tensor_tensor(X[:, tiles(i, g), :], by_tile(bank(g, Q)[:, S:2 * S]), unit_src(i, g), ALU.add)
                dve.drain()
                stats_step(dve, g, lambda t: X[:, TPU * i + HT * g + t, :], s["stats2"])
            for g in range(2):
                dve.wait_ge(s["rstd2"], 2 * n0 + g + 1)
                norm_step(dve, g, lambda t: X[:, TPU * i + HT * g + t, :], lambda t: z[:, g, t, :], s["z2"])
            before_hidden()
            for g in range(2):
                dve.wait_ge(s["zT2"], 2 * n0 + g + 1)
            ahead()
            for g in range(2):
                dve.wait_ge(s["y"], 2 * n0 + g + 1)
                dve.tensor_tensor(X[:, tiles(i, g), :], by_tile(bank(g, Q)[:, 0:S]), X[:, tiles(i, g), :], ALU.add)\
                   .then_inc(s["xout"], 1)
            after_y()

        lg = early([P, 2, TPU, E0])
        rep = early([P, 2, TPU, E0])
        ex = early([P, 2, TPU, E0])
        mx8 = early([P, 2, TPU, 8])
        nl = early([P, 2, TPU])
        sw = early([P, 2, TPU])
        rsw = early([P, 2, TPU])
        wr = early([P, 2, TPU, E0])
        kk = early([P, TPU, 2, E0])
        hs = early([F0, 2, S])

        def stage1():
            s = dict(layer_sems)
            s.update(norm_sems)
            s.update(sems("s1", ["logits", "lg", "lmax", "lexp", "wrow", "key",
                                    "keyTp", "keyT", "gu", "sg", "hs", "down", "ff"]))
            xn_out = [sem(f"s1_xn_out{g}") for g in range(2)]
            w_out = [sem(f"s1_w_out{g}") for g in range(2)]
            ff_out = [sem(f"s1_ff_out{g}") for g in range(2)]
            with nc.Block() as block:
                @block.sync
                def _(sp):
                    sp.dma_start(srt_t, zero[:, :].unsqueeze(1).to_broadcast([P, SORTED_TILES, C])).then_inc(zeroed, 16)

                    def turn(i, last):
                        for g in range(2):
                            u = 2 * i + g
                            sp.wait_ge(s["xn"], u + 1)
                            if not last:
                                sp.dma_start(xin[:, g, :, :], x_t[:, tiles(i + 1, g), :]).then_inc(in_sem[g], 16)
                            sp.dma_start(xw_t[:, tiles(i, g), 0:C], z0[:, g, :, :]).then_inc(xn_out[g], 16)
                        for g in range(2):
                            u = 2 * i + g
                            sp.wait_ge(s["wrow"], u + 1)
                            sp.dma_start(xw_t[:, tiles(i, g), C:XW], wr[:, g, :, :]).then_inc(w_out[g], 16)
                        for g in range(2):
                            u = 2 * i + g
                            sp.wait_ge(s["ff"], u + 1)
                            sp.dma_start(ffn0_t[:, tiles(i, g), :], ff[:, g, :, :]).then_inc(ff_out[g], 16)

                    with sp.Fori(0, HALF - 1) as i:
                        turn(i, False)
                    turn(HALF - 1, True)
                    sp.wait_ge(zeroed, 16)
                    sp.wait_ge(ld_late, 32)
                    for g in range(2):
                        sp.wait_ge(xn_out[g], 16 * HALF)
                        sp.wait_ge(w_out[g], 16 * HALF)
                        sp.wait_ge(ff_out[g], 16 * HALF)

                @block.gpsimd
                def _(pool):
                    def ahead(i):
                        for n in ("0", "1"):
                            for g in range(2):
                                rstd_step(pool, s, 2 * i + g, g, "stats" + n, "rstd" + n)

                    def turn(i, last):
                        for g in range(2):
                            rstd_step(pool, s, 2 * i + g, g, "stats2", "rstd2")
                        if not last:
                            ahead(i + 1)
                    ahead(0)
                    with pool.Fori(0, HALF - 1) as i:
                        turn(i, False)
                    turn(HALF - 1, True)

                @block.tensor
                def _(pe):
                    def turn_rows(i, first=False):
                        if not first:
                            pe.wait_ge(s["keyT"], i)
                        for g in range(2):
                            pe.wait_ge(s["xn"], 2 * i + g + 1)
                            transpose_unit(pe, g, T, 0, z0, s["xnTp"])

                    def ahead(i):
                        for g in range(2):
                            pe.wait_ge(s["xnT"], 2 * i + g + 1)
                        front_tensor(pe, s, i, 0)
                        for g in range(2):
                            for t in range(TPU):
                                last = pe.matmul(bank(g, S0)[:, t * E0:(t + 1) * E0],
                                                 xnT[:, g, t * P:(t + 1) * P], WS[:, 0:E0], start=True, stop=True)
                            last.then_inc(s["logits"], 1)

                    def turn(i, first, final):
                        def key_transposes():
                            pe.wait_ge(s["key"], i + 1)
                            pe.wait_ge(s["xl2"], 2 * i + 2)
                            for t in range(TPU):
                                last = pe.transpose(bank(1, T)[:, S + t * P:S + (t + 1) * P],
                                                    kk[:, t, :, :].rearrange("p g e -> p (g e)"), ident)
                            last.then_inc(s["keyTp"], 1)

                        def shared(g):
                            for n in range(2):
                                last = pe.matmul(bank(g, S0)[0:F0, n * S:(n + 1) * S],
                                                 WS[:, E0 + n * F0:E0 + (n + 1) * F0], xnT[:, g, :],
                                                 start=True, stop=True)
                            last.then_inc(s["gu"], 1)

                        def shared_down():
                            for g in range(2):
                                pe.wait_ge(s["hs"], 2 * i + g + 1)
                                for t in range(TPU):
                                    last = pe.matmul(bank(g, Q)[:, t * C:(t + 1) * C],
                                                     hs[:, g, t * P:(t + 1) * P], WSD[:, :], start=True, stop=True)
                                last.then_inc(s["down"], 1)
                            key_transposes()

                        layer_tensor(pe, s, i, 0, after_att=shared, after_wo=lambda: None,
                                     after_norm2=shared_down,
                                     after_hidden=lambda: None if final else turn_rows(i + 1),
                                     after_y=lambda: None if final else ahead(i + 1),
                                     score_free=lambda g: pe.wait_ge(s["lg"], 2 * i + g + 1), ff_read=s["ff"],
                                     first=first)
                    turn_rows(0, True)
                    ahead(0)
                    turn(0, True, False)
                    with pe.Fori(1, HALF - 1) as i:
                        turn(i, False, False)
                    turn(HALF - 1, False, True)

                @block.scalar
                def _(act):
                    def ahead(i):
                        for g in range(2):
                            act.wait_ge(s["xnTp"], 2 * i + g + 1)
                            act.activation(xnT[:, g, :], bank(g, T)[:, 0:S], ACT.Copy).then_inc(s["xnT"], 1)
                        front_scalar(act, s, i, 0)

                    def turn(i, final):
                        def silu():
                            act.wait_ge(s["lmax"], i + 1)
                            for g in range(2):
                                for t in range(TPU):
                                    last = act.activation(ex[:, g, t, :], lg[:, g, t, :], ACT.Exp,
                                                          bias=nl[:, g, t:t + 1])
                            last.then_inc(s["lexp"], 1)
                            for g in range(2):
                                act.wait_ge(s["gu"], 2 * i + g + 1)
                                act.activation(hs[:, g, :], bank(g, S0)[0:F0, 0:S], ACT.Silu).then_inc(s["sg"], 1)

                        layer_scalar(act, s, i, 0, before_norm2=silu)
                        if not final:
                            ahead(i + 1)
                    ahead(0)
                    with act.Fori(0, HALF - 1) as i:
                        turn(i, False)
                    turn(HALF - 1, True)

                @block.vector
                def _(dve):
                    def from_z0(i, g, t):
                        return z0[:, g, t, :]

                    def stats(i):
                        for g in range(2):
                            dve.wait_ge(in_sem[g], 16 * (i + 1))
                            stats_step(dve, g, lambda t: xin[:, g, t, :], s["stats0"])

                    def norms(i):
                        for g in range(2):
                            dve.wait_ge(s["rstd0"], 2 * i + g + 1)
                            norm_step(dve, g, lambda t: xin[:, g, t, :], lambda t: z0[:, g, t, :], s["xn"])
                        dve.drain()
                        front_vector(dve, s, i, 0, from_z0)

                    def logits(i):
                        for g in range(2):
                            dve.wait_ge(s["logits"], 2 * i + g + 1)
                            dve.tensor_copy(lg[:, g, :, :].rearrange("p t e -> p (t e)"),
                                            bank(g, S0)[:, 0:TPU * E0]).then_inc(s["lg"], 1)

                    def turn(i, final):
                        def router():
                            units = [(g, t) for g in range(2) for t in range(TPU)]
                            for g, t in units:
                                dve.max(out=mx8[:, g, t, :], in_=lg[:, g, t, :])
                            dve.drain()
                            dve.tensor_scalar(nl[:, :, :], mx8[:, :, :, 0], -1.0, None, ALU.mult)\
                               .then_inc(s["lmax"], 1)
                            for g, t in units:
                                dve.match_replace(out=rep[:, g, t, :], in_to_replace=mx8[:, g, t, :],
                                                  in_values=lg[:, g, t, :], imm_value=NEG)
                            dve.drain()
                            for g, t in units:
                                last = dve.tensor_scalar(kk[:, t, g, :], rep[:, g, t, :], NEG / 2,
                                                         CST[:, bass.ds(C_TOKV + TPU * i + HT * g + t, 1)],
                                                         ALU.is_lt, ALU.mult)
                            last.then_inc(s["key"], 1)

                        def weights():
                            dve.wait_ge(s["lexp"], i + 1)
                            for g in range(2):
                                for t in range(TPU):
                                    dve.scalar_tensor_tensor(ex[:, g, t, :], rep[:, g, t, :], NEG / 2, ex[:, g, t, :],
                                                             ALU.is_lt, ALU.mult, accum_out=sw[:, g, t:t + 1])
                            dve.drain()
                            dve.reciprocal(rsw[:, :, :], sw[:, :, :])
                            dve.drain()
                            for g in range(2):
                                dve.tensor_tensor(wr[:, g, :, :], ex[:, g, :, :],
                                                  rsw[:, g, :].unsqueeze(2).to_broadcast([P, TPU, E0]), ALU.mult)\
                                   .then_inc(s["wrow"], 1)

                        def shared():
                            for g in range(2):
                                dve.wait_ge(s["sg"], 2 * i + g + 1)
                                dve.tensor_tensor(hs[:, g, :], bank(g, S0)[0:F0, S:2 * S], hs[:, g, :], ALU.mult)\
                                   .then_inc(s["hs"], 1)

                        def ahead():
                            if not final:
                                stats(i + 1)
                            for g in range(2):
                                dve.wait_ge(s["down"], 2 * i + g + 1)
                                dve.tensor_copy(ff[:, g, :, :].rearrange("p t c -> p (t c)"), bank(g, Q)[:, 0:S])\
                                   .then_inc(s["ff"], 1)
                            dve.wait_ge(s["keyTp"], i + 1)
                            dve.tensor_copy(keys[:, bass.ds(S * i, S)], bank(1, T)[:, S:2 * S]).then_inc(s["keyT"], 1)
                            if not final:
                                for g in range(2):
                                    dve.wait_ge(xn_out[g], 16 * (i + 1))
                                norms(i + 1)
                            weights()

                        layer_vector(dve, s, i, 0, lambda i, g: z0[:, g, :, :], after_probs=router, before_hidden=shared, ahead=ahead,
                                     after_y=lambda: None)
                        for g in range(2):
                            dve.wait_ge(w_out[g], 16 * (i + 1))
                            dve.wait_ge(ff_out[g], 16 * (i + 1))
                        if not final:
                            logits(i + 1)
                    stats(0)
                    norms(0)
                    logits(0)
                    with dve.Fori(0, HALF - 1) as i:
                        turn(i, False)
                    turn(HALF - 1, True)
        stage1()

        gidx = sb("gidx", [CAP, E0], I32)
        sidx = sb("sidx", [CAP, E0], I32)

        def pick():
            lst = early([P, CAP])
            both = early([E0, 2 * CAP])
            fin = early([E0, CAP])
            kf = early([CAP, E0])
            tk = early([CAP, E0])
            em = early([CAP, E0])
            halves, moved, firsts, turned = sem("p_halves"), sem("p_moved"), sem("p_firsts"), sem("p_turned")
            with nc.Block() as block:
                @block.gpsimd
                def _(pool):
                    for n in range(NP // C):
                        pool.tensor_tensor(W1[:, n * C:(n + 1) * C], W1[:, n * C:(n + 1) * C], ident, ALU.add)
                    pool.tensor_scalar(W0[:, 1, 1024:1536], W0[:, 1, 1024:1536], 1.0 / GELU, None, ALU.mult)

                @block.sync
                def _(sp):
                    sp.wait_ge(halves, 1)
                    sp.dma_start(both[:, CAP:2 * CAP], lst[E0:P, :]).then_inc(moved, 16)
                    sp.wait_ge(moved, 16)

                @block.tensor
                def _(pe):
                    pe.wait_ge(firsts, 1)
                    pe.transpose(bank(0, T)[0:CAP, 0:E0], fin[:, :], ident[0:E0, 0:E0]).then_inc(turned, 1)

                @block.vector
                def _(dve):
                    def largest(dst, src):
                        for r in range(CAP // 8):
                            dve.max(out=dst[:, 8 * r:8 * r + 8], in_=src)
                            dve.drain()
                            if r < CAP // 8 - 1:
                                dve.match_replace(out=src, in_to_replace=dst[:, 8 * r:8 * r + 8], in_values=src,
                                                  imm_value=0.0)
                                dve.drain()
                    largest(lst, keys)
                    dve.tensor_copy(both[:, 0:CAP], lst[0:E0, :]).then_inc(halves, 1)
                    dve.drain()
                    dve.wait_ge(moved, 16)
                    largest(fin, both[:, :])
                    dve.tensor_copy(em[:, :], CST[0:CAP, C_ONE:C_ONE + E0]).then_inc(firsts, 1)
                    dve.wait_ge(turned, 1)
                    dve.tensor_copy(kf[:, :], bank(0, T)[0:CAP, 0:E0])
                    dve.drain()
                    dve.tensor_scalar(tk[:, :], kf[:, :], -1.0, float(TOK), ALU.mult, ALU.add)
                    dve.tensor_scalar(em[:, :], kf[:, :], 0.0, CST[0:CAP, C_P:C_P + 1], ALU.is_equal, ALU.mult)
                    dve.drain()
                    dve.tensor_scalar(gidx[:, :], tk[:, :], float(TOK - 1), None, ALU.min)
                    dve.tensor_tensor(sidx[:, :], tk[:, :], em[:, :], ALU.add)
        pick()

        wg = early([P, EPT, 2 * F0])
        wdn = early([F0, EPT, C])
        gi = sb("gi", [CAP, EPT], I32)
        si = sb("si", [CAP, EPT], I32)
        carrier = sb("carrier", [CAP, EPT + 1])
        xe = early([CAP, EPT, XW])
        xeT = early([P, EPT, CAP])
        he = early([CAP, EPT, F0])
        heT = early([F0, EPT, CAP])
        ye = early([CAP, EPT, C])
        EG = EPT // 2

        def stage2():
            s = dict(layer_sems)
            s.update(sems("s2", ["xeTp", "xeT", "eg", "es", "eh", "ehTp", "ehT", "ey", "ye", "idx"]))
            we_in = sem("s2_we_in")
            rows_in = [sem(f"s2_rows_in{j}") for j in range(EPT)]
            added = sem("s2_added")
            with nc.Block() as block:
                @block.sync
                def _(sp):
                    def load_experts(i):
                        sp.dma_start(wg[:, :, :], we0[bass.ds(EPT * i, EPT), :, :].rearrange("e p f -> p e f"))\
                          .then_inc(we_in, 16)
                        sp.dma_start(wdn[:, :, :], wd0[bass.ds(EPT * i, EPT), :, :].rearrange("e p f -> p e f"))\
                          .then_inc(we_in, 16)
                    load_experts(0)
                    with sp.Fori(0, HALF - 1) as i:
                        sp.wait_ge(s["ey"], 2 * i + 2)
                        load_experts(i + 1)
                    sp.wait_ge(we_in, 32 * HALF)

                @block.gpsimd
                def _(pool):
                    pool.memset(carrier[:, :], 0.0)
                    pool.drain()

                    def carry_wait(n):
                        pool.tensor_tensor(carrier[:, n:n + 1], carrier[:, EPT:EPT + 1], carrier[:, EPT:EPT + 1], ALU.add)

                    def ahead(i):
                        for g in range(2):
                            rstd_step(pool, s, B + 2 * i + g, g, "stats1", "rstd1")

                    def scatter(i, j):
                        pool.indirect_dma_start(out=ffn0[:, :],
                                                out_offset=bass.IndirectOffsetOnAxis(ap=si[:, j:j + 1], axis=0),
                                                in_=ye[:, j, :], in_offset=None, bounds_check=TOK + CAP - 1,
                                                compute_op=ALU.add).then_inc(added, 16)

                    def scattered(i, j):
                        pool.wait_ge(added, 16 * (EPT * i + j + 1))

                    def turn(i, first, final):
                        pool.wait_ge(s["idx"], i + 1)
                        carry_wait(EPT - 1)
                        for j in range(EPT):
                            if not first:
                                scatter(i - 1, j)
                            pool.indirect_dma_start(out=xe[:, j, :], out_offset=None, in_=xw[:, :],
                                                    in_offset=bass.IndirectOffsetOnAxis(ap=gi[:, j:j + 1], axis=0),
                                                    bounds_check=TOK - 1).then_inc(rows_in[j], 16)
                            if not first:
                                scattered(i - 1, j)
                                if j < EPT - 1:
                                    carry_wait(j)
                        for g in range(2):
                            rstd_step(pool, s, B + 2 * i + g, g, "stats2", "rstd2")
                        if not final:
                            ahead(i + 1)

                    ahead(0)
                    turn(0, True, False)
                    with pool.Fori(1, HALF - 1) as i:
                        turn(i, False, False)
                    turn(HALF - 1, False, True)
                    pool.wait_ge(s["idx"], HALF + 1)
                    for j in range(EPT):
                        scatter(HALF - 1, j)
                        scattered(HALF - 1, j)

                @block.tensor
                def _(pe):
                    def turn(i, first, final):
                        def experts(part, units=(0, 1)):
                            for g in units:
                                u = 2 * i + g
                                for j in range(EG):
                                    n = EG * g + j
                                    if part == 0:
                                        pe.wait_ge(rows_in[n], 16 * (i + 1))
                                        last = pe.matmul(bank(g, S0)[:, j * CAP:(j + 1) * CAP], xe[:, n, 0:C],
                                                         ident[0:CAP, 0:CAP], start=True, stop=True)
                                    if part == 1:
                                        if j == 0:
                                            pe.wait_ge(s["xeT"], u + 1)
                                            pe.wait_ge(we_in, 32 * (i + 1))
                                        last = pe.matmul(bank(g, S1)[0:CAP, j * S:j * S + 2 * F0], xeT[:, n, :],
                                                         wg[:, n, :], start=True, stop=True)
                                    if part == 2:
                                        last = pe.matmul(bank(g, T)[0:F0, j * CAP:(j + 1) * CAP], he[:, n, :],
                                                         ident[0:CAP, 0:CAP], start=True, stop=True)
                                    if part == 3:
                                        last = pe.matmul(bank(g, S0)[0:CAP, j * C:(j + 1) * C], heT[:, n, :],
                                                         wdn[:, n, :], start=True, stop=True)
                                last.then_inc(s[("xeTp", "eg", "ehTp", "ey")[part]], 1)

                        def after_y():
                            for g in range(2):
                                pe.wait_ge(s["ehT"], 2 * i + g + 1)
                            if not final:
                                front_tensor(pe, s, i + 1, 1)
                            experts(3)
                        layer_tensor(pe, s, i, 1, after_att=lambda g: experts(0, (g,)), after_wo=lambda: experts(1),
                                     after_norm2=lambda: None, after_hidden=lambda: experts(2), after_y=after_y,
                                     hidden_free=s["eh"], first=False,
                                     score_free=lambda g: None if first else pe.wait_ge(s["ye"], 2 * i + g - 1))
                    front_tensor(pe, s, 0, 1)
                    turn(0, True, False)
                    with pe.Fori(1, HALF - 1) as i:
                        turn(i, False, False)
                    turn(HALF - 1, False, True)

                @block.scalar
                def _(act):
                    def turn(i, final):
                        def rows():
                            for g in range(2):
                                act.wait_ge(s["xeTp"], 2 * i + g + 1)
                                act.activation(xeT[:, EG * g:EG * (g + 1), :].rearrange("p j c -> p (j c)"),
                                               bank(g, S0)[:, 0:EG * CAP], ACT.Copy).then_inc(s["xeT"], 1)

                        def silu():
                            for g in range(2):
                                act.wait_ge(s["eg"], 2 * i + g + 1)
                                act.activation(he[:, EG * g:EG * (g + 1), :],
                                               bank(g, S1)[0:CAP, :].rearrange("p (j f) -> p j f", j=EG)[:, :, 0:F0],
                                               ACT.Silu).then_inc(s["es"], 1)
                        layer_scalar(act, s, i, 1, before_norm2=lambda: (rows(), silu()))
                        if not final:
                            front_scalar(act, s, i + 1, 1)
                    front_scalar(act, s, 0, 1)
                    with act.Fori(0, HALF - 1) as i:
                        turn(i, False)
                    turn(HALF - 1, True)

                @block.vector
                def _(dve):
                    def from_x(i, g, t):
                        return X[:, TPU * i + HT * g + t, :]

                    def turn(i, final):
                        def hidden():
                            for g in range(2):
                                e = slice(EG * g, EG * (g + 1))
                                dve.wait_ge(s["es"], 2 * i + g + 1)
                                dve.tensor_tensor(he[:, e, :],
                                                  bank(g, S1)[0:CAP, :].rearrange("p (j f) -> p j f", j=EG)
                                                  [:, :, F0:2 * F0], he[:, e, :], ALU.mult).then_inc(s["eh"], 1)
                            for g in range(2):
                                dve.wait_ge(s["ehTp"], 2 * i + g + 1)
                                dve.tensor_copy(heT[:, EG * g:EG * (g + 1), :].rearrange("p j c -> p (j c)"),
                                                bank(g, T)[0:F0, 0:EG * CAP]).then_inc(s["ehT"], 1)

                        def weighted():
                            for g in range(2):
                                dve.wait_ge(s["ey"], 2 * i + g + 1)
                                for j in range(EG):
                                    n = EG * g + j
                                    last = dve.tensor_scalar(ye[:, n, :], bank(g, S0)[0:CAP, j * C:(j + 1) * C],
                                                             xe[:, n, bass.ds(EPT * i + C + n, 1)], None, ALU.mult)
                                last.then_inc(s["ye"], 1)
                            if not final:
                                dve.tensor_copy(gi[:, :], gidx[:, bass.ds(EPT * (i + 1), EPT)])
                            dve.tensor_copy(si[:, :], sidx[:, bass.ds(EPT * i, EPT)]).then_inc(s["idx"], 1)

                        layer_vector(dve, s, i, 1, lambda i, g: X[:, tiles(i, g), :], before_hidden=hidden, after_y=weighted,
                                     ahead=lambda: None if final else front_vector(dve, s, i + 1, 1, from_x))
                    dve.tensor_copy(gi[:, :], gidx[:, 0:EPT]).then_inc(s["idx"], 1)
                    front_vector(dve, s, 0, 1, from_x)
                    with dve.Fori(0, HALF - 1) as i:
                        turn(i, False)
                    turn(HALF - 1, True)
        stage2()

        EID = sb("EID", [P, NT])
        RNK = sb("RNK", [P, NT])
        SLOT = sb("SLOT", [P, NT])
        TE = sb("TE", [1, SORTED_TILES], I32)
        cum = sb("cum", [P, 2, E1], BF16)

        def stage3():
            s = dict(norm_sems)
            s.update(sems("s3", ["gsil", "x1", "proj", "biased", "silu", "sq", "n2",
                            "nrm", "kn", "lg", "top", "tanh", "sc", "xs", "oh", "cum", "rank", "gu", "sgate",
                            "hmul", "down", "sh", "states", "state", "qTp", "qT", "lin", "stats2", "rstd2", "z2",
                            "zTp", "zT", "wo", "s1"]))
            in_bufs = (late([P, 2, TPU, 6]), late([P, 2, TPU, 2]), late([P, 2, TPU]), late([P, 2, TPU]))
            xin3 = late([P, 2, TPU, C])
            gin = late([P, 2, TPU, C])
            x1b = late([P, 2, TPU, C])
            pj = [pr[:, g, :, :, :].rearrange("p a b c -> p (a b c)") for g in range(2)]
            qkp = [ctx.enter_context(nc.sbuf_tensor(f"qkp{g}", [P, TPU, 3 * C], F32)) for g in range(2)]
            sqb = [pj[g][:, 0:TPU * 3 * C].rearrange("p (t c) -> p t c", t=TPU) for g in range(2)]
            vv = [pT[:, g, :, :, :].rearrange("p a b c -> p (a b c)")[:, 0:TPU * 2 * C]
                  .rearrange("p (t c) -> p t c", t=TPU) for g in range(2)]
            hid = [pT[:, g, :, :, :].rearrange("p a b c -> p (a b c)")[:, 512:1024] for g in range(2)]
            xn = z
            xnT3 = attT
            qT = qk[:, :, 0, :]
            stt_ = [qk[:, g, 1, 0:C] for g in range(2)]
            st0 = [qk[:, g, 1, C:2 * C] for g in range(2)]
            z2 = v
            xsb = att
            shb = late([P, 2, TPU, C])
            n2 = late([P, 2, NG])
            rn = late([P, 2, NG])
            lg1 = late([P, 2, TPU, E1])
            m8 = late([P, 2, TPU, 8])
            i8 = sb("i8", [P, 2, TPU, 8], U32)
            ei = late([P, 2, TPU])
            th = late([P, 2, TPU])
            sc = late([P, 2, TPU])
            rk = late([P, 2, TPU])
            oh = sb("oh", [P, 2, TPU, E1], BF16)
            ct = sb("ct", [P, 2, E1], BF16)
            junk = late([P, 2, TPU, E1])
            RANKS = S + TPU * E1
            W_WO, W_GATE, W_SG, W_SU, W_SD = 640, 768, 800, 1056, 1312
            in_x = [sem(f"s3_in_x{g}") for g in range(2)]
            in_g = [sem(f"s3_in_g{g}") for g in range(2)]
            o_x1 = [sem(f"s3_o_x1{g}") for g in range(2)]
            o_xs = [sem(f"s3_o_xs{g}") for g in range(2)]
            o_sh = [sem(f"s3_o_sh{g}") for g in range(2)]
            we1_in = sem("s3_we1")
            ls, lb = (COL[:, DEPTH * NCOL + n:DEPTH * NCOL + n + 1] for n in range(2))

            with nc.Block() as block:
                @block.sync
                def _(sp):
                    def load(i, g):
                        sp.dma_start(xin3[:, g, :, :], x_t[:, tiles(i, g), :]).then_inc(in_x[g], 16)
                        sp.dma_start(gin[:, g, :, :], ffn0_t[:, tiles(i, g), :]).then_inc(in_g[g], 16)

                    n_w = E1 * 768 // HALF

                    def turn(i, last):
                        for g in range(2):
                            sp.wait_ge(s["x1"], 2 * i + g + 1)
                            if not last:
                                load(i + 1, g)
                            sp.dma_start(x1_t[:, tiles(i, g), :], x1b[:, g, :, :]).then_inc(o_x1[g], 16)
                        sp.dma_start(big[:, bass.ds(n_w * i, n_w)], we1[:, bass.ds(n_w * i, n_w)]).then_inc(we1_in, 16)
                        for g in range(2):
                            sp.wait_ge(s["xs"], 2 * i + g + 1)
                            sp.dma_start(xs_t[:, tiles(i, g), :], xsb[:, g, :, :]).then_inc(o_xs[g], 16)
                        for g in range(2):
                            sp.wait_ge(s["sh"], 2 * i + g + 1)
                            sp.dma_start(sh_t[:, tiles(i, g), :], shb[:, g, :, :]).then_inc(o_sh[g], 16)

                    for g in range(2):
                        load(0, g)
                    with sp.Fori(0, HALF - 1) as i:
                        turn(i, False)
                    turn(HALF - 1, True)
                    sp.wait_ge(we1_in, 16 * HALF)
                    for g in range(2):
                        sp.wait_ge(o_x1[g], 16 * HALF)
                        sp.wait_ge(o_xs[g], 16 * HALF)
                        sp.wait_ge(o_sh[g], 16 * HALF)

                @block.gpsimd
                def _(pool):
                    pool.memset(cum[:, :, :], 0.0)
                    pool.drain()
                    pool.tensor_tensor(ct[:, 0, :], cum[:, 0, :], cum[:, 1, :], ALU.add).then_inc(s["cum"], 1)

                    def ahead(i):
                        for g in range(2):
                            pool.wait_ge(s["gsil"], 2 * i + g + 1)
                            pool.tensor_tensor(gin[:, g, :, :], gin[:, g, :, :], X[:, tiles(i, g), :], ALU.mult)
                            pool.drain()
                            pool.tensor_tensor(x1b[:, g, :, :], gin[:, g, :, :], xin3[:, g, :, :], ALU.add)\
                                .then_inc(s["x1"], 1)
                        for g in range(2):
                            rstd_step(pool, s, B + 2 * i + g, g, "stats0", "rstd0", in_bufs)

                    def turn(i, final):
                        for g in range(2):
                            u = 2 * i + g
                            pool.wait_ge(s["oh"], u + 1)
                            pool.tensor_tensor(ct[:, g, :], oh[:, g, 0, :], oh[:, g, 1, :], ALU.add)
                            pool.drain()
                            if g == 1:
                                pool.wait_ge(s["rank"], 2 * i + 1)
                            pool.tensor_tensor(cum[:, 1 - g, :], cum[:, g, :], ct[:, g, :], ALU.add)\
                                .then_inc(s["cum"], 1)
                        if not final:
                            ahead(i + 1)
                        for g in range(2):
                            rstd_step(pool, s, 2 * i + g, g, "stats2", "rstd2")
                    ahead(0)
                    with pool.Fori(0, HALF - 1) as i:
                        turn(i, False)
                    turn(HALF - 1, True)

                @block.tensor
                def _(pe):
                    def ahead(i):
                        for g in range(2):
                            pe.wait_ge(s["xn"], B + 2 * i + g + 1)
                            transpose_unit(pe, g, T, 0, xn, s["xnTp"])

                    def turn(i, first, final):
                        for g in range(2):
                            for t in range(TPU):
                                xt = xnT3[:, g, t * P:(t + 1) * P]
                                if t and not first:
                                    pe.wait_ge(s["s1"], 2 * i + g - 1)
                                pe.matmul(bank(g, (S0, Q)[t]), xt, W1[:, 0:4 * C], start=True, stop=True)
                                pe.matmul(bank(g, S1)[:, t * C:(t + 1) * C], xt, W1[:, 4 * C:5 * C],
                                          start=True, stop=True)
                                last = pe.matmul(bank(g, T)[:, S + t * E1:S + (t + 1) * E1], xt,
                                                 W1[:, W_GATE:W_GATE + E1], start=True, stop=True)
                            last.then_inc(s["proj"], 1)
                        for g in range(2):
                            u = 2 * i + g
                            pe.wait_ge(s["lg"], u + 1)
                            for n in range(2 * TPU):
                                w = W1[:, W_SG + n * P:W_SG + (n + 1) * P]
                                last = pe.matmul(bank(g, S0 + n // 2)[:, n % 2 * S:(n % 2 + 1) * S], w,
                                                 xnT3[:, g, :], start=True, stop=True)
                            last.then_inc(s["gu"], 1)
                            pe.wait_ge(s["oh"], u + 1)
                            pe.wait_ge(s["cum"], u + 1)
                            for t in range(TPU):
                                r = bank(g, T)[:, RANKS + t * E1:RANKS + (t + 1) * E1]
                                pe.matmul(r, TRI[:, :], oh[:, g, t, :], start=True, stop=False)
                                if t:
                                    pe.matmul(r, ONES[:, :], oh[:, g, 0, :], start=False, stop=False)
                                last = pe.matmul(r, ONES[:, :], cum[:, g, :], start=False, stop=True)
                            last.then_inc(s["rank"], 1)
                        for g in range(2):
                            pe.wait_ge(s["kn"], 2 * i + g + 1)
                            for k in range(2):
                                for t in range(TPU):
                                    last = pe.matmul(bank(g, Q)[:, k * C:(k + 1) * C],
                                                     qkp[g][:, t, (k + 1) * C:(k + 2) * C],
                                                     vv[g][:, t, k * C:(k + 1) * C],
                                                     start=(t == 0), stop=(t == TPU - 1))
                            last.then_inc(s["states"], 1)
                            for t in range(TPU):
                                last = pe.transpose(bank(g, T)[:, t * P:(t + 1) * P], qkp[g][:, t, 0:C], ident)
                            last.then_inc(s["qTp"], 1)
                        for g in range(2):
                            pe.wait_ge(s["hmul"], 2 * i + g + 1)
                            for t in range(TPU):
                                for n in range(2):
                                    last = pe.matmul(bank(g, S0)[:, t * C:(t + 1) * C],
                                                     hid[g][:, n * S + t * P:n * S + (t + 1) * P],
                                                     W1[:, W_SD + n * C:W_SD + (n + 1) * C],
                                                     start=(n == 0), stop=(n == 1))
                            last.then_inc(s["down"], 1)
                        for g in range(2):
                            pe.wait_ge(s["qT"], 2 * i + g + 1)
                            pe.wait_ge(s["state"], 2 * i + g + 1)
                            for t in range(TPU):
                                last = pe.matmul(bank(g, Q)[:, S + t * C:S + (t + 1) * C], qT[:, g, t * P:(t + 1) * P],
                                                 stt_[g], start=True, stop=True)
                            last.then_inc(s["lin"], 1)
                        if not final:
                            ahead(i + 1)
                            for g in range(2):
                                pe.wait_ge(s["xnT"], B + 2 * (i + 1) + g + 1)
                        for g in range(2):
                            pe.wait_ge(s["z2"], 2 * i + g + 1)
                            transpose_unit(pe, g, T, 0, z2, s["zTp"])
                        for g in range(2):
                            pe.wait_ge(s["zT"], 2 * i + g + 1)
                            for t in range(TPU):
                                last = pe.matmul(bank(g, Q)[:, t * C:(t + 1) * C], zT[:, g, t * P:(t + 1) * P],
                                                 W1[:, W_WO:W_WO + C], start=True, stop=True)
                            last.then_inc(s["wo"], 1)
                    ahead(0)
                    for g in range(2):
                        pe.wait_ge(s["xnT"], B + g + 1)
                    turn(0, True, False)
                    with pe.Fori(1, HALF - 1) as i:
                        turn(i, False, False)
                    turn(HALF - 1, False, True)

                @block.scalar
                def _(act):
                    def gate(i):
                        for g in range(2):
                            act.wait_ge(in_g[g], 16 * (i + 1))
                            act.wait_ge(in_x[g], 16 * (i + 1))
                            act.activation(gin[:, g, :, :], gin[:, g, :, :], ACT.Silu).then_inc(s["gsil"], 1)

                    def rows(i):
                        for g in range(2):
                            act.wait_ge(s["xnTp"], B + 2 * i + g + 1)
                            act.activation(xnT3[:, g, :], bank(g, T)[:, 0:S], ACT.Copy).then_inc(s["xnT"], 1)

                    def turn(i, final):
                        for g in range(2):
                            act.wait_ge(s["biased"], 2 * i + g + 1)
                            act.activation(qkp[g][:, :, :], qkp[g][:, :, :], ACT.Silu).then_inc(s["silu"], 1)
                            act.drain()
                            act.activation(sqb[g], qkp[g][:, :, :], ACT.Square, bias=PHALF[:, 0:1]).then_inc(s["sq"], 1)
                        for g in range(2):
                            act.wait_ge(s["top"], 2 * i + g + 1)
                            act.activation(th[:, g, :], m8[:, g, :, 0], ACT.Tanh, scale=0.5).then_inc(s["tanh"], 1)
                        act.wait_ge(s["n2"], 2 * i + 2)
                        act.activation(n2[:, :, :], n2[:, :, :], ACT.Sqrt).then_inc(s["nrm"], 1)
                        for g in range(2):
                            act.wait_ge(s["gu"], 2 * i + g + 1)
                            act.activation(hid[g], bank(g, S0), ACT.Silu).then_inc(s["sgate"], 1)
                        if not final:
                            for g in range(2):
                                act.wait_ge(o_x1[g], 16 * (i + 1))
                            gate(i + 1)
                        for g in range(2):
                            act.wait_ge(s["qTp"], 2 * i + g + 1)
                            act.activation(qT[:, g, :], bank(g, T)[:, 0:S], ACT.Copy).then_inc(s["qT"], 1)
                        for g in range(2):
                            act.wait_ge(s["sc"], 2 * i + g + 1)
                            for t in range(TPU):
                                last = act.activation(xsb[:, g, t, :], xn[:, g, t, :], ACT.Identity,
                                                      scale=sc[:, g, t:t + 1])
                            last.then_inc(s["xs"], 1)
                        for g in range(2):
                            act.wait_ge(s["down"], 2 * i + g + 1)
                            act.activation(shb[:, g, :, :].rearrange("p t c -> p (t c)"), bank(g, S0)[:, 0:S], ACT.Copy)\
                               .then_inc(s["sh"], 1)
                        if not final:
                            rows(i + 1)
                        for g in range(2):
                            act.wait_ge(s["zTp"], 2 * i + g + 1)
                            affine_step(act, g, ls, lb, s["zT"])
                        for g in range(2):
                            act.wait_ge(o_xs[g], 16 * (i + 1))
                            act.wait_ge(o_sh[g], 16 * (i + 1))
                    gate(0)
                    rows(0)
                    with act.Fori(0, HALF - 1) as i:
                        turn(i, False)
                    turn(HALF - 1, True)

                @block.vector
                def _(dve):
                    def stats(i):
                        for g in range(2):
                            dve.wait_ge(s["x1"], 2 * i + g + 1)
                            stats_step(dve, g, lambda t: x1b[:, g, t, :], s["stats0"], in_bufs)

                    def norms(i):
                        for g in range(2):
                            dve.wait_ge(s["rstd0"], B + 2 * i + g + 1)
                            norm_step(dve, g, lambda t: x1b[:, g, t, :], lambda t: xn[:, g, t, :], s["xn"], in_bufs)

                    def turn(i, final):
                        for g in range(2):
                            dve.wait_ge(s["proj"], 2 * i + g + 1)
                            bias = ROW[:, DEPTH * C:DEPTH * C + NP]
                            for t in range(TPU):
                                b = bank(g, (S0, Q)[t])
                                last = dve.tensor_tensor(qkp[g][:, t, :], b[:, 0:3 * C], bias[:, 0:3 * C], ALU.add)
                            last.then_inc(s["biased"], 1)
                            for t in range(TPU):
                                b = bank(g, (S0, Q)[t])
                                dve.tensor_tensor(vv[g][:, t, 0:C], b[:, 3 * C:4 * C], bias[:, 3 * C:4 * C], ALU.add)
                            dve.tensor_tensor(vv[g][:, :, C:2 * C],
                                              bank(g, S1)[:, 0:S].rearrange("p (t c) -> p t c", t=TPU),
                                              bias[:, 4 * C:5 * C].unsqueeze(1).to_broadcast([P, TPU, C]), ALU.add)
                            dve.tensor_copy(lg1[:, g, :, :].rearrange("p t e -> p (t e)"),
                                            bank(g, T)[:, S:S + TPU * E1]).then_inc(s["lg"], 1)
                            dve.drain()
                            for t in range(TPU):
                                last = dve.max(out=m8[:, g, t, :], in_=lg1[:, g, t, :])
                            last.then_inc(s["top"], 1)
                            dve.drain()
                            for t in range(TPU):
                                dve.max_index(out=i8[:, g, t, :], in_max=m8[:, g, t, :], in_values=lg1[:, g, t, :])
                            dve.drain()
                            dve.tensor_copy(ei[:, g, :], i8[:, g, :, 0])
                            dve.drain()
                            for t in range(TPU):
                                last = dve.tensor_scalar(oh[:, g, t, :], CST[:, C_IOTA:C_IOTA + E1], ei[:, g, t:t + 1],
                                                         None, ALU.is_equal)
                            last.then_inc(s["oh"], 1)
                            dve.tensor_copy(EID[:, tiles(i, g)], ei[:, g, :])
                        for g in range(2):
                            dve.wait_ge(s["sq"], 2 * i + g + 1)
                            dve.tensor_reduce(n2[:, g, :], sqb[g].rearrange("p t (h d) -> p (t h) d", d=LD), X_AXIS,
                                              ALU.add).then_inc(s["n2"], 1)
                        for g in range(2):
                            dve.wait_ge(s["rank"], 2 * i + g + 1)
                            for t in range(TPU):
                                dve.scalar_tensor_tensor(junk[:, g, t, :], bank(g, T)[:, RANKS + t * E1:RANKS + (t + 1) * E1],
                                                                1.0, oh[:, g, t, :], ALU.mult, ALU.mult,
                                                                accum_out=rk[:, g, t:t + 1])
                        dve.drain()
                        dve.wait_ge(s["nrm"], i + 1)
                        dve.tensor_scalar(n2[:, :, :], n2[:, :, :], 1e-6, None, ALU.add)
                        dve.drain()
                        for g in range(2):
                            dve.reciprocal(rn[:, g, :], n2[:, g, :])
                            dve.drain()
                            f = qkp[g][:, :, :].rearrange("p t (h d) -> p (t h) d", d=LD)
                            dve.scalar_tensor_tensor(f, f, 0.5, rn[:, g, :].unsqueeze(2).to_broadcast([P, NG, LD]),
                                                     ALU.add, ALU.mult).then_inc(s["kn"], 1)
                        for g in range(2):
                            dve.wait_ge(s["sgate"], 2 * i + g + 1)
                            dve.tensor_tensor(hid[g], bank(g, S1), hid[g], ALU.mult).then_inc(s["hmul"], 1)
                        for g in range(2):
                            dve.wait_ge(s["states"], 2 * i + g + 1)
                            dve.tensor_tensor(st0[g], bank(g, Q)[:, 0:C], CST[:, C_BLK:C_BLK + C], ALU.mult)
                            dve.drain()
                            dve.tensor_tensor(stt_[g], bank(g, Q)[:, C:2 * C], st0[g], ALU.mult).then_inc(s["state"], 1)
                        for g in range(2):
                            dve.tensor_copy(RNK[:, tiles(i, g)], rk[:, g, :])
                        for g in range(2):
                            dve.wait_ge(s["tanh"], 2 * i + g + 1)
                            dve.tensor_scalar(sc[:, g, :], th[:, g, :], 0.5, 0.5, ALU.mult, ALU.add).then_inc(s["sc"], 1)
                        if not final:
                            stats(i + 1)
                        for g in range(2):
                            dve.wait_ge(s["lin"], 2 * i + g + 1)
                            stats_step(dve, g, lambda t: bank(g, Q)[:, S + t * C:S + (t + 1) * C], s["stats2"])
                        if not final:
                            dve.wait_ge(s["xs"], 2 * i + 2)
                            norms(i + 1)
                        for g in range(2):
                            dve.wait_ge(s["rstd2"], 2 * i + g + 1)
                            norm_step(dve, g, lambda t: bank(g, Q)[:, S + t * C:S + (t + 1) * C],
                                      lambda t: z2[:, g, t, :], s["z2"])
                        for g in range(2):
                            dve.wait_ge(s["wo"], 2 * i + g + 1)
                            dve.tensor_tensor(X[:, tiles(i, g), :], by_tile(bank(g, Q)[:, 0:S]),
                                              ROW[:, DEPTH * C + NP:DEPTH * C + NP + C].unsqueeze(1)
                                              .to_broadcast([P, TPU, C]), ALU.add).then_inc(s["s1"], 1)
                    stats(0)
                    norms(0)
                    with dve.Fori(0, HALF - 1) as i:
                        turn(i, False)
                    turn(HALF - 1, True)
        stage3()

        def place():
            placed = [sem(f"pl_placed{b}") for b in range(2)]
            loaded = [sem(f"pl_loaded{b}") for b in range(2)]
            counted, slots, started = sem("pl_counted"), sem("pl_slots"), sem("pl_started")
            cnt = late([P, E1])
            ci = sb("ci", [P, E1], I32)
            nt = late([P, E1])
            end = late([P, E1])
            off = late([P, E1])
            eq = pr[:, :, :, :, :].rearrange("p g a b c -> p (g a b c)")[:, 0:NT * E1].rearrange("p (t e) -> p t e", e=E1)
            sl = late([P, NT])
            n_b = IN_FLIGHT
            xb = [buf[:, :, :, :].rearrange("p g a b -> p (g a) b") for buf in (z, v)]
            ix = [sb(f"ix{b}", [P, n_b], I32) for b in range(2)]
            carrier1 = sb("carrier1", [P, 4], I32)
            zb = sb("zb", [P, n_b])
            pairs = NT // (2 * n_b)
            with nc.Block() as block:
                @block.tensor
                def _(pe):
                    pe.matmul(bank(0, T)[:, 0:E1], ONES[:, :], cum[:, 0, :], start=True, stop=True).then_inc(counted, 1)

                @block.vector
                def _(dve):
                    dve.memset(zb[:, :], 0.0)
                    dve.wait_ge(counted, 1)
                    dve.tensor_scalar(ci[:, :], bank(0, T)[:, 0:E1], float(P - 1), None, ALU.add)
                    dve.drain()
                    dve.tensor_scalar(ci[:, :], ci[:, :], P.bit_length() - 1, None, ALU.logical_shift_right)
                    dve.drain()
                    dve.tensor_copy(nt[:, :], ci[:, :])
                    dve.drain()
                    dve.tensor_tensor_scan(end[:, :], nt[:, :], CST[:, C_ONE:C_ONE + E1], 0.0, ALU.add, ALU.mult)
                    dve.drain()
                    dve.tensor_tensor(off[:, :], end[:, :], nt[:, :], ALU.subtract)
                    dve.drain()
                    dve.tensor_scalar(off[:, :], off[:, :], float(P), None, ALU.mult)
                    dve.tensor_tensor(eq, EID[:, :].unsqueeze(2).to_broadcast([P, NT, E1]),
                                      CST[:, C_IOTA:C_IOTA + E1].unsqueeze(1).to_broadcast([P, NT, E1]), ALU.is_equal)
                    dve.drain()
                    dve.tensor_tensor(eq, eq, off[:, :].unsqueeze(1).to_broadcast([P, NT, E1]), ALU.mult)
                    dve.drain()
                    dve.tensor_reduce(sl[:, :], eq, X_AXIS, ALU.add)
                    dve.drain()
                    dve.tensor_tensor(SLOT[:, :], sl[:, :], RNK[:, :], ALU.add)
                    dve.drain()
                    for b in range(2):
                        dve.tensor_copy(ix[b][:, :], SLOT[:, n_b * b:n_b * (b + 1)]).then_inc(slots, 1)
                    te = pT[0:1, :, :, :, :].rearrange("p g a b c -> p (g a b c)")
                    for h in range(3):
                        n = SORTED_TILES // 3
                        part = te[:, 0:n * E1].rearrange("p (t e) -> p t e", e=E1)
                        t0 = C_TILE + h * n
                        dve.tensor_tensor(part, end[0:1, :].unsqueeze(1).to_broadcast([1, n, E1]),
                                          CST[0:1, t0:t0 + n].unsqueeze(2).to_broadcast([1, n, E1]), ALU.is_le)
                        dve.drain()
                        dve.tensor_reduce(tef[:, h * n:(h + 1) * n], part, X_AXIS, ALU.add)
                        dve.drain()
                    dve.tensor_scalar(TE[:, :], tef[:, :], float(E1 - 1), None, ALU.min)
                    with dve.Fori(1, pairs) as j:
                        for b in range(2):
                            dve.wait_ge(started, 2 * j + b - 1)
                            dve.wait_ge(placed[b], 16 * n_b * j)
                            dve.tensor_tensor(ix[b][:, :], SLOT[:, bass.ds(n_b * (2 * j + b), n_b)], zb[:, :], ALU.add)\
                               .then_inc(slots, 1)

                @block.sync
                def _(sp):
                    def load(j, b):
                        sp.dma_start(xb[b], xs_t[:, bass.ds(n_b * (2 * j + b), n_b), :]).then_inc(loaded[b], 16)
                    for b in range(2):
                        load(0, b)
                    with sp.Fori(0, pairs - 1) as j:
                        for b in range(2):
                            sp.wait_ge(placed[b], 16 * n_b * (j + 1))
                            load(j + 1, b)
                    for b in range(2):
                        sp.wait_ge(placed[b], 16 * n_b * pairs)

                @block.gpsimd
                def _(pool):
                    def scatter(j, b):
                        pool.wait_ge(loaded[b], 16 * (j + 1))
                        pool.wait_ge(slots, 2 * j + b + 1)
                        pool.tensor_tensor(carrier1[:, b:b + 1], carrier1[:, 2:3], carrier1[:, 3:4], ALU.add).then_inc(started, 1)
                        for k in range(n_b):
                            pool.indirect_dma_start(out=srt[:, :],
                                                    out_offset=bass.IndirectOffsetOnAxis(ap=ix[b][:, k:k + 1], axis=0),
                                                    in_=xb[b][:, k, :], in_offset=None,
                                                    bounds_check=SORTED_TILES * P - 1).then_inc(placed[b], 16)
                    pool.memset(carrier1[:, :], 0)
                    pool.drain()
                    with pool.Fori(0, pairs) as j:
                        for b in range(2):
                            scatter(j, b)

        tef = late([1, SORTED_TILES])
        place()

        def stage4():
            n_t = IN_FLIGHT
            s = sems("s4", ["row_in", "xTp", "xT", "gu", "silu", "h", "hTp", "hT", "yp", "y", "row_out"])

            def four(buf):
                return buf[:, :, :, :].rearrange("p g a b -> p (g a) b")
            xt, yb = four(v), four(att)
            xT = [zT[:, k // 2, k % 2 * P:(k % 2 + 1) * P] for k in range(n_t)]
            hb = [pr[:, k // 2, k % 2, :, :].rearrange("p a b -> p (a b)")[:, 0:F1] for k in range(n_t)]
            hT = [pT[:, k // 2, k % 2, :, :].rearrange("p a b -> p (a b)")[:, 0:F1] for k in range(n_t)]

            def gu(k):
                return ps[:, 2 * k, :]

            def misc(k):
                return ps[:, 2 * k + 1, :]
            turns = SORTED_TILES // n_t
            with nc.Block() as block:
                @block.sync
                def _(sp):
                    def load(i):
                        sp.dma_start(xt, srt_t[:, bass.ds(n_t * i, n_t), :]).then_inc(s["row_in"], 16)

                    def turn(i, ahead):
                        if ahead:
                            sp.wait_ge(s["xTp"], n_t * (i + 2))
                            load(i + 2)
                        sp.wait_ge(s["y"], n_t * (i + 1))
                        sp.dma_start(ys_t[:, bass.ds(n_t * i, n_t), :], yb).then_inc(s["row_out"], 16)
                    load(0)
                    sp.wait_ge(s["xTp"], n_t)
                    load(1)
                    with sp.Fori(0, turns - 2) as i:
                        turn(i, True)
                    turn(turns - 2, False)
                    turn(turns - 1, False)
                    sp.wait_ge(s["row_out"], 16 * turns)

                @block.tensor
                def _(pe):
                    def turn_rows(i):
                        pe.wait_ge(s["row_in"], 16 * (i + 1))
                        for k in range(n_t):
                            pe.transpose(misc(k)[:, 0:P], xt[:, k, :], ident).then_inc(s["xTp"], 1)

                    def turn(i, e, first, final):
                        for k in range(n_t):
                            if not first:
                                pe.wait_ge(s["y"], n_t * (i - 1) + k + 1)
                            pe.matmul(gu(k), xT[k], WE1[:, e[k], 0:2 * F1], start=True, stop=True).then_inc(s["gu"], 1)
                        if not final:
                            turn_rows(i + 1)
                            pe.wait_ge(s["xT"], n_t * (i + 2))
                        for k in range(n_t):
                            pe.wait_ge(s["h"], n_t * i + k + 1)
                            for f in range(2):
                                last = pe.transpose(misc(k)[:, (f + 1) * P:(f + 2) * P], hb[k][:, f * P:(f + 1) * P],
                                                    ident)
                            last.then_inc(s["hTp"], 1)
                        for k in range(n_t):
                            pe.wait_ge(s["hT"], n_t * i + k + 1)
                            for f in range(2):
                                last = pe.matmul(gu(k)[:, 0:C], hT[k][:, f * P:(f + 1) * P],
                                                 WE1[:, e[k], 2 * F1 + f * C:2 * F1 + (f + 1) * C],
                                                 start=(f == 0), stop=(f == 1))
                            last.then_inc(s["yp"], 1)

                    def group(j, first=False, final=False):
                        _, e = nc.values_load_multi_w_load_instructions(
                            TE[0:1, bass.ds(n_t * PER_LOAD * j, n_t * PER_LOAD)], engines=[mybir.EngineType.PE],
                            min_val=0, max_val=E1 - 1)
                        for n in range(PER_LOAD):
                            turn(PER_LOAD * j + n, e[n_t * n:n_t * (n + 1)], first and n == 0,
                                 final and n == PER_LOAD - 1)
                    turn_rows(0)
                    pe.wait_ge(s["xT"], n_t)
                    group(0, first=True)
                    with pe.Fori(1, turns // PER_LOAD - 1) as j:
                        group(j)
                    group(turns // PER_LOAD - 1, final=True)

                @block.scalar
                def _(act):
                    def rows(i):
                        for k in range(n_t):
                            act.wait_ge(s["xTp"], n_t * i + k + 1)
                            act.activation(xT[k], misc(k)[:, 0:P], ACT.Copy).then_inc(s["xT"], 1)

                    def turn(i, first, final):
                        for k in range(n_t):
                            act.wait_ge(s["gu"], n_t * i + k + 1)
                            act.activation(hb[k], gu(k)[:, 0:F1], ACT.Silu).then_inc(s["silu"], 1)
                        if not final:
                            rows(i + 1)
                        if not first:
                            act.wait_ge(s["row_out"], 16 * i)
                        for k in range(n_t):
                            act.wait_ge(s["yp"], n_t * i + k + 1)
                            act.activation(yb[:, k, :], gu(k)[:, 0:C], ACT.Copy).then_inc(s["y"], 1)
                    rows(0)
                    turn(0, True, False)
                    with act.Fori(1, turns - 1) as i:
                        turn(i, False, False)
                    turn(turns - 1, False, True)

                @block.vector
                def _(dve):
                    with dve.Fori(0, turns) as i:
                        for k in range(n_t):
                            dve.wait_ge(s["silu"], n_t * i + k + 1)
                            dve.tensor_tensor(hb[k], gu(k)[:, F1:2 * F1], hb[k], ALU.mult).then_inc(s["h"], 1)
                        for k in range(n_t):
                            dve.wait_ge(s["hTp"], n_t * i + k + 1)
                            dve.tensor_copy(hT[k], misc(k)[:, P:3 * P]).then_inc(s["hT"], 1)
        stage4()

        def stage5():
            n_t = IN_FLIGHT
            s = sems("s5", ["sum", "silu", "res", "idx", "started"])
            got, ld, stored = ([sem(f"s5_{n}{k}") for k in range(2)] for n in ("got", "ld", "stored"))

            def four(buf):
                return buf[:, :, :, :].rearrange("p g a b -> p (g a) b")

            def half_of(buf, k):
                return buf[:, k, :, :, :].rearrange("p a b c -> p (a b c)")[:, 0:n_t * C]\
                    .rearrange("p (a c) -> p a c", c=C)
            yg = [four(v), four(z)]
            a1 = [half_of(pr, k) for k in range(2)]
            a2 = [half_of(pT, k) for k in range(2)]
            ob = [qk[:, k, :, :].rearrange("p n (b c) -> p (n b) c", c=C) for k in range(2)]
            pairs = NT // (2 * n_t)
            with nc.Block() as block:
                @block.sync
                def _(sp):
                    def load(j, k):
                        at = bass.ds(n_t * (2 * j + k), n_t)
                        sp.dma_start(a1[k], x1_t[:, at, :]).then_inc(ld[k], 16)
                        sp.dma_start(a2[k], sh_t[:, at, :]).then_inc(ld[k], 16)

                    def pair(j, last):
                        for k in range(2):
                            sp.wait_ge(s["res"], 2 * j + k + 1)
                            if not last:
                                load(j + 1, k)
                            sp.dma_start(out_t[:, bass.ds(n_t * (2 * j + k), n_t), :], ob[k]).then_inc(stored[k], 16)
                    for k in range(2):
                        load(0, k)
                    with sp.Fori(0, pairs - 1) as j:
                        pair(j, False)
                    pair(pairs - 1, True)
                    for k in range(2):
                        sp.wait_ge(stored[k], 16 * pairs)

                @block.gpsimd
                def _(pool):
                    pool.memset(carrier5[:, :], 0)
                    pool.drain()
                    with pool.Fori(0, pairs) as j:
                        for k in range(2):
                            pool.wait_ge(s["idx"], 2 * j + k + 1)
                            pool.tensor_tensor(carrier5[:, k:k + 1], carrier5[:, 2:3], carrier5[:, 3:4], ALU.add)\
                                .then_inc(s["started"], 1)
                            for n in range(n_t):
                                pool.indirect_dma_start(out=yg[k][:, n, :], out_offset=None, in_=ysd[:, :],
                                                        in_offset=bass.IndirectOffsetOnAxis(ap=iv[k][:, n:n + 1], axis=0),
                                                        bounds_check=SORTED_TILES * P - 1).then_inc(got[k], 16)

                @block.scalar
                def _(act):
                    with act.Fori(0, pairs) as j:
                        for k in range(2):
                            act.wait_ge(s["sum"], 2 * j + k + 1)
                            act.activation(a2[k], a2[k], ACT.Silu).then_inc(s["silu"], 1)

                @block.vector
                def _(dve):
                    def pair(j, first, final):
                        for k in range(2):
                            dve.wait_ge(s["started"], 2 * j + k + 1)
                            dve.wait_ge(got[k], 16 * n_t * (j + 1))
                            dve.wait_ge(ld[k], 32 * (j + 1))
                            dve.tensor_tensor(a2[k], a2[k], yg[k], ALU.add).then_inc(s["sum"], 1)
                            if not final:
                                dve.drain()
                                dve.tensor_copy(iv[k][:, :], SLOT[:, bass.ds(n_t * (2 * j + 2 + k), n_t)])\
                                   .then_inc(s["idx"], 1)
                            dve.wait_ge(s["silu"], 2 * j + k + 1)
                            dve.tensor_tensor(a2[k], a2[k], X[:, bass.ds(n_t * (2 * j + k), n_t), :], ALU.mult)
                            dve.drain()
                            if not first:
                                dve.wait_ge(stored[k], 16 * j)
                            dve.tensor_tensor(ob[k], a2[k], a1[k], ALU.add).then_inc(s["res"], 1)
                    for k in range(2):
                        dve.tensor_copy(iv[k][:, :], SLOT[:, n_t * k:n_t * (k + 1)]).then_inc(s["idx"], 1)
                    pair(0, True, False)
                    with dve.Fori(1, pairs - 1) as j:
                        pair(j, False, False)
                    pair(pairs - 1, False, True)
        iv = [sb(f"iv{k}", [P, IN_FLIGHT], I32) for k in range(2)]
        carrier5 = sb("carrier5", [P, 4], I32)
        stage5()


def pack(inputs):
    import numpy as np
    a = {k: np.asarray(v) for k, v in inputs.items()}
    f = np.float32
    d = {}
    d["x"] = a["L0_attn_x"].reshape(TOK, C)
    w = []
    for l in range(DEPTH):
        w += [a["L0_attn_wq"][l], a["L0_attn_wk"][l], a["L0_attn_wv"][l], a["L0_attn_wo"][l], a["L0_attn_w1"][l],
              a["L0_attn_w2"][l].reshape(FC, P, C).transpose(1, 0, 2).reshape(P, FC * C)]
    d["w0"] = np.concatenate(w, axis=1)
    c = []
    for l in range(DEPTH):
        c += [a[f"L0_attn_{n}"][l][:, None] for n in ("ln1_g", "ln1_b", "ln2_g", "ln2_b", "bq", "bk")]
        c.append(a["L0_attn_b1"][l].reshape(FC, P).T)
    c += [a["L1_attn_ln_g"][:, None], a["L1_attn_ln_b"][:, None]]
    d["cols"] = np.concatenate(c, axis=1)
    r = np.concatenate([a["L0_attn_bv"].reshape(-1), a["L1_attn_bq"], a["L1_attn_bk"].reshape(-1),
                        a["L1_attn_bv"].reshape(-1), a["L1_attn_bo"]])
    d["rows"] = np.broadcast_to(r[None, :], (P, r.size))
    freq = np.array([float.fromhex(h) for h in (
        "0x1.0p+0", "0x1.1cfed8p+0", "0x1.3d466cp+0", "0x1.6135f6p+0", "0x1.89377ap+0", "0x1.b5c0fcp+0",
        "0x1.e755dep+0", "0x1.0f4432p+1", "0x1.2dfdb2p+1", "0x1.503210p+1", "0x1.764638p+1", "0x1.a0aa7ap+1",
        "0x1.cfdbe8p+1", "0x1.0232dcp+2", "0x1.1f7176p+2", "0x1.3ffffep+2")], f)
    rad = ((np.arange(1, S + 1, dtype=f)[None, :] * freq[:, None]) * f(np.pi)).astype(np.float64)
    rad = np.concatenate([rad, rad])
    sign = np.where(np.arange(2 * freq.size) % 2 == 0, -1.0, 1.0)[:, None]
    head = np.concatenate([np.sin(rad) + sign * np.cos(rad), np.ones((DH - 2 * freq.size, S))])
    rk = np.concatenate([head] * HEADS)
    d["rot"] = np.concatenate([rk * DH ** -0.5, rk], axis=1).astype(f)
    k = np.zeros((P, NCST), f)
    p = np.arange(P)
    k[:, C_ID:C_ID + P] = np.eye(P)
    k[:, C_BLK:C_BLK + P] = (p[:, None] // LD == p[None, :] // LD) * (1.0 / S) ** 2
    k[:, C_TRI:C_TRI + P] = p[:, None] < p[None, :]
    k[:, C_IOTA:C_IOTA + E1] = np.arange(E1)
    k[:, C_TOKV:C_TOKV + NT] = TOK - P * np.arange(NT)[None, :] - p[:, None]
    k[:, C_ONE:C_ONE + P] = 1.0
    k[:, C_P] = p
    k[:, C_TILE:] = np.arange(SORTED_TILES)
    d["cst"] = k
    d["ws"] = np.concatenate([a["L0_ffn_router_w"].T, a["L0_ffn_ws_gate_up"]], axis=1)
    d["wsd"] = a["L0_ffn_ws_down"]
    d["we0"] = np.concatenate([a["L0_ffn_w_gate"], a["L0_ffn_w_up"]], axis=2)
    d["wd0"] = a["L0_ffn_w_down"]
    d["w1"] = np.concatenate([a["L1_attn_Wq"].T, a["L1_attn_Wk"][0].T, a["L1_attn_Wk"][1].T, a["L1_attn_Wv"][0].T,
                              a["L1_attn_Wv"][1].T, a["L1_attn_Wo"].T, a["L1_ffn_gate_w"], a["L1_ffn_shared_gate_w"],
                              a["L1_ffn_shared_up_w"],
                              a["L1_ffn_shared_down_w"].reshape(2, P, C).transpose(1, 0, 2).reshape(P, 2 * C)], axis=1)
    e = np.concatenate([a["L1_ffn_routed_gate_w"], a["L1_ffn_routed_up_w"],
                        a["L1_ffn_routed_down_w"].reshape(E1, 2, P, C).transpose(0, 2, 1, 3).reshape(E1, P, 2 * C)],
                       axis=2)
    d["we1"] = e.transpose(1, 0, 2).reshape(P, E1 * 768)
    return {n: np.ascontiguousarray(v) for n, v in d.items()}


_ARGS = ["x", "w0", "cols", "rows", "rot", "cst", "ws", "wsd", "we0", "wd0", "w1", "we1"]


def kernel(**inputs):
    import concourse.bacc as _bacc
    from concourse import mybir as _mybir
    from concourse.bass_utils import run_bass_kernel_spmd as _run

    arrays = pack(inputs)
    nc = _bacc.Bacc("TRN2", target_bir_lowering=False, num_devices=1)
    args = [nc.dram_tensor(n, arrays[n].shape, _mybir.dt.from_np(arrays[n].dtype), kind="ExternalInput").ap()
            for n in _ARGS]
    out = nc.dram_tensor("out", (TOK, C), F32, kind="ExternalOutput").ap()
    mixed_layers(nc, *args, out)
    r = _run(nc, [arrays], core_ids=[0])
    return r.results[0]["out"].reshape(B, S, C)
```
